# Optimizing a Trainium2 kernel written in Bass

```python
import numpy as np
import jax
import jax.numpy as jnp

def _softmax(x, axis=-1):
    return jax.nn.softmax(x, axis=axis)

def _gelu(x):
    return jax.nn.gelu(x, approximate=True)

def _silu(x):
    return jax.nn.silu(x)

def _sigmoid(x):
    return jax.nn.sigmoid(x)

def _layernorm(x, axis=-1, eps=1e-05):
    m = jnp.mean(x, axis=axis, keepdims=True)
    v = jnp.var(x, axis=axis, keepdims=True)
    return (x - m) / jnp.sqrt(v + eps)

def _scatter_add(tgt, idx, src, axis=0):
    return tgt.at[idx].add(src)

def _segment_sum(src, seg, n):
    return jax.ops.segment_sum(src, seg, n)
kernel_name = 'mk_xattn_ffn_d1_seqx_r4_092552'

def setup_inputs(seed: int=0):
    np.random.seed(seed)
    _w = jnp.asarray

    def _rec_inputs():
        import jax
        import jax.numpy as jnp
        _rk = jax.random.key(seed)
        x = 7.22e-05 + 1 * jax.random.normal(jax.random.fold_in(_rk, 1), (4, 512, 512), jnp.float32)
        _lenS = 512 - jax.random.randint(jax.random.fold_in(_rk, 7), (4,), 0, max(1, 512 // 4) + 1, jnp.int32)
        _lenS2 = 512 - jax.random.randint(jax.random.fold_in(_rk, 8), (4,), 0, max(1, 512 // 4) + 1, jnp.int32)
        _ctx_1024P = jax.random.normal(jax.random.fold_in(_rk, 11), (4, 16, 256), jnp.float32)
        _ctx_1024c = jax.random.dirichlet(jax.random.fold_in(_rk, 511), 0.3 * jnp.ones((16,), jnp.float32), (4, 512))
        _ctx_1024t = jnp.einsum('bsk,bkd->bsd', _ctx_1024c, _ctx_1024P)
        _ctx_1024t = _ctx_1024t * jax.lax.rsqrt(jnp.mean(jnp.square(_ctx_1024t)) + 1e-12) * 0.953939
        ctx_1024 = 2.81802e-05 + 1.00001 * (_ctx_1024t + 0.3 * jax.random.normal(jax.random.fold_in(_rk, 611), (4, 512, 256), jnp.float32))
        return (x, ctx_1024)
    x, ctx_1024 = _rec_inputs()

    def _L0_xattn_setup():
        import jax, jax.numpy as jnp
        import numpy as np
        key = jax.random.key(seed)
        ks = jax.random.split(key, 6)
        B, L, N, C, D = (8, 128, 512, 256, 128)
        return {'teacher_logits': jax.random.normal(ks[0], (B, L, N), dtype=jnp.float32), 'teacher_features': jax.random.normal(ks[1], (B, N, C), dtype=jnp.float32), 'Wq': jax.random.normal(ks[2], (D, C), dtype=jnp.float32) * (1.0 / np.sqrt(C)), 'bq': jnp.zeros((D,), dtype=jnp.float32), 'Wk': jax.random.normal(ks[3], (D, C), dtype=jnp.float32) * (1.0 / np.sqrt(C)), 'bk': jnp.zeros((D,), dtype=jnp.float32)}
    _L0_xattn_all = _L0_xattn_setup()
    _L0_xattn_in = {k: v for k, v in _L0_xattn_all.items() if k in ('Wq', 'bq', 'Wk', 'bk')}
    del _L0_xattn_all

    def _L0_ffn_setup():
        import jax, jax.numpy as jnp
        import numpy as np
        B, S, D = (2, 512, 512)
        H, HD = (16, 128)
        E, K, I = (16, 6, 352)
        SI = 704
        EPS = 1e-06

        def rmsnorm(x, w):
            v = jnp.mean(jnp.square(x), axis=-1, keepdims=True)
            return x * jax.lax.rsqrt(v + EPS) * w
        key = jax.random.key(seed)
        ks = jax.random.split(key, 14)
        s = 0.02
        return {'hidden_states': jax.random.normal(ks[0], (B, S, D), jnp.float32), 'ln1_w': jnp.ones((D,), jnp.float32), 'ln2_w': jnp.ones((D,), jnp.float32), 'wq': jax.random.normal(ks[1], (D, H * HD), jnp.float32) * s, 'wk': jax.random.normal(ks[2], (D, H * HD), jnp.float32) * s, 'wv': jax.random.normal(ks[3], (D, H * HD), jnp.float32) * s, 'wo': jax.random.normal(ks[4], (H * HD, D), jnp.float32) * s, 'gate_w': jax.random.normal(ks[5], (E, D), jnp.float32) * s, 'eg_w': jax.random.normal(ks[6], (E, I, D), jnp.float32) * s, 'eu_w': jax.random.normal(ks[7], (E, I, D), jnp.float32) * s, 'ed_w': jax.random.normal(ks[8], (E, D, I), jnp.float32) * s, 'sg_w': jax.random.normal(ks[9], (SI, D), jnp.float32) * s, 'su_w': jax.random.normal(ks[10], (SI, D), jnp.float32) * s, 'sd_w': jax.random.normal(ks[11], (D, SI), jnp.float32) * s}
    _L0_ffn_all = _L0_ffn_setup()
    _L0_ffn_in = {k: v for k, v in _L0_ffn_all.items() if k in ('ln1_w', 'ln2_w', 'wq', 'wk', 'wv', 'wo', 'gate_w', 'eg_w', 'eu_w', 'ed_w', 'sg_w', 'su_w', 'sd_w')}
    del _L0_ffn_all
    return {'x': x, 'ctx_1024': ctx_1024, 'L0_xattn_Wq': _L0_xattn_in['Wq'], 'L0_xattn_bq': _L0_xattn_in['bq'], 'L0_xattn_Wk': _L0_xattn_in['Wk'], 'L0_xattn_bk': _L0_xattn_in['bk'], 'L0_ffn_ln1_w': _L0_ffn_in['ln1_w'], 'L0_ffn_ln2_w': _L0_ffn_in['ln2_w'], 'L0_ffn_wq': _L0_ffn_in['wq'], 'L0_ffn_wk': _L0_ffn_in['wk'], 'L0_ffn_wv': _L0_ffn_in['wv'], 'L0_ffn_wo': _L0_ffn_in['wo'], 'L0_ffn_gate_w': _L0_ffn_in['gate_w'], 'L0_ffn_eg_w': _L0_ffn_in['eg_w'], 'L0_ffn_eu_w': _L0_ffn_in['eu_w'], 'L0_ffn_ed_w': _L0_ffn_in['ed_w'], 'L0_ffn_sg_w': _L0_ffn_in['sg_w'], 'L0_ffn_su_w': _L0_ffn_in['su_w'], 'L0_ffn_sd_w': _L0_ffn_in['sd_w']}

def reference(x, ctx_1024, L0_xattn_Wq, L0_xattn_bq, L0_xattn_Wk, L0_xattn_bk, L0_ffn_ln1_w, L0_ffn_ln2_w, L0_ffn_wq, L0_ffn_wk, L0_ffn_wv, L0_ffn_wo, L0_ffn_gate_w, L0_ffn_eg_w, L0_ffn_eu_w, L0_ffn_ed_w, L0_ffn_sg_w, L0_ffn_su_w, L0_ffn_sd_w):
    import jax
    import jax.numpy as jnp

    def _L0_xattn_ref(teacher_logits, teacher_features, Wq, bq, Wk, bk):
        import jax, jax.numpy as jnp
        import numpy as np
        query = jnp.einsum('bnc,dc->bnd', teacher_features, Wq) + bq
        key = jnp.einsum('bnc,dc->bnd', teacher_features, Wk) + bk
        energy = jnp.einsum('bnd,bmd->bnm', query, key)
        attention = jax.nn.softmax(energy, axis=-1)
        x_m = jnp.einsum('bln,bmn->blm', teacher_logits, attention)
        return x_m

    def _L0_ffn_ref(hidden_states, ln1_w, ln2_w, wq, wk, wv, wo, gate_w, eg_w, eu_w, ed_w, sg_w, su_w, sd_w):
        import jax, jax.numpy as jnp
        import numpy as np
        B, S, D = (2, 512, 512)
        H, HD = (16, 128)
        E, K, I = (16, 6, 352)
        SI = 704
        EPS = 1e-06

        def rmsnorm(x, w):
            v = jnp.mean(jnp.square(x), axis=-1, keepdims=True)
            return x * jax.lax.rsqrt(v + EPS) * w
        b, s, d = hidden_states.shape
        x = hidden_states
        h = rmsnorm(x, ln1_w)
        q = (h @ wq).reshape(b, s, H, HD)
        k = (h @ wk).reshape(b, s, H, HD)
        v = (h @ wv).reshape(b, s, H, HD)
        scores = jnp.einsum('bqhd,bkhd->bhqk', q, k) / np.sqrt(HD).astype(np.float32)
        causal = jnp.tril(jnp.ones((s, s), bool))
        scores = jnp.where(causal, scores, jnp.float32(-1000000000.0))
        attn = jax.nn.softmax(scores, axis=-1)
        ao = jnp.einsum('bhqk,bkhd->bqhd', attn, v).reshape(b, s, H * HD) @ wo
        x = x + ao
        h = rmsnorm(x, ln2_w)
        t = h.reshape(-1, d)
        T = t.shape[0]
        logits = t @ gate_w.T
        probs = jax.nn.softmax(logits, axis=-1)
        topv, topi = jax.lax.top_k(probs, K)
        topv = topv / jnp.sum(topv, axis=-1, keepdims=True)
        cw = jnp.zeros((T, E), t.dtype).at[jnp.arange(T)[:, None], topi].add(topv)
        g = jnp.einsum('td,eid->eti', t, eg_w)
        u = jnp.einsum('td,eid->eti', t, eu_w)
        hh = jax.nn.silu(g) * u
        routed = jnp.einsum('eti,edi,te->td', hh, ed_w, cw)
        shared = jax.nn.silu(t @ sg_w.T) * (t @ su_w.T) @ sd_w.T
        out = x + (routed + shared).reshape(b, s, d)
        return out
    x = x + _L0_xattn_ref(_layernorm(x, axis=-1), ctx_1024, L0_xattn_Wq, L0_xattn_bq, L0_xattn_Wk, L0_xattn_bk)
    x = x + _L0_ffn_ref(_layernorm(x, axis=-1), L0_ffn_ln1_w, L0_ffn_ln2_w, L0_ffn_wq, L0_ffn_wk, L0_ffn_wv, L0_ffn_wo, L0_ffn_gate_w, L0_ffn_eg_w, L0_ffn_eu_w, L0_ffn_ed_w, L0_ffn_sg_w, L0_ffn_su_w, L0_ffn_sd_w)
    return x

_drawn_inputs = setup_inputs


def setup_inputs(seed=0):
    import zlib

    import numpy as np

    out = dict(_drawn_inputs(seed))
    spreads = {'L0_xattn_bq': (0.0, 0.1),
     'L0_xattn_bk': (0.0, 2.0),
     'L0_ffn_ln1_w': (1.0, 0.6),
     'L0_ffn_ln2_w': (1.0, 0.6)}
    factors = {'L0_ffn_wq': 8.0,
     'L0_ffn_wk': 8.0,
     'L0_ffn_gate_w': 8.0,
     'L0_ffn_eg_w': 6.943,
     'L0_ffn_eu_w': 6.789,
     'L0_ffn_ed_w': 6.789,
     'L0_ffn_sg_w': 8.0,
     'L0_ffn_su_w': 8.0,
     'L0_ffn_sd_w': 8.0}
    for name, (base, spread) in spreads.items():
        noise = np.random.default_rng([zlib.crc32(name.encode()), seed]).standard_normal(out[name].shape)
        drawn = base * np.exp(spread * noise) if base else spread * noise
        out[name] = jnp.asarray(drawn.astype(out[name].dtype))
    for name, factor in factors.items():
        out[name] = (out[name] * factor).astype(out[name].dtype)
    return out
```

```python
from contextlib import ExitStack

import concourse.bass as bass
from concourse import mybir

F32 = mybir.dt.float32
F32R = mybir.dt.float32r
BF16 = mybir.dt.bfloat16
ALU = mybir.AluOpType
ACT = mybir.ActivationFunctionType
AX = mybir.AxisListType

P = 128
NB = 4
S = 512
D = 512
DC = D // P
C = 256
CC = C // P
ST = S // P
T = NB * S
TT = T // P
H = 16
HD = 128
HP = H // 2
E = 16
TOPK = 6
I = 352
NSH = 2
NE = E + NSH
IT = [(0, 128), (128, 128), (256, 96)]
LN_EPS = 1e-5
RMS_EPS = 1e-6
MASKED = -1e30


def matmul3(nc, out, lhs, rhs, start, stop):
    nc.tensor.matmul(out, lhs[0], rhs[0], start=start, stop=False)
    nc.tensor.matmul(out, lhs[0], rhs[1], start=False, stop=False)
    return nc.tensor.matmul(out, lhs[1], rhs[0], start=False, stop=stop)


def constants(nc, sem, ident, ident16, causal, neg_half, eps):
    made = sem("const_made")
    with nc.Block() as block:
        @block.gpsimd
        def _(pool):
            nc.gpsimd.memset(ident[:], 0.0).then_inc(made, 1)
            nc.gpsimd.memset(causal[:], 0.0).then_inc(made, 1)
            nc.gpsimd.memset(neg_half[:], -0.5).then_inc(made, 1)
            nc.gpsimd.memset(eps[:, 0, :], LN_EPS).then_inc(made, 1)
            nc.gpsimd.memset(eps[:, 1, :], RMS_EPS).then_inc(made, 1)
            pool.wait_ge(made, 5)
            nc.gpsimd.affine_select(out=ident[:], in_=ident[:], compare_op=ALU.not_equal, fill=1.0, base=0,
                                    pattern=[[-1, P]], channel_multiplier=1).then_inc(made, 1)
            nc.gpsimd.affine_select(out=causal[:], in_=causal[:], compare_op=ALU.is_ge, fill=MASKED, base=0,
                                    pattern=[[-1, P]], channel_multiplier=1).then_inc(made, 1)
            pool.wait_ge(made, 7)
            nc.gpsimd.tensor_copy(ident16[:], ident[:]).then_inc(made, 1)


def cross_attention(nc, sem, ps, ident, neg_half, eps, HS, hT, x, ctxT, wqkT, bqk, ln1, spill):
    NU = 2
    n_of = lambda g, u: NU * g + u
    with ExitStack() as ctx:
        sb = lambda name, shape, dt=F32: ctx.enter_context(nc.sbuf_tensor(name, shape, dt))
        X = [sb(f"x_{u}", [P, ST, S]) for u in range(NU)]
        feat = [sb(f"feat_{u}", [P, CC, S]) for u in range(NU)]
        feat_s = [sb(f"feat_{s}", [P, CC, S], F32R) for s in ("hi", "lo")]
        w_raw = sb("wqk_raw", [P, 2, CC, P])
        w_s = [sb(f"wqk1_{s}", [P, 2, CC, P], F32R) for s in ("hi", "lo")]
        bias = sb("bqk", [P, 2])
        ln1b = sb("ln1b", [P, D])
        qkT = [sb(f"qkT1_{s}", [P, 2, S], F32R) for s in ("hi", "lo")]
        xT = [sb(f"xT_{s}", [P, ST, S], F32R) for s in ("hi", "lo")]
        aT = [sb(f"aT_{s}", [P, ST, S], F32R) for s in ("hi", "lo")]
        prob = sb("prob1", [P, ST, S])
        norm = sb("norm1", [P, ST, S])
        st6 = sb("st6", [P, ST, 6])
        mv = sb("mv", [P, 2, ST, 2])
        rstd = sb("rstd", [P, 2, ST])
        ms = sb("ms", [P, ST])
        carry = sb("carry1", [P, 1])
        rms = sb("rms", [P, ST])
        negmax = sb("negmax1", [P, ST])
        rsum = sb("rsum1", [P, ST])
        rinv = sb("rinv1", [P, ST])

        ld_w, ld_x, ld_f = sem("ld_w"), [sem(f"ld_x{u}") for u in range(NU)], [sem(f"ld_f{u}") for u in range(NU)]
        spilled = [sem(f"spilled{u}") for u in range(NU)]
        act_w, dve_w = sem("act_w1"), sem("dve_w1")
        act_f, dve_f = sem("act_f"), sem("dve_f")
        pe_qk, act_qk, dve_qk = sem("pe_qk1"), sem("act_qk1"), sem("dve_qk1")
        dve_st, dve_mv, pool_r, dve_xn = sem("dve_st"), sem("dve_mv"), sem("pool_r"), sem("dve_xn")
        pe_t, act_t, dve_t = sem("pe_t1"), sem("act_t1"), sem("dve_t1")
        pe_e, dve_max, act_exp = sem("pe_e1"), sem("dve_max1"), sem("act_exp1")
        dve_ri, dve_nrm = sem("dve_ri1"), sem("dve_nrm")
        pe_m, dve_x1 = sem("pe_m"), sem("dve_x1")
        dve_hs, dve_h, pool_p = sem("dve_hs"), sem("dve_h1"), sem("pool_p1")

        block = ctx.enter_context(nc.Block())

        @block.sync
        def _(sp):
            sp.dma_start(w_raw[:], wqkT).then_inc(ld_w, 16)
            sp.dma_start(bias[:], bqk).then_inc(ld_w, 16)
            sp.dma_start(ln1b[:], ln1.partition_broadcast(P)).then_inc(ld_w, 16)
            for u in range(NU):
                sp.dma_start(feat[u][:], ctxT[u]).then_inc(ld_f[u], 16)
                sp.dma_start(X[u][:], x[u]).then_inc(ld_x[u], 16)
            with sp.Fori(0, NB // NU) as g:
                for u in range(NU):
                    n = n_of(g, u)
                    sp.wait_ge(dve_x1, ST * n + ST)
                    sp.dma_start(spill[bass.ds(n, 1)].rearrange("a p t n -> p (a t) n"), X[u][:]).then_inc(spilled[u], 16)
                    nxt = NU + u
                    sp.wait_ge(dve_f, n + 1)
                    sp.dma_start(feat[u][:], ctxT[nxt]).then_inc(ld_f[u], 16)
                    sp.wait_ge(dve_hs, ST * n + ST)
                    sp.wait_ge(spilled[u], 16 * g + 16)
                    sp.dma_start(X[u][:], x[nxt]).then_inc(ld_x[u], 16)
            for u in range(NU):
                sp.wait_ge(ld_f[u], 48)
                sp.wait_ge(ld_x[u], 48)

        @block.gpsimd
        def _(pool):
            with pool.Fori(0, NB // NU) as g:
                for u in range(NU):
                    n = n_of(g, u)
                    pool.wait_ge(dve_mv, 2 * ST * n + ST)
                    nc.gpsimd.tensor_tensor(rstd[:, 0, :], mv[:, 0, :, 1], eps[:, 0, :], ALU.add).then_inc(pool_p, 1)
                    pool.wait_ge(pool_p, 6 * n + 1)
                    nc.gpsimd.tensor_tensor(rstd[:, 0, :], rstd[:, 0, :], neg_half[:, 0:ST], ALU.pow).then_inc(pool_r, 1)
                    pool.wait_ge(dve_mv, 2 * ST * n + 2 * ST)
                    nc.gpsimd.tensor_tensor(rstd[:, 1, :], mv[:, 1, :, 1], eps[:, 0, :], ALU.add).then_inc(pool_p, 1)
                    pool.wait_ge(pool_p, 6 * n + 2)
                    nc.gpsimd.tensor_tensor(rstd[:, 1, :], rstd[:, 1, :], neg_half[:, 0:ST], ALU.pow).then_inc(pool_p, 1)
                    pool.wait_ge(pool_p, 6 * n + 3)
                    nc.gpsimd.tensor_tensor(ms[:], mv[:, 1, :, 1], rstd[:, 1, :], ALU.mult).then_inc(pool_p, 1)
                    pool.wait_ge(pool_p, 6 * n + 4)
                    nc.gpsimd.tensor_tensor(ms[:], ms[:], rstd[:, 1, :], ALU.mult).then_inc(pool_p, 1)
                    pool.wait_ge(pool_p, 6 * n + 5)
                    nc.gpsimd.tensor_tensor(rms[:], ms[:], eps[:, 1, :], ALU.add).then_inc(pool_p, 1)
                    pool.wait_ge(pool_p, 6 * n + 6)
                    nc.gpsimd.tensor_tensor(rms[:], rms[:], neg_half[:, 0:ST], ALU.pow).then_inc(pool_r, 1)

        @block.tensor
        def _(pe):
            def transposed(src, i):
                for j in range(ST):
                    last = nc.tensor.transpose(ps[4 + i % 2][:, j * P:(j + 1) * P], src[:, i, j * P:(j + 1) * P], ident[:])
                last.then_inc(pe_t, 1)

            pe.wait_ge(dve_w, 1)
            with pe.Fori(0, NB // NU) as g:
                for u in range(NU):
                    n = n_of(g, u)
                    tiles = 3 * ST * n
                    pe.wait_ge(dve_f, n + 1)
                    pe.wait_ge(dve_qk, 2 * n)
                    for m in range(2):
                        for c in range(CC):
                            last = matmul3(nc, ps[m][:], [w[:, m, c, :] for w in w_s], [f[:, c, :] for f in feat_s],
                                           c == 0, c == CC - 1)
                        last.then_inc(pe_qk, 1)
                    for i in range(ST):
                        pe.wait_ge(dve_xn, ST * n + i + 1)
                        pe.wait_ge(dve_t, tiles + max(i - 1, 0))
                        transposed(norm, i)
                    pe.wait_ge(dve_qk, 2 * n + 2)
                    for i in range(ST):
                        if i >= 2:
                            pe.wait_ge(act_exp, ST * n + i - 1)
                        matmul3(nc, ps[2 + i % 2][:], [q[:, 0, i * P:(i + 1) * P] for q in qkT],
                                [k[:, 1, :] for k in qkT], True, True).then_inc(pe_e, 1)
                    for i in range(ST):
                        pe.wait_ge(dve_nrm, ST * n + i + 1)
                        pe.wait_ge(dve_t, tiles + ST + i - 1)
                        transposed(prob, i)
                    pe.wait_ge(dve_t, tiles + 2 * ST)
                    pe.wait_ge(dve_x1, ST * n)
                    for i in range(ST):
                        if i >= 2:
                            pe.wait_ge(dve_x1, ST * n + i - 1)
                        for j in range(ST):
                            last = matmul3(nc, ps[6 + i % 2][:], [a[:, j, i * P:(i + 1) * P] for a in xT],
                                           [a[:, j, :] for a in aT], j == 0, j == ST - 1)
                        last.then_inc(pe_m, 1)
                    for i in range(ST):
                        pe.wait_ge(dve_h, ST * n + i + 1)
                        pe.wait_ge(dve_t, tiles + 2 * ST + i - 1)
                        transposed(norm, i)

        @block.scalar
        def _(act):
            act.wait_ge(ld_w, 48)
            nc.scalar.copy(w_s[0][:], w_raw[:]).then_inc(act_w, 1)
            with act.Fori(0, NB // NU) as g:
                for u in range(NU):
                    n = n_of(g, u)
                    tiles = 3 * ST * n
                    act.wait_ge(ld_f[u], 16 * g + 16)
                    act.wait_ge(pe_qk, 2 * n)
                    nc.scalar.copy(feat_s[0][:], feat[u][:]).then_inc(act_f, 1)
                    for m in range(2):
                        act.wait_ge(pe_qk, 2 * n + m + 1)
                        nc.scalar.activation(qkT[0][:, m, :], ps[m][:], ACT.Identity, bias=bias[:, m:m + 1]).then_inc(act_qk, 1)
                    for i in range(ST):
                        act.wait_ge(pe_t, tiles + i + 1)
                        nc.scalar.copy(xT[0][:, :, i * P:(i + 1) * P],
                                       ps[4 + i % 2][:].rearrange("p (j t) -> p j t", j=ST)).then_inc(act_t, 1)
                    for i in range(ST):
                        act.wait_ge(dve_max, ST * n + i + 1)
                        nc.scalar.activation(prob[:, i, :], ps[2 + i % 2][:], ACT.Exp, bias=negmax[:, i:i + 1],
                                             accum_out=rsum[:, i:i + 1]).then_inc(act_exp, 1)
                    for i in range(ST):
                        act.wait_ge(pe_t, tiles + ST + i + 1)
                        nc.scalar.copy(aT[0][:, :, i * P:(i + 1) * P],
                                       ps[4 + i % 2][:].rearrange("p (j t) -> p j t", j=ST)).then_inc(act_t, 1)
                    for i in range(ST):
                        act.wait_ge(pe_t, tiles + 2 * ST + i + 1)
                        nc.scalar.copy(hT[0][:, :, bass.ds((ST * n + i) * P, P)],
                                       ps[4 + i % 2][:].rearrange("p (j t) -> p j t", j=DC)).then_inc(act_t, 1)

        @block.vector
        def _(dve):
            def stats(src, which, n, row):
                for i in range(ST):
                    if which:
                        dve.wait_ge(dve_x1, ST * n + i + 1)
                    nc.vector.bn_stats(st6[:, i, :], src[:, i, :]).then_inc(dve_st, 1)
                dve.wait_ge(dve_st, row + ST)
                nc.vector.memset(carry[:], 0.0)
                for i in range(ST):
                    nc.vector.bn_aggr(mv[:, which, i, :], st6[:, i, :]).then_inc(dve_mv, 1)

            def low_of_tile(lo, hi, i, done):
                dve.wait_ge(act_t, done)
                nc.vector.tensor_tensor(lo, ps[4 + i % 2][:].rearrange("p (j t) -> p j t", j=ST),
                                        hi.bitcast(F32), ALU.subtract).then_inc(dve_t, 1)

            dve.wait_ge(ld_w, 48)
            dve.wait_ge(act_w, 1)
            nc.vector.tensor_tensor(w_s[1][:], w_raw[:], w_s[0][:].bitcast(F32), ALU.subtract).then_inc(dve_w, 1)
            with dve.Fori(0, NB // NU) as g:
                for u in range(NU):
                    n = n_of(g, u)
                    tiles = 3 * ST * n
                    dve.wait_ge(ld_x[u], 16 * g + 16)
                    stats(X[u], 0, n, 2 * ST * n)
                    dve.wait_ge(ld_f[u], 16 * g + 16)
                    dve.wait_ge(act_f, n + 1)
                    nc.vector.tensor_tensor(feat_s[1][:], feat[u][:], feat_s[0][:].bitcast(F32), ALU.subtract).then_inc(dve_f, 1)
                    dve.wait_ge(pool_r, 2 * n + 1)
                    dve.wait_ge(dve_mv, 2 * ST * n + ST)
                    for i in range(ST):
                        nc.vector.tensor_scalar(norm[:, i, :], X[u][:, i, :], mv[:, 0, i, 0:1], rstd[:, 0, i:i + 1],
                                                ALU.subtract, ALU.mult).then_inc(dve_xn, 1)
                    for m in range(2):
                        dve.wait_ge(act_qk, 2 * n + m + 1)
                        nc.vector.scalar_tensor_tensor(out=qkT[1][:, m, :], in0=ps[m][:], scalar=bias[:, m:m + 1],
                                                       in1=qkT[0][:, m, :].bitcast(F32), op0=ALU.add,
                                                       op1=ALU.subtract).then_inc(dve_qk, 1)
                    for i in range(ST):
                        w = slice(i * P, (i + 1) * P)
                        low_of_tile(xT[1][:, :, w], xT[0][:, :, w], i, tiles + i + 1)
                    for i in range(ST):
                        dve.wait_ge(pe_e, ST * n + i + 1)
                        nc.vector.tensor_reduce(negmax[:, i:i + 1], ps[2 + i % 2][:], AX.X, ALU.max,
                                                negate=True).then_inc(dve_max, 1)
                    for i in range(ST):
                        dve.wait_ge(act_exp, ST * n + i + 1)
                        nc.vector.reciprocal(rinv[:, i:i + 1], rsum[:, i:i + 1]).then_inc(dve_ri, 1)
                        dve.wait_ge(dve_ri, ST * n + i + 1)
                        nc.vector.tensor_scalar(prob[:, i, :], prob[:, i, :], rinv[:, i:i + 1], None,
                                                ALU.mult).then_inc(dve_nrm, 1)
                    for i in range(ST):
                        w = slice(i * P, (i + 1) * P)
                        low_of_tile(aT[1][:, :, w], aT[0][:, :, w], i, tiles + ST + i + 1)
                    for i in range(ST):
                        dve.wait_ge(pe_m, ST * n + i + 1)
                        nc.vector.tensor_tensor(X[u][:, i, :], ps[6 + i % 2][:], X[u][:, i, :], ALU.add).then_inc(dve_x1, 1)
                    stats(X[u], 1, n, 2 * ST * n + ST)
                    dve.wait_ge(pool_r, 2 * n + 2)
                    dve.wait_ge(dve_mv, 2 * ST * n + 2 * ST)
                    for i in range(ST):
                        row = bass.ds((ST * n + i) * D, D)
                        nc.vector.tensor_scalar(HS[:, row], X[u][:, i, :], mv[:, 1, i, 0:1], rstd[:, 1, i:i + 1],
                                                ALU.subtract, ALU.mult).then_inc(dve_hs, 1)
                        dve.wait_ge(dve_hs, ST * n + i + 1)
                        nc.vector.scalar_tensor_tensor(out=norm[:, i, :], in0=HS[:, row], scalar=rms[:, i:i + 1],
                                                       in1=ln1b[:], op0=ALU.mult, op1=ALU.mult).then_inc(dve_h, 1)
                    for i in range(ST):
                        w = bass.ds((ST * n + i) * P, P)
                        low_of_tile(hT[1][:, :, w], hT[0][:, :, w], i, tiles + 2 * ST + i + 1)


def self_attention(nc, sem, ps, ident, ident16, causal, HS, hT, wqk, wv, wo):
    STEPS = 2 * NB
    VG = TT // 2
    with ExitStack() as ctx:
        sb = lambda name, shape, dt=F32: ctx.enter_context(nc.sbuf_tensor(name, shape, dt))
        raw = [sb(f"w_raw{r}", [P, 1024]) for r in range(2)]
        wqk_s = [[sb(f"wqk_{hh}{s}", [P, 2, DC, HD], F32R) for s in ("hi", "lo")] for hh in range(2)]
        wv_s = [sb(f"wv_{s}", [P, DC, 2 * HD], F32R) for s in ("hi", "lo")]
        wo_s = [sb(f"wo_{s}", [P, 2, D], F32R) for s in ("hi", "lo")]
        v_s = [sb(f"v_{s}", [P, TT, 2 * HD], F32R) for s in ("hi", "lo")]
        qkT = [sb(f"qkT_{s}", [P, 2, S], F32R) for s in ("hi", "lo")]
        prob = sb("prob", [P, ST, S])
        pT = [sb(f"pT_{s}", [P, ST, S], F32R) for s in ("hi", "lo")]
        oT = [sb(f"oT_{s}", [P, S], F32R) for s in ("hi", "lo")]
        negmax = sb("negmax", [P, 2, ST])
        rsum = sb("rsum", [P, 2, ST])
        rinv = sb("rinv", [P, 2, ST])
        zero = sb("zero", [P, 1])
        ps_s, ps_t, ps_p, ps_w = ps[0:2], ps[2:4], ps[4:6], ps[6:8]
        ps_o = ps_t[0]
        SCALE = float(HD) ** -0.5
        width = [max(2, i + 1) * P for i in range(ST)]
        first = [0, P, 2 * P, 2 * P]

        ld_raw = [sem(f"ld_raw{r}") for r in range(2)]
        pool_hi, pool_lo, pool_0 = sem("pool_hi"), sem("pool_lo"), sem("pool_0")
        pe_qk, act_qk, dve_qk = sem("pe_qk"), sem("act_qk"), sem("dve_qk")
        pe_v, act_v, dve_v = sem("pe_v"), sem("act_v"), sem("dve_v")
        pe_s, dve_max, act_exp = sem("pe_s"), sem("dve_max"), sem("act_exp")
        pe_t, act_t, dve_t = sem("pe_t"), sem("act_t"), sem("dve_t")
        pe_o, act_o, dve_o = sem("pe_o"), sem("act_o"), sem("dve_o")
        dve_ri, pe_w, dve_acc = sem("dve_ri"), sem("pe_w"), sem("dve_acc")

        JOBS = 4
        block = ctx.enter_context(nc.Block())

        @block.sync
        def _(sp):
            with sp.Fori(0, HP) as g:
                for job in range(JOBS):
                    r = job % 2
                    src = [wqk[bass.ds(2 * g, 1)], wv[bass.ds(g, 1)], wqk[bass.ds(2 * g + 1, 1)], wo[bass.ds(g, 1)]][job]
                    if job >= 2:
                        sp.wait_ge(pool_lo, JOBS * g + job - 1)
                    else:
                        sp.wait_ge(pool_lo, JOBS * g)
                    sp.dma_start(raw[r][:], src.rearrange("a p n -> p (a n)")).then_inc(ld_raw[r], 16)

        @block.gpsimd
        def _(pool):
            for buf in oT + wo_s:
                nc.gpsimd.memset(buf[:].bitcast(F32), 0.0).then_inc(pool_0, 1)
            for buf in pT:
                nc.gpsimd.memset(buf[:].bitcast(F32), 0.0).then_inc(pool_0, 1)
            nc.gpsimd.memset(rinv[:], 0.0).then_inc(pool_0, 1)
            nc.gpsimd.memset(zero[:], 0.0).then_inc(pool_0, 1)
            pool.wait_ge(pool_0, 8)
            with pool.Fori(0, HP) as g:
                for job in range(JOBS):
                    r = job % 2
                    dst = [[w[:].rearrange("p a c n -> p (a c n)") for w in wqk_s[0]],
                           [w[:].rearrange("p c n -> p (c n)") for w in wv_s],
                           [w[:].rearrange("p a c n -> p (a c n)") for w in wqk_s[1]],
                           [w[:].rearrange("p a n -> p (a n)") for w in wo_s]][job]
                    pool.wait_ge(ld_raw[r], 32 * g + 16 * (job // 2) + 16)
                    if job == 0:
                        pool.wait_ge(pe_qk, 2 * STEPS * g)
                    elif job == 1:
                        pool.wait_ge(pe_v, VG * g)
                    elif job == 3:
                        pool.wait_ge(pe_w, ST * (STEPS * g + 1))
                    nc.gpsimd.tensor_tensor(dst[0], raw[r][:], zero[:].to_broadcast([P, 1024]), ALU.add).then_inc(pool_hi, 1)
                    pool.wait_ge(pool_hi, JOBS * g + job + 1)
                    nc.gpsimd.tensor_tensor(dst[1], raw[r][:], dst[0].bitcast(F32), ALU.subtract).then_inc(pool_lo, 1)

        @block.tensor
        def _(pe):
            def project(hh, b, m):
                for c in range(DC):
                    last = matmul3(nc, ps_p[m][:], [w[:, m, c, :] for w in wqk_s[hh]],
                                   [h[:, c, b * S:(b + 1) * S] for h in hT], c == 0, c == DC - 1)
                last.then_inc(pe_qk, 1)

            def output(s, i, n):
                hh = (s - 1) % STEPS // NB
                if i < 2:
                    pe.wait_ge(dve_acc, ST * n)
                else:
                    pe.wait_ge(dve_acc, ST * n + i - 1)
                matmul3(nc, ps_w[i % 2][:], [o[:, i * P:(i + 1) * P] for o in oT], [w[:, hh, :] for w in wo_s],
                        True, True).then_inc(pe_w, 1)

            pe.wait_ge(pool_0, 8)
            with pe.Fori(0, HP) as g:
                pe.wait_ge(pool_lo, JOBS * g + 1)
                project(0, 0, 0)
                project(0, 0, 1)
                pe.wait_ge(pool_lo, JOBS * g + 2)
                for v in range(VG):
                    if v < 2:
                        pe.wait_ge(dve_qk, 2 * STEPS * g + v + 1)
                    else:
                        pe.wait_ge(dve_v, VG * g + v - 1)
                    for k in range(2):
                        for c in range(DC):
                            last = matmul3(nc, ps_p[v % 2][:, k * 2 * HD:(k + 1) * 2 * HD],
                                           [h[:, c, (2 * v + k) * P:(2 * v + k + 1) * P] for h in hT],
                                           [w[:, c, :] for w in wv_s], c == 0, c == DC - 1)
                    last.then_inc(pe_v, 1)
                for s in range(STEPS):
                    hh, b = s // NB, s % NB
                    n = STEPS * g + s
                    pe.wait_ge(dve_qk, 2 * n + 2)
                    for i in range(ST):
                        if i >= 2:
                            pe.wait_ge(act_exp, ST * n + i - 1)
                        matmul = [q[:, 0, i * P:(i + 1) * P] for q in qkT], [k[:, 1, 0:width[i]] for k in qkT]
                        matmul3(nc, ps_s[i % 2][:, 0:width[i]], *matmul, True, False)
                        nc.tensor.matmul(ps_s[i % 2][:, i * P:(i + 1) * P], ident16[:], causal[:],
                                         start=False, stop=True).then_inc(pe_s, 1)
                    if s + 1 < STEPS:
                        if s == 0:
                            pe.wait_ge(dve_v, VG * g + VG)
                        if s + 1 == NB:
                            pe.wait_ge(pool_lo, JOBS * g + 3)
                        for m in range(2):
                            project((s + 1) // NB, (s + 1) % NB, m)
                    for i in range(ST):
                        pe.wait_ge(act_exp, ST * n + i + 1)
                        if i >= 2:
                            pe.wait_ge(dve_t, ST * n + i - 1)
                        elif i == 0:
                            pe.wait_ge(dve_o, n)
                        for j in range(i + 1):
                            last = nc.tensor.transpose(ps_t[i % 2][:, j * P:(j + 1) * P], prob[:, i, j * P:(j + 1) * P], ident[:])
                        last.then_inc(pe_t, 1)
                        if s == 1 and i == 0:
                            pe.wait_ge(pool_lo, JOBS * g + 4)
                        output(s, i, n)
                    pe.wait_ge(dve_t, ST * n + ST)
                    for j in range(ST):
                        last = matmul3(nc, ps_o[:, first[j]:S],
                                       [v[:, b * ST + j, hh * HD:(hh + 1) * HD] for v in v_s],
                                       [p[:, j, first[j]:S] for p in pT], j == 0, j == ST - 1)
                    last.then_inc(pe_o, 1)
            pe.wait_ge(dve_o, STEPS * HP)
            for i in range(ST):
                output(0, i, STEPS * HP)

        @block.scalar
        def _(act):
            def high_qk(m, done):
                act.wait_ge(pe_qk, done)
                nc.scalar.mul(qkT[0][:, m, :], ps_p[m][:], SCALE if m == 0 else 1.0).then_inc(act_qk, 1)

            act.wait_ge(pool_0, 8)
            with act.Fori(0, HP) as g:
                high_qk(0, 2 * STEPS * g + 1)
                high_qk(1, 2 * STEPS * g + 2)
                for v in range(VG):
                    act.wait_ge(pe_v, VG * g + v + 1)
                    nc.scalar.copy(v_s[0][:, 2 * v:2 * v + 2, :],
                                   ps_p[v % 2][:].rearrange("p (k n) -> p k n", k=2)).then_inc(act_v, 1)
                for s in range(STEPS):
                    n = STEPS * g + s
                    for i in range(ST):
                        act.wait_ge(dve_max, ST * n + i + 1)
                        nc.scalar.activation(prob[:, i, 0:(i + 1) * P], ps_s[i % 2][:, 0:(i + 1) * P], ACT.Exp,
                                             bias=negmax[:, s % 2, i:i + 1],
                                             accum_out=rsum[:, s % 2, i:i + 1]).then_inc(act_exp, 1)
                    if s + 1 < STEPS:
                        high_qk(0, 2 * n + 3)
                        high_qk(1, 2 * n + 4)
                    for i in range(ST):
                        act.wait_ge(pe_t, ST * n + i + 1)
                        nc.scalar.copy(pT[0][:, 0:i + 1, i * P:(i + 1) * P],
                                       ps_t[i % 2][:, 0:(i + 1) * P].rearrange("p (j t) -> p j t", t=P)).then_inc(act_t, 1)
                    act.wait_ge(pe_o, n + 1)
                    nc.scalar.copy(oT[0][:], ps_o[:]).then_inc(act_o, 1)

        @block.vector
        def _(dve):
            def low_qk(m, done):
                dve.wait_ge(act_qk, done)
                nc.vector.scalar_tensor_tensor(out=qkT[1][:, m, :], in0=ps_p[m][:], scalar=SCALE if m == 0 else 1.0,
                                               in1=qkT[0][:, m, :].bitcast(F32), op0=ALU.mult,
                                               op1=ALU.subtract).then_inc(dve_qk, 1)

            def add_output(s, i, n):
                tile = (s - 1) % NB * ST + i
                dve.wait_ge(pe_w, ST * n + i + 1)
                hs = HS[:, tile * D:(tile + 1) * D]
                nc.vector.scalar_tensor_tensor(out=hs, in0=ps_w[i % 2][:], scalar=rinv[:, (s - 1) % 2, i:i + 1], in1=hs,
                                               op0=ALU.mult, op1=ALU.add).then_inc(dve_acc, 1)

            dve.wait_ge(pool_0, 8)
            with dve.Fori(0, HP) as g:
                low_qk(0, 2 * STEPS * g + 1)
                low_qk(1, 2 * STEPS * g + 2)
                for v in range(VG):
                    dve.wait_ge(act_v, VG * g + v + 1)
                    nc.vector.tensor_tensor(v_s[1][:, 2 * v:2 * v + 2, :], ps_p[v % 2][:].rearrange("p (k n) -> p k n", k=2),
                                            v_s[0][:, 2 * v:2 * v + 2, :].bitcast(F32), ALU.subtract).then_inc(dve_v, 1)
                for s in range(STEPS):
                    n = STEPS * g + s
                    for i in range(ST):
                        dve.wait_ge(pe_s, ST * n + i + 1)
                        nc.vector.tensor_reduce(negmax[:, s % 2, i:i + 1], ps_s[i % 2][:, 0:(i + 1) * P], AX.X,
                                                ALU.max, negate=True).then_inc(dve_max, 1)
                    if s + 1 < STEPS:
                        low_qk(0, 2 * n + 3)
                        low_qk(1, 2 * n + 4)
                    dve.wait_ge(act_exp, ST * n + ST)
                    nc.vector.reciprocal(rinv[:, s % 2, :], rsum[:, s % 2, :]).then_inc(dve_ri, 1)
                    dve.wait_ge(dve_ri, n)
                    dve.wait_ge(dve_acc, ST * n)
                    for i in range(ST):
                        dve.wait_ge(act_t, ST * n + i + 1)
                        w = slice(i * P, (i + 1) * P)
                        nc.vector.tensor_tensor(pT[1][:, 0:i + 1, w], ps_t[i % 2][:, 0:(i + 1) * P].rearrange("p (j t) -> p j t", t=P),
                                                pT[0][:, 0:i + 1, w].bitcast(F32), ALU.subtract).then_inc(dve_t, 1)
                        add_output(s, i, n)
                    dve.wait_ge(act_o, n + 1)
                    nc.vector.tensor_tensor(oT[1][:], ps_o[:], oT[0][:].bitcast(F32), ALU.subtract).then_inc(dve_o, 1)
            dve.wait_ge(dve_ri, STEPS * HP)
            dve.wait_ge(dve_acc, ST * STEPS * HP)
            for i in range(ST):
                add_output(0, i, STEPS * HP)


def route(nc, sem, ps, ident, neg_half, eps, HS, hT, cw, ln2, gateT, spill):
    NG = TT // ST
    with ExitStack() as ctx:
        sb = lambda name, shape, dt=F32: ctx.enter_context(nc.sbuf_tensor(name, shape, dt))
        x1 = [sb(f"x1_{u}", [P, ST, D]) for u in range(2)]
        ln2b = sb("ln2b", [P, D])
        gate = sb("gate", [P, DC, P])
        gate_s = [sb(f"gate_{s}", [P, DC, P], F32R) for s in ("hi", "lo")]
        norm = sb("norm3", [P, ST, D])
        st6 = sb("st6_3", [P, ST, 6])
        mv = sb("mv3", [P, ST, 2])
        ms = sb("ms3", [P, 2, ST])
        rms = sb("rms3", [P, ST])
        carry = sb("carry3", [P, 1])
        logT = sb("logT", [P, T])
        ex = sb("ex", [P, TT, E])
        mx = sb("mx", [P, TT])
        top = sb("top", [P, TT, 8])
        gt = sb("gt", [P, TT, E])
        eq = sb("eq", [P, TT, E])
        cum = [sb(f"cum{k}", [P, TT, E]) for k in range(2)]
        cnt = sb("cnt", [P, TT])
        wide = lambda a: a.unsqueeze(2).to_broadcast([P, TT, E])

        ld_g, ld_x1 = sem("ld_g"), [sem(f"ld_x1{u}") for u in range(2)]
        pool_z, act_g, dve_g = sem("pool_z"), sem("act_g"), sem("dve_g")
        dve_st, dve_mv, pool_p, pool_r = sem("dve_st3"), sem("dve_mv3"), sem("pool_p3"), sem("pool_r3")
        dve_h, pe_t, act_t, dve_t = sem("dve_h3"), sem("pe_t3"), sem("act_t3"), sem("dve_t3")
        pool_a = sem("pool_a")
        pe_l, act_l, pe_lt, dve_c, act_e = sem("pe_l"), sem("act_l"), sem("pe_lt"), sem("dve_c"), sem("act_e3")

        block = ctx.enter_context(nc.Block())

        @block.sync
        def _(sp):
            sp.dma_start(ln2b[:], ln2.partition_broadcast(P)).then_inc(ld_g, 16)
            sp.wait_ge(pool_z, 1)
            sp.dma_start(gate[:, :, 0:E], gateT).then_inc(ld_g, 16)
            with sp.Fori(0, NG // 2) as g:
                for u in range(2):
                    sp.wait_ge(pool_a, ST * (2 * g))
                    sp.dma_start(x1[u][:], spill[bass.ds(2 * g + u, 1)].rearrange("a p t n -> p (a t) n")).then_inc(ld_x1[u], 16)

        @block.gpsimd
        def _(pool):
            nc.gpsimd.memset(gate[:], 0.0).then_inc(pool_z, 1)
            with pool.Fori(0, NG // 2) as g2:
                for u in range(2):
                    g = 2 * g2 + u
                    pool.wait_ge(dve_mv, ST * g + ST)
                    nc.gpsimd.tensor_tensor(ms[:, 0, :], mv[:, :, 0], mv[:, :, 0], ALU.mult).then_inc(pool_p, 1)
                    pool.wait_ge(pool_p, 3 * g + 1)
                    nc.gpsimd.tensor_tensor(ms[:, 0, :], ms[:, 0, :], mv[:, :, 1], ALU.add).then_inc(pool_p, 1)
                    pool.wait_ge(pool_p, 3 * g + 2)
                    nc.gpsimd.tensor_tensor(ms[:, 1, :], ms[:, 0, :], eps[:, 1, :], ALU.add).then_inc(pool_p, 1)
                    pool.wait_ge(pool_p, 3 * g + 3)
                    nc.gpsimd.tensor_tensor(rms[:], ms[:, 1, :], neg_half[:, 0:ST], ALU.pow).then_inc(pool_r, 1)
                    pool.wait_ge(ld_x1[u], 16 * g2 + 16)
                    for i in range(ST):
                        row = bass.ds((ST * g + i) * D, D)
                        pool.wait_ge(dve_h, ST * g + i + 1)
                        nc.gpsimd.tensor_tensor(HS[:, row], HS[:, row], x1[u][:, i, :], ALU.add).then_inc(pool_a, 1)

        @block.tensor
        def _(pe):
            pe.wait_ge(dve_g, 1)
            with pe.Fori(0, NG) as g:
                for i in range(ST):
                    pe.wait_ge(dve_h, ST * g + i + 1)
                    pe.wait_ge(dve_t, ST * g + max(i - 1, 0))
                    for j in range(DC):
                        last = nc.tensor.transpose(ps[i % 2][:, j * P:(j + 1) * P], norm[:, i, j * P:(j + 1) * P], ident[:])
                    last.then_inc(pe_t, 1)
                pe.wait_ge(dve_t, ST * g + ST)
                pe.wait_ge(act_l, g)
                for c in range(DC):
                    last = matmul3(nc, ps[2][:], [w[:, c, :] for w in gate_s],
                                   [h[:, c, bass.ds(g * S, S)] for h in hT], c == 0, c == DC - 1)
                last.then_inc(pe_l, 1)
            pe.wait_ge(act_l, NG)
            for t in range(TT):
                last = nc.tensor.transpose(ps[3][:, t * E:(t + 1) * E], logT[0:E, t * P:(t + 1) * P], ident[0:E, 0:E])
            last.then_inc(pe_lt, 1)

        @block.scalar
        def _(act):
            act.wait_ge(ld_g, 32)
            nc.scalar.copy(gate_s[0][:], gate[:]).then_inc(act_g, 1)
            with act.Fori(0, NG) as g:
                for i in range(ST):
                    act.wait_ge(pe_t, ST * g + i + 1)
                    nc.scalar.copy(hT[0][:, :, bass.ds((ST * g + i) * P, P)],
                                   ps[i % 2][:].rearrange("p (j t) -> p j t", j=DC)).then_inc(act_t, 1)
                act.wait_ge(pe_l, g + 1)
                nc.scalar.copy(logT[:, bass.ds(g * S, S)], ps[2][:]).then_inc(act_l, 1)
            act.wait_ge(dve_c, 2)
            nc.scalar.activation(ex[:], gt[:], ACT.Exp).then_inc(act_e, 1)

        @block.vector
        def _(dve):
            dve.wait_ge(ld_g, 32)
            dve.wait_ge(act_g, 1)
            nc.vector.tensor_tensor(gate_s[1][:], gate[:], gate_s[0][:].bitcast(F32), ALU.subtract).then_inc(dve_g, 1)
            with dve.Fori(0, NG) as g:
                for i in range(ST):
                    nc.vector.bn_stats(st6[:, i, :], HS[:, bass.ds((ST * g + i) * D, D)]).then_inc(dve_st, 1)
                dve.wait_ge(dve_st, ST * g + ST)
                nc.vector.memset(carry[:], 0.0)
                for i in range(ST):
                    nc.vector.bn_aggr(mv[:, i, :], st6[:, i, :]).then_inc(dve_mv, 1)
                dve.wait_ge(pool_r, g + 1)
                for i in range(ST):
                    nc.vector.scalar_tensor_tensor(out=norm[:, i, :], in0=HS[:, bass.ds((ST * g + i) * D, D)],
                                                   scalar=rms[:, i:i + 1], in1=ln2b[:], op0=ALU.mult,
                                                   op1=ALU.mult).then_inc(dve_h, 1)
                for i in range(ST):
                    w = bass.ds((ST * g + i) * P, P)
                    dve.wait_ge(act_t, ST * g + i + 1)
                    nc.vector.tensor_tensor(hT[1][:, :, w], ps[i % 2][:].rearrange("p (j t) -> p j t", j=DC),
                                            hT[0][:, :, w].bitcast(F32), ALU.subtract).then_inc(dve_t, 1)
            done = [0]

            def step(ins):
                done[0] += 1
                ins.then_inc(dve_c, 1)
                dve.wait_ge(dve_c, done[0])

            dve.wait_ge(pe_lt, 1)
            logits = ps[3][:, 0:TT * E].rearrange("p (t e) -> p t e", e=E)
            step(nc.vector.tensor_reduce(mx[:], logits, AX.X, ALU.max))
            step(nc.vector.tensor_tensor(gt[:], logits, wide(mx[:]), ALU.subtract))
            dve.wait_ge(act_e, 1)
            for t in range(TT):
                last = nc.vector.max(top[:, t, :], ex[:, t, :])
            step(last)
            sixth = wide(top[:, :, TOPK - 1])
            step(nc.vector.tensor_tensor(gt[:], ex[:], sixth, ALU.is_gt))
            step(nc.vector.tensor_tensor(eq[:], ex[:], sixth, ALU.is_equal))
            step(nc.vector.tensor_reduce(cnt[:], gt[:], AX.X, ALU.add))
            step(nc.vector.tensor_scalar(cnt[:], cnt[:], -1.0, float(TOPK), ALU.mult, ALU.add))
            src = eq
            for k, dist in enumerate((1, 2, 4, 8)):
                dst = cum[k % 2]
                step(nc.vector.tensor_copy(dst[:, :, 0:dist], src[:, :, 0:dist]))
                step(nc.vector.tensor_tensor(dst[:, :, dist:E], src[:, :, dist:E], src[:, :, 0:E - dist], ALU.add))
                src = dst
            step(nc.vector.tensor_tensor(cum[0][:], src[:], wide(cnt[:]), ALU.is_le))
            step(nc.vector.tensor_tensor(eq[:], eq[:], cum[0][:], ALU.mult))
            step(nc.vector.tensor_tensor(gt[:], gt[:], eq[:], ALU.add))
            step(nc.vector.tensor_tensor(ex[:], ex[:], gt[:], ALU.mult))
            step(nc.vector.tensor_reduce(mx[:], ex[:], AX.X, ALU.add))
            step(nc.vector.reciprocal(cnt[:], mx[:]))
            step(nc.vector.tensor_tensor(cw[:, :, 0:E], ex[:], wide(cnt[:]), ALU.mult))
            step(nc.vector.memset(cw[:, :, E:NE], 1.0))


def experts(nc, sem, ps, HS, hT, cw, wgu, wdn, out):
    NBLK = T // S
    STEPS = 2 * NBLK
    TURNS = NE // 2
    JOBS = 3
    with ExitStack() as ctx:
        sb = lambda name, shape, dt=F32: ctx.enter_context(nc.sbuf_tensor(name, shape, dt))
        raw = sb("wx_raw", [P, len(IT) * D])
        wgu_s = [[sb(f"wgu_{k}{s}", [P, 2, DC, I], F32R) for s in ("hi", "lo")] for k in range(2)]
        wdn_s = [[sb(f"wdn_{k}{s}", [P, len(IT), D], F32R) for s in ("hi", "lo")] for k in range(2)]
        hh = [[sb(f"hh_{k}{s}", [P, len(IT), S], F32R) for s in ("hi", "lo")] for k in range(2)]
        silu = sb("silu", [P, S])
        prod = sb("prod", [P, S])
        cwe = sb("cwe", [P, 2, TT])
        zero = sb("zero4", [P, 1])
        ps_g, ps_u, ps_d = ps[0:2], ps[2:4], ps[4:8]

        ld_w, pool_hi, pool_lo, pool_0 = sem("ld_w4"), sem("pool_hi4"), sem("pool_lo4"), sem("pool_04")
        pe_g, pe_u, act_s, dve_p, act_h, dve_h = (sem(k) for k in ("pe_g", "pe_u", "act_s", "dve_p", "act_h4", "dve_h4"))
        pe_d, dve_acc, dve_cw, stored = sem("pe_d"), sem("dve_acc4"), sem("dve_cw"), sem("stored")
        NI = len(IT)
        block = ctx.enter_context(nc.Block())

        @block.sync
        def _(sp):
            with sp.Fori(0, NE) as e:
                for job in range(JOBS):
                    sp.wait_ge(pool_lo, JOBS * e + job)
                    if job < 2:
                        src = wgu[bass.ds(2 * e + job, 1)].rearrange("a p n -> p (a n)")
                        sp.dma_start(raw[:, 0:DC * I], src).then_inc(ld_w, 16)
                    else:
                        src = wdn[bass.ds(e, 1)].rearrange("a p n -> p (a n)")
                        sp.dma_start(raw[:], src).then_inc(ld_w, 16)
            for t in range(0, TT, ST):
                sp.wait_ge(dve_acc, ST * STEPS * TURNS + (ST if t == TT - ST else 0))
                sp.dma_start(out[t // ST], HS[:, t * D:(t + ST) * D].rearrange("p (t n) -> p t n", n=D)).then_inc(stored, 16)
            sp.wait_ge(stored, 16 * NB)

        @block.gpsimd
        def _(pool):
            for buf in hh[1] + wdn_s[1]:
                nc.gpsimd.memset(buf[:].bitcast(F32), 0.0).then_inc(pool_0, 1)
            nc.gpsimd.memset(cwe[:, 1, :], 0.0).then_inc(pool_0, 1)
            nc.gpsimd.memset(zero[:], 0.0).then_inc(pool_0, 1)
            pool.wait_ge(pool_0, 6)
            with pool.Fori(0, TURNS) as g:
                for k in range(2):
                    e = 2 * g + k
                    for job in range(JOBS):
                        n = DC * I if job < 2 else NI * D
                        pool.wait_ge(ld_w, 16 * (JOBS * e + job + 1))
                        if job < 2:
                            dst = [w[:, job].rearrange("p c n -> p (c n)") for w in wgu_s[k]]
                            pool.wait_ge(pe_u, NI * (NBLK * e - (NBLK if k else 0)))
                        else:
                            dst = [w[:].rearrange("p c n -> p (c n)") for w in wdn_s[k]]
                            pool.wait_ge(pe_d, ST * (NBLK * e - (NBLK - 1 if k else 0) + (0 if k else 0)))
                        nc.gpsimd.tensor_tensor(dst[0], raw[:, 0:n], zero[:].to_broadcast([P, n]), ALU.add).then_inc(pool_hi, 1)
                        pool.wait_ge(pool_hi, JOBS * e + job + 1)
                        nc.gpsimd.tensor_tensor(dst[1], raw[:, 0:n], dst[0].bitcast(F32), ALU.subtract).then_inc(pool_lo, 1)

        @block.tensor
        def _(pe):
            def down(s, n):
                k = (s - 1) % STEPS // NBLK
                for i in range(ST):
                    pe.wait_ge(dve_acc, ST * n)
                    for c, (_, w) in enumerate(IT):
                        last = matmul3(nc, ps_d[i][:], [h[0:w, c, i * P:(i + 1) * P] for h in hh[(s - 1) % 2]],
                                       [x[0:w, c, :] for x in wdn_s[k]], c == 0, c == NI - 1)
                    last.then_inc(pe_d, 1)

            pe.wait_ge(pool_0, 6)
            with pe.Fori(0, TURNS) as g:
                for s in range(STEPS):
                    k, blk = s // NBLK, s % NBLK
                    n = STEPS * g + s
                    if blk == 0:
                        pe.wait_ge(pool_lo, JOBS * (2 * g + k) + 2)
                    for c, (i0, w) in enumerate(IT):
                        if c >= 2:
                            pe.wait_ge(dve_p, NI * n + c - 1)
                        else:
                            pe.wait_ge(dve_p, NI * n)
                        for m, bank in enumerate((ps_g[c % 2], ps_u[c % 2])):
                            for j in range(DC):
                                last = matmul3(nc, bank[0:w, :], [x[:, m, j, i0:i0 + w] for x in wgu_s[k]],
                                               [h[:, j, blk * S:(blk + 1) * S] for h in hT], j == 0, j == DC - 1)
                            last.then_inc((pe_g, pe_u)[m], 1)
                    if blk == 1:
                        pe.wait_ge(pool_lo, JOBS * (2 * g + k) + 3)
                    pe.wait_ge(dve_h, NI * n)
                    down(s, n)
            pe.wait_ge(dve_h, NI * STEPS * TURNS)
            down(0, STEPS * TURNS)

        @block.scalar
        def _(act):
            act.wait_ge(pool_0, 6)
            with act.Fori(0, TURNS) as g:
                for s in range(STEPS):
                    n = STEPS * g + s
                    for c, (_, w) in enumerate(IT):
                        act.wait_ge(pe_g, NI * n + c + 1)
                        act.wait_ge(dve_p, NI * n + c)
                        nc.scalar.activation(silu[0:w, :], ps_g[c % 2][0:w, :], ACT.Silu).then_inc(act_s, 1)
                        act.wait_ge(dve_p, NI * n + c + 1)
                        nc.scalar.copy(hh[s % 2][0][0:w, c, :], prod[0:w, :]).then_inc(act_h, 1)

        @block.vector
        def _(dve):
            def add_down(s, n):
                k, blk = (s - 1) % STEPS // NBLK, (s - 1) % NBLK
                for i in range(ST):
                    t = blk * ST + i
                    dve.wait_ge(pe_d, ST * n + i + 1)
                    hs = HS[:, t * D:(t + 1) * D]
                    nc.vector.scalar_tensor_tensor(out=hs, in0=ps_d[i][:], scalar=cwe[:, k, t:t + 1], in1=hs,
                                                   op0=ALU.mult, op1=ALU.add).then_inc(dve_acc, 1)

            dve.wait_ge(pool_0, 6)
            with dve.Fori(0, TURNS) as g:
                for s in range(STEPS):
                    k, blk = s // NBLK, s % NBLK
                    n = STEPS * g + s
                    if blk == 1:
                        nc.vector.tensor_copy(cwe[:, k, :].unsqueeze(2), cw[:, :, bass.ds(2 * g + k, 1)]).then_inc(dve_cw, 1)
                    for c, (_, w) in enumerate(IT):
                        dve.wait_ge(act_s, NI * n + c + 1)
                        dve.wait_ge(pe_u, NI * n + c + 1)
                        dve.wait_ge(dve_h, NI * n + c)
                        nc.vector.tensor_tensor(prod[0:w, :], ps_u[c % 2][0:w, :], silu[0:w, :], ALU.mult).then_inc(dve_p, 1)
                        dve.wait_ge(act_h, NI * n + c + 1)
                        nc.vector.tensor_tensor(hh[s % 2][1][0:w, c, :], prod[0:w, :],
                                                hh[s % 2][0][0:w, c, :].bitcast(F32), ALU.subtract).then_inc(dve_h, 1)
                    dve.wait_ge(dve_acc, ST * n)
                    if blk == 1:
                        dve.wait_ge(dve_cw, 2 * g + k + 1)
                    add_down(s, n)
            dve.wait_ge(dve_acc, ST * STEPS * TURNS)
            add_down(0, STEPS * TURNS)


def program(nc, x, ctxT, wqkT, bqk, ln1, ln2, wqk, wv, wo, gateT, wgu, wdn, out):
    with ExitStack() as ctx:
        sb = lambda name, shape, dt=F32: ctx.enter_context(nc.sbuf_tensor(name, shape, dt))
        sem = lambda name: ctx.enter_context(nc.semaphore(name))
        spill = nc.dram_tensor("x1_spill", [NB, P, ST, D], F32, kind="Internal").ap()
        ident = sb("ident", [P, P])
        ident16 = sb("ident16", [P, P], BF16)
        causal = sb("causal", [P, P], BF16)
        neg_half = sb("neg_half", [P, ST])
        eps = sb("eps", [P, 2, ST])
        HS = sb("HS", [P, TT * D])
        hT = [sb(f"hT_{s}", [P, DC, T], F32R) for s in ("hi", "lo")]
        ps = [ctx.enter_context(nc.psum_tensor(f"ps{k}", [P, 512], F32)) for k in range(8)]
        constants(nc, sem, ident, ident16, causal, neg_half, eps)
        cross_attention(nc, sem, ps, ident, neg_half, eps, HS, hT, x, ctxT, wqkT, bqk, ln1, spill)
        self_attention(nc, sem, ps, ident, ident16, causal, HS, hT, wqk, wv, wo)
        cw = sb("cw", [P, TT, NE])
        route(nc, sem, ps, ident, neg_half, eps, HS, hT, cw, ln2, gateT, spill)
        experts(nc, sem, ps, HS, hT, cw, wgu, wdn, out)


def kernel(**inputs):
    import numpy as np
    import concourse.bacc as bacc
    from concourse.bass_utils import run_bass_kernel_spmd

    a = {k: np.asarray(v) for k, v in inputs.items()}
    w = lambda name: a["L0_ffn_" + name]
    chunks = lambda m: m.reshape(-1, P, m.shape[-1]).transpose(1, 0, 2)
    experts_of = lambda e, s: np.concatenate([w(e), w(s).reshape(NSH, I, D)])
    down = np.concatenate([w("ed_w").transpose(0, 2, 1), w("sd_w").T.reshape(NSH, I, D)])
    down = np.concatenate([down, np.zeros((NE, len(IT) * P - I, D), np.float32)], axis=1)
    gu = np.stack([experts_of("eg_w", "sg_w"), experts_of("eu_w", "su_w")], axis=1).reshape(2 * NE, I, D)
    qk = np.stack([w("wq").reshape(DC, P, H, HD), w("wk").reshape(DC, P, H, HD)])
    arrays = {
        "x": a["x"].reshape(NB, ST, P, D).transpose(0, 2, 1, 3),
        "ctxT": a["ctx_1024"].transpose(0, 2, 1).reshape(NB, CC, P, S).transpose(0, 2, 1, 3),
        "wqkT": np.stack([chunks(a["L0_xattn_Wq"].T), chunks(a["L0_xattn_Wk"].T)], axis=1),
        "bqk": np.stack([a["L0_xattn_bq"], a["L0_xattn_bk"]], axis=1),
        "ln1": w("ln1_w"),
        "ln2": w("ln2_w"),
        "wqk": qk.transpose(3, 2, 0, 1, 4).reshape(H, P, 2 * DC * HD),
        "wv": w("wv").reshape(DC, P, HP, 2 * HD).transpose(2, 1, 0, 3).reshape(HP, P, DC * 2 * HD),
        "wo": w("wo").reshape(HP, 2, P, D).transpose(0, 2, 1, 3).reshape(HP, P, 2 * D),
        "gateT": chunks(w("gate_w").T),
        "wgu": gu.transpose(0, 2, 1).reshape(2 * NE, DC, P, I).transpose(0, 2, 1, 3).reshape(2 * NE, P, DC * I),
        "wdn": down.reshape(NE, len(IT), P, D).transpose(0, 2, 1, 3).reshape(NE, P, len(IT) * D),
    }
    nc = bacc.Bacc("TRN2", target_bir_lowering=False, num_devices=1)
    arrays = {"in_" + k: np.ascontiguousarray(v) for k, v in arrays.items()}
    args = [nc.dram_tensor(k, v.shape, mybir.dt.from_np(v.dtype), kind="ExternalInput").ap() for k, v in arrays.items()]
    out = nc.dram_tensor("out", (NB, S, D), F32, kind="ExternalOutput").ap()
    program(nc, *args, out.rearrange("b (t p) n -> b p t n", p=P))
    r = run_bass_kernel_spmd(nc, [arrays], core_ids=[0])
    return r.results[0]["out"]
```

```python
from contextlib import ExitStack

import concourse.bass as bass
from concourse import mybir

F32 = mybir.dt.float32
F32R = mybir.dt.float32r
BF16 = mybir.dt.bfloat16
I32 = mybir.dt.int32
U32 = mybir.dt.uint32
ALU = mybir.AluOpType
ACT = mybir.ActivationFunctionType
AX = mybir.AxisListType

P = 128
NB = 4
S = 512
D = 512
DC = D // P
C = 256
CC = C // P
ST = S // P
T = NB * S
TT = T // P
H = 16
HD = 128
HP = H // 2
E = 16
TOPK = 6
I = 352
NSH = 2
NE = E + NSH
IT = [(0, 128), (128, 128), (256, 96)]
BT = 256
NBLOCKS = (T * TOPK + E * (BT - 1)) // BT // 2 * 2 + 2
SLOTS = NBLOCKS * BT
NEXP = NBLOCKS + 4
LN_EPS = 1e-5
RMS_EPS = 1e-6
MASKED = -1e30
ONE = 1


def matmul3(nc, out, lhs, rhs, start, stop):
    nc.tensor.matmul(out, lhs[0], rhs[0], start=start, stop=False)
    nc.tensor.matmul(out, lhs[0], rhs[1], start=False, stop=False)
    return nc.tensor.matmul(out, lhs[1], rhs[0], start=False, stop=stop)


def counting(sem):
    counters = []

    def count(name):
        counters.append(sem(name))
        return counters[-1]

    return counters, count


def constants(nc, sem, ident, ident16, causal, neg_half, eps):
    made = sem("const_made")
    with nc.Block() as block:
        @block.gpsimd
        def _(pool):
            nc.gpsimd.memset(ident[:], 0.0).then_inc(made, 1)
            nc.gpsimd.memset(causal[:], 0.0).then_inc(made, 1)
            nc.gpsimd.memset(neg_half[:], -0.5).then_inc(made, 1)
            nc.gpsimd.memset(eps[:, 0, :], LN_EPS).then_inc(made, 1)
            nc.gpsimd.memset(eps[:, 1, :], RMS_EPS).then_inc(made, 1)
            pool.wait_ge(made, 5)
            nc.gpsimd.affine_select(out=ident[:], in_=ident[:], compare_op=ALU.not_equal, fill=1.0, base=0,
                                    pattern=[[-1, P]], channel_multiplier=1).then_inc(made, 1)
            nc.gpsimd.affine_select(out=causal[:], in_=causal[:], compare_op=ALU.is_ge, fill=MASKED, base=0,
                                    pattern=[[-1, P]], channel_multiplier=1).then_inc(made, 1)
            pool.wait_ge(made, 7)
            nc.gpsimd.tensor_copy(ident16[:], ident[:]).then_inc(made, 1)


def cross_attention(nc, sem, ps, ident, neg_half, eps, HS, hT, x, ctxT, wqkT, bqk, ln1, spill):
    NU = 2
    n_of = lambda g, u: NU * g + u
    with ExitStack() as ctx:
        sb = lambda name, shape, dt=F32: ctx.enter_context(nc.sbuf_tensor(name, shape, dt))
        counters, count = counting(sem)
        X = [sb(f"x_{u}", [P, ST, S]) for u in range(NU)]
        feat = [sb(f"feat_{u}", [P, CC, S]) for u in range(NU)]
        feat_s = [sb(f"feat_{s}", [P, CC, S], F32R) for s in ("hi", "lo")]
        w_raw = sb("wqk_raw", [P, 2, CC, P])
        w_s = [sb(f"wqk1_{s}", [P, 2, CC, P], F32R) for s in ("hi", "lo")]
        bias = sb("bqk", [P, 2])
        ln1b = sb("ln1b", [P, D])
        qkT = [sb(f"qkT1_{s}", [P, 2, S], F32R) for s in ("hi", "lo")]
        xT = [sb(f"xT_{s}", [P, ST, S], F32R) for s in ("hi", "lo")]
        aT = [sb(f"aT_{s}", [P, ST, S], F32R) for s in ("hi", "lo")]
        prob = sb("prob1", [P, ST, S])
        norm = sb("norm1", [P, ST, S])
        st6 = sb("st6", [P, ST, 6])
        mv = sb("mv", [P, 2, ST, 2])
        rstd = sb("rstd", [P, 2, ST])
        ms = sb("ms", [P, ST])
        carry = sb("carry1", [P, 1])
        rms = sb("rms", [P, ST])
        negmax = sb("negmax1", [P, ST])
        rsum = sb("rsum1", [P, ST])
        rinv = sb("rinv1", [P, ST])

        ld_w, ld_x, ld_f = sem("ld_w"), [sem(f"ld_x{u}") for u in range(NU)], [sem(f"ld_f{u}") for u in range(NU)]
        spilled = [sem(f"spilled{u}") for u in range(NU)]
        act_w, dve_w = sem("act_w1"), sem("dve_w1")
        act_f, dve_f = count("act_f"), count("dve_f")
        pe_qk, act_qk, dve_qk = count("pe_qk1"), count("act_qk1"), count("dve_qk1")
        dve_st, dve_mv, pool_r, dve_xn = count("dve_st"), count("dve_mv"), count("pool_r"), count("dve_xn")
        pe_t, act_t, dve_t = count("pe_t1"), count("act_t1"), count("dve_t1")
        pe_e, dve_max, act_exp = count("pe_e1"), count("dve_max1"), count("act_exp1")
        dve_ri, dve_nrm = count("dve_ri1"), count("dve_nrm")
        pe_m, dve_x1 = count("pe_m"), count("dve_x1")
        dve_hs, dve_h, pool_p = count("dve_hs"), count("dve_h1"), count("pool_p1")

        block = ctx.enter_context(nc.Block())

        @block.sync
        def _(sp):
            sp.dma_start(w_raw[:], wqkT).then_inc(ld_w, 16)
            sp.dma_start(bias[:], bqk).then_inc(ld_w, 16)
            sp.dma_start(ln1b[:], ln1.partition_broadcast(P)).then_inc(ld_w, 16)
            for u in range(NU):
                sp.dma_start(feat[u][:], ctxT[u]).then_inc(ld_f[u], 16)
                sp.dma_start(X[u][:], x[u]).then_inc(ld_x[u], 16)
            with sp.Fori(0, NB // NU) as g:
                for u in range(NU):
                    n = n_of(g, u)
                    sp.wait_ge(dve_x1, ONE + ST * n + ST)
                    sp.dma_start(spill[bass.ds(n, 1)].rearrange("a p t n -> p (a t) n"), X[u][:]).then_inc(spilled[u], 16)
                    nxt = NU + u
                    sp.wait_ge(dve_f, ONE + n + 1)
                    sp.dma_start(feat[u][:], ctxT[nxt]).then_inc(ld_f[u], 16)
                    sp.wait_ge(dve_hs, ONE + ST * n + ST)
                    sp.wait_ge(spilled[u], 16 * g + 16)
                    sp.dma_start(X[u][:], x[nxt]).then_inc(ld_x[u], 16)
            for u in range(NU):
                sp.wait_ge(ld_f[u], 48)
                sp.wait_ge(ld_x[u], 48)

        @block.gpsimd
        def _(pool):
            for counter in counters:
                nc.gpsimd.sem_inc(counter, ONE)
            with pool.Fori(0, NB // NU) as g:
                for u in range(NU):
                    n = n_of(g, u)
                    pool.wait_ge(dve_mv, ONE + 2 * ST * n + ST)
                    nc.gpsimd.tensor_tensor(rstd[:, 0, :], mv[:, 0, :, 1], eps[:, 0, :], ALU.add).then_inc(pool_p, 1)
                    pool.wait_ge(pool_p, ONE + 6 * n + 1)
                    nc.gpsimd.tensor_tensor(rstd[:, 0, :], rstd[:, 0, :], neg_half[:, 0:ST], ALU.pow).then_inc(pool_r, 1)
                    pool.wait_ge(dve_mv, ONE + 2 * ST * n + 2 * ST)
                    nc.gpsimd.tensor_tensor(rstd[:, 1, :], mv[:, 1, :, 1], eps[:, 0, :], ALU.add).then_inc(pool_p, 1)
                    pool.wait_ge(pool_p, ONE + 6 * n + 2)
                    nc.gpsimd.tensor_tensor(rstd[:, 1, :], rstd[:, 1, :], neg_half[:, 0:ST], ALU.pow).then_inc(pool_p, 1)
                    pool.wait_ge(pool_p, ONE + 6 * n + 3)
                    nc.gpsimd.tensor_tensor(ms[:], mv[:, 1, :, 1], rstd[:, 1, :], ALU.mult).then_inc(pool_p, 1)
                    pool.wait_ge(pool_p, ONE + 6 * n + 4)
                    nc.gpsimd.tensor_tensor(ms[:], ms[:], rstd[:, 1, :], ALU.mult).then_inc(pool_p, 1)
                    pool.wait_ge(pool_p, ONE + 6 * n + 5)
                    nc.gpsimd.tensor_tensor(rms[:], ms[:], eps[:, 1, :], ALU.add).then_inc(pool_p, 1)
                    pool.wait_ge(pool_p, ONE + 6 * n + 6)
                    nc.gpsimd.tensor_tensor(rms[:], rms[:], neg_half[:, 0:ST], ALU.pow).then_inc(pool_r, 1)

        @block.tensor
        def _(pe):
            def transposed(src, i):
                for j in range(ST):
                    last = nc.tensor.transpose(ps[4 + i % 2][:, j * P:(j + 1) * P], src[:, i, j * P:(j + 1) * P], ident[:])
                last.then_inc(pe_t, 1)

            pe.wait_ge(dve_w, 1)
            with pe.Fori(0, NB // NU) as g:
                for u in range(NU):
                    n = n_of(g, u)
                    tiles = 3 * ST * n
                    pe.wait_ge(dve_f, ONE + n + 1)
                    pe.wait_ge(dve_qk, ONE + 2 * n)
                    for m in range(2):
                        for c in range(CC):
                            last = matmul3(nc, ps[m][:], [w[:, m, c, :] for w in w_s], [f[:, c, :] for f in feat_s],
                                           c == 0, c == CC - 1)
                        last.then_inc(pe_qk, 1)
                    for i in range(ST):
                        pe.wait_ge(dve_xn, ONE + ST * n + i + 1)
                        pe.wait_ge(dve_t, ONE + tiles + max(i - 1, 0))
                        transposed(norm, i)
                    pe.wait_ge(dve_qk, ONE + 2 * n + 2)
                    for i in range(ST):
                        if i >= 2:
                            pe.wait_ge(act_exp, ONE + ST * n + i - 1)
                        matmul3(nc, ps[2 + i % 2][:], [q[:, 0, i * P:(i + 1) * P] for q in qkT],
                                [k[:, 1, :] for k in qkT], True, True).then_inc(pe_e, 1)
                    for i in range(ST):
                        pe.wait_ge(dve_nrm, ONE + ST * n + i + 1)
                        pe.wait_ge(dve_t, ONE + tiles + ST + i - 1)
                        transposed(prob, i)
                    pe.wait_ge(dve_t, ONE + tiles + 2 * ST)
                    pe.wait_ge(dve_x1, ONE + ST * n)
                    for i in range(ST):
                        if i >= 2:
                            pe.wait_ge(dve_x1, ONE + ST * n + i - 1)
                        for j in range(ST):
                            last = matmul3(nc, ps[6 + i % 2][:], [a[:, j, i * P:(i + 1) * P] for a in xT],
                                           [a[:, j, :] for a in aT], j == 0, j == ST - 1)
                        last.then_inc(pe_m, 1)
                    for i in range(ST):
                        pe.wait_ge(dve_h, ONE + ST * n + i + 1)
                        pe.wait_ge(dve_t, ONE + tiles + 2 * ST + i - 1)
                        transposed(norm, i)

        @block.scalar
        def _(act):
            act.wait_ge(ld_w, 48)
            nc.scalar.copy(w_s[0][:], w_raw[:]).then_inc(act_w, 1)
            with act.Fori(0, NB // NU) as g:
                for u in range(NU):
                    n = n_of(g, u)
                    tiles = 3 * ST * n
                    act.wait_ge(ld_f[u], 16 * g + 16)
                    act.wait_ge(pe_qk, ONE + 2 * n)
                    nc.scalar.copy(feat_s[0][:], feat[u][:]).then_inc(act_f, 1)
                    for m in range(2):
                        act.wait_ge(pe_qk, ONE + 2 * n + m + 1)
                        nc.scalar.activation(qkT[0][:, m, :], ps[m][:], ACT.Identity, bias=bias[:, m:m + 1]).then_inc(act_qk, 1)
                    for i in range(ST):
                        act.wait_ge(pe_t, ONE + tiles + i + 1)
                        nc.scalar.copy(xT[0][:, :, i * P:(i + 1) * P],
                                       ps[4 + i % 2][:].rearrange("p (j t) -> p j t", j=ST)).then_inc(act_t, 1)
                    for i in range(ST):
                        act.wait_ge(dve_max, ONE + ST * n + i + 1)
                        nc.scalar.activation(prob[:, i, :], ps[2 + i % 2][:], ACT.Exp, bias=negmax[:, i:i + 1],
                                             accum_out=rsum[:, i:i + 1]).then_inc(act_exp, 1)
                    for i in range(ST):
                        act.wait_ge(pe_t, ONE + tiles + ST + i + 1)
                        nc.scalar.copy(aT[0][:, :, i * P:(i + 1) * P],
                                       ps[4 + i % 2][:].rearrange("p (j t) -> p j t", j=ST)).then_inc(act_t, 1)
                    for i in range(ST):
                        act.wait_ge(pe_t, ONE + tiles + 2 * ST + i + 1)
                        nc.scalar.copy(hT[0][:, :, bass.ds((ST * n + i) * P, P)],
                                       ps[4 + i % 2][:].rearrange("p (j t) -> p j t", j=DC)).then_inc(act_t, 1)

        @block.vector
        def _(dve):
            def stats(src, which, n, row):
                for i in range(ST):
                    if which:
                        dve.wait_ge(dve_x1, ONE + ST * n + i + 1)
                    nc.vector.bn_stats(st6[:, i, :], src[:, i, :]).then_inc(dve_st, 1)
                dve.wait_ge(dve_st, ONE + row + ST)
                nc.vector.memset(carry[:], 0.0)
                for i in range(ST):
                    nc.vector.bn_aggr(mv[:, which, i, :], st6[:, i, :]).then_inc(dve_mv, 1)

            def low_of_tile(lo, hi, i, done):
                dve.wait_ge(act_t, ONE + done)
                nc.vector.tensor_tensor(lo, ps[4 + i % 2][:].rearrange("p (j t) -> p j t", j=ST),
                                        hi.bitcast(F32), ALU.subtract).then_inc(dve_t, 1)

            dve.wait_ge(ld_w, 48)
            dve.wait_ge(act_w, 1)
            nc.vector.tensor_tensor(w_s[1][:], w_raw[:], w_s[0][:].bitcast(F32), ALU.subtract).then_inc(dve_w, 1)
            with dve.Fori(0, NB // NU) as g:
                for u in range(NU):
                    n = n_of(g, u)
                    tiles = 3 * ST * n
                    dve.wait_ge(ld_x[u], 16 * g + 16)
                    stats(X[u], 0, n, 2 * ST * n)
                    dve.wait_ge(ld_f[u], 16 * g + 16)
                    dve.wait_ge(act_f, ONE + n + 1)
                    nc.vector.tensor_tensor(feat_s[1][:], feat[u][:], feat_s[0][:].bitcast(F32), ALU.subtract).then_inc(dve_f, 1)
                    dve.wait_ge(pool_r, ONE + 2 * n + 1)
                    dve.wait_ge(dve_mv, ONE + 2 * ST * n + ST)
                    for i in range(ST):
                        nc.vector.tensor_scalar(norm[:, i, :], X[u][:, i, :], mv[:, 0, i, 0:1], rstd[:, 0, i:i + 1],
                                                ALU.subtract, ALU.mult).then_inc(dve_xn, 1)
                    for m in range(2):
                        dve.wait_ge(act_qk, ONE + 2 * n + m + 1)
                        nc.vector.scalar_tensor_tensor(out=qkT[1][:, m, :], in0=ps[m][:], scalar=bias[:, m:m + 1],
                                                       in1=qkT[0][:, m, :].bitcast(F32), op0=ALU.add,
                                                       op1=ALU.subtract).then_inc(dve_qk, 1)
                    for i in range(ST):
                        w = slice(i * P, (i + 1) * P)
                        low_of_tile(xT[1][:, :, w], xT[0][:, :, w], i, tiles + i + 1)
                    for i in range(ST):
                        dve.wait_ge(pe_e, ONE + ST * n + i + 1)
                        nc.vector.tensor_reduce(negmax[:, i:i + 1], ps[2 + i % 2][:], AX.X, ALU.max,
                                                negate=True).then_inc(dve_max, 1)
                    for i in range(ST):
                        dve.wait_ge(act_exp, ONE + ST * n + i + 1)
                        nc.vector.reciprocal(rinv[:, i:i + 1], rsum[:, i:i + 1]).then_inc(dve_ri, 1)
                        dve.wait_ge(dve_ri, ONE + ST * n + i + 1)
                        nc.vector.tensor_scalar(prob[:, i, :], prob[:, i, :], rinv[:, i:i + 1], None,
                                                ALU.mult).then_inc(dve_nrm, 1)
                    for i in range(ST):
                        w = slice(i * P, (i + 1) * P)
                        low_of_tile(aT[1][:, :, w], aT[0][:, :, w], i, tiles + ST + i + 1)
                    for i in range(ST):
                        dve.wait_ge(pe_m, ONE + ST * n + i + 1)
                        nc.vector.tensor_tensor(X[u][:, i, :], ps[6 + i % 2][:], X[u][:, i, :], ALU.add).then_inc(dve_x1, 1)
                    stats(X[u], 1, n, 2 * ST * n + ST)
                    dve.wait_ge(pool_r, ONE + 2 * n + 2)
                    dve.wait_ge(dve_mv, ONE + 2 * ST * n + 2 * ST)
                    for i in range(ST):
                        row = bass.ds((ST * n + i) * D, D)
                        nc.vector.tensor_scalar(HS[:, row], X[u][:, i, :], mv[:, 1, i, 0:1], rstd[:, 1, i:i + 1],
                                                ALU.subtract, ALU.mult).then_inc(dve_hs, 1)
                        dve.wait_ge(dve_hs, ONE + ST * n + i + 1)
                        nc.vector.scalar_tensor_tensor(out=norm[:, i, :], in0=HS[:, row], scalar=rms[:, i:i + 1],
                                                       in1=ln1b[:], op0=ALU.mult, op1=ALU.mult).then_inc(dve_h, 1)
                    for i in range(ST):
                        w = bass.ds((ST * n + i) * P, P)
                        low_of_tile(hT[1][:, :, w], hT[0][:, :, w], i, tiles + 2 * ST + i + 1)


def self_attention(nc, sem, ps, ident, ident16, causal, HS, hT, wqk, wv, wo):
    STEPS = 2 * NB
    VG = TT // 2
    with ExitStack() as ctx:
        sb = lambda name, shape, dt=F32: ctx.enter_context(nc.sbuf_tensor(name, shape, dt))
        counters, count = counting(sem)
        raw = [sb(f"w_raw{r}", [P, 1024]) for r in range(2)]
        wqk_s = [[sb(f"wqk_{hh}{s}", [P, 2, DC, HD], F32R) for s in ("hi", "lo")] for hh in range(2)]
        wv_s = [sb(f"wv_{s}", [P, DC, 2 * HD], F32R) for s in ("hi", "lo")]
        wo_s = [sb(f"wo_{s}", [P, 2, D], F32R) for s in ("hi", "lo")]
        v_s = [sb(f"v_{s}", [P, TT, 2 * HD], F32R) for s in ("hi", "lo")]
        qkT = [sb(f"qkT_{s}", [P, 2, S], F32R) for s in ("hi", "lo")]
        prob = sb("prob", [P, ST, S])
        pT = [sb(f"pT_{s}", [P, ST, S], F32R) for s in ("hi", "lo")]
        oT = [sb(f"oT_{s}", [P, S], F32R) for s in ("hi", "lo")]
        negmax = sb("negmax", [P, 2, ST])
        rsum = sb("rsum", [P, 2, ST])
        rinv = sb("rinv", [P, 2, ST])
        zero = sb("zero", [P, 1])
        ps_t, ps_p, ps_w = ps[2:4], ps[4:6], ps[6:8]
        ps_s = [ps_p[1], ps_p[0], ps[1], ps[0]]
        TILES = list(reversed(range(ST)))
        ps_o = ps_t[0]
        SCALE = float(HD) ** -0.5
        width = [max(2, i + 1) * P for i in range(ST)]
        first = [0, P, 2 * P, 2 * P]

        ld_raw = [sem(f"ld_raw{r}") for r in range(2)]
        pool_hi, pool_lo, pool_0 = count("pool_hi"), count("pool_lo"), sem("pool_0")
        pe_qk, act_qk, dve_qk = count("pe_qk"), count("act_qk"), count("dve_qk")
        pe_v, act_v, dve_v = count("pe_v"), count("act_v"), count("dve_v")
        pe_s, dve_max, act_exp = count("pe_s"), count("dve_max"), count("act_exp")
        pe_t, act_t, dve_t = count("pe_t"), count("act_t"), count("dve_t")
        pe_o, act_o, dve_o = count("pe_o"), count("act_o"), count("dve_o")
        dve_ri, pe_w, dve_acc = count("dve_ri"), count("pe_w"), count("dve_acc")

        JOBS = 4
        block = ctx.enter_context(nc.Block())

        @block.sync
        def _(sp):
            with sp.Fori(0, HP) as g:
                for job in range(JOBS):
                    r = job % 2
                    src = [wqk[bass.ds(2 * g, 1)], wv[bass.ds(g, 1)], wqk[bass.ds(2 * g + 1, 1)], wo[bass.ds(g, 1)]][job]
                    if job >= 2:
                        sp.wait_ge(pool_lo, ONE + JOBS * g + job - 1)
                    else:
                        sp.wait_ge(pool_lo, ONE + JOBS * g)
                    sp.dma_start(raw[r][:], src.rearrange("a p n -> p (a n)")).then_inc(ld_raw[r], 16)

        @block.gpsimd
        def _(pool):
            for counter in counters:
                nc.gpsimd.sem_inc(counter, ONE)
            for buf in oT + wo_s:
                nc.gpsimd.memset(buf[:].bitcast(F32), 0.0).then_inc(pool_0, 1)
            for buf in pT:
                nc.gpsimd.memset(buf[:].bitcast(F32), 0.0).then_inc(pool_0, 1)
            nc.gpsimd.memset(rinv[:], 0.0).then_inc(pool_0, 1)
            nc.gpsimd.memset(zero[:], 0.0).then_inc(pool_0, 1)
            pool.wait_ge(pool_0, 8)
            with pool.Fori(0, HP) as g:
                for job in range(JOBS):
                    r = job % 2
                    dst = [[w[:].rearrange("p a c n -> p (a c n)") for w in wqk_s[0]],
                           [w[:].rearrange("p c n -> p (c n)") for w in wv_s],
                           [w[:].rearrange("p a c n -> p (a c n)") for w in wqk_s[1]],
                           [w[:].rearrange("p a n -> p (a n)") for w in wo_s]][job]
                    pool.wait_ge(ld_raw[r], 32 * g + 16 * (job // 2) + 16)
                    if job == 0:
                        pool.wait_ge(pe_qk, ONE + 2 * STEPS * g)
                    elif job == 1:
                        pool.wait_ge(pe_v, ONE + VG * g)
                    elif job == 3:
                        pool.wait_ge(pe_w, ONE + ST * (STEPS * g + 1))
                    nc.gpsimd.tensor_tensor(dst[0], raw[r][:], zero[:].to_broadcast([P, 1024]), ALU.add).then_inc(pool_hi, 1)
                    pool.wait_ge(pool_hi, ONE + JOBS * g + job + 1)
                    nc.gpsimd.tensor_tensor(dst[1], raw[r][:], dst[0].bitcast(F32), ALU.subtract).then_inc(pool_lo, 1)

        @block.tensor
        def _(pe):
            def project(hh, b, m, c):
                last = matmul3(nc, ps_p[m][:], [w[:, m, c, :] for w in wqk_s[hh]],
                               [h[:, c, b * S:(b + 1) * S] for h in hT], c == 0, c == DC - 1)
                if c == DC - 1:
                    last.then_inc(pe_qk, 1)

            def output(s, i, n):
                hh = (s - 1) % STEPS // NB
                pe.wait_ge(dve_acc, ONE + ST * n + max(i - 1, 0))
                matmul3(nc, ps_w[i % 2][:], [o[:, i * P:(i + 1) * P] for o in oT], [w[:, hh, :] for w in wo_s],
                        True, True).then_inc(pe_w, 1)

            pe.wait_ge(pool_0, 8)
            with pe.Fori(0, HP) as g:
                pe.wait_ge(pool_lo, ONE + JOBS * g + 1)
                for m in range(2):
                    for c in range(DC):
                        project(0, 0, m, c)
                pe.wait_ge(pool_lo, ONE + JOBS * g + 2)
                for v in range(VG):
                    if v < 2:
                        pe.wait_ge(dve_qk, ONE + 2 * STEPS * g + v + 1)
                    else:
                        pe.wait_ge(dve_v, ONE + VG * g + v - 1)
                    for k in range(2):
                        for c in range(DC):
                            last = matmul3(nc, ps_p[v % 2][:, k * 2 * HD:(k + 1) * 2 * HD],
                                           [h[:, c, (2 * v + k) * P:(2 * v + k + 1) * P] for h in hT],
                                           [w[:, c, :] for w in wv_s], c == 0, c == DC - 1)
                    last.then_inc(pe_v, 1)
                for s in range(STEPS):
                    hh, b = s // NB, s % NB
                    n = STEPS * g + s
                    nxt = ((s + 1) // NB, (s + 1) % NB)
                    pe.wait_ge(dve_qk, ONE + 2 * n + 2)
                    if s == 0:
                        pe.wait_ge(dve_v, ONE + VG * g + VG)
                    for i in TILES:
                        matmul3(nc, ps_s[i][:, 0:width[i]], [q[:, 0, i * P:(i + 1) * P] for q in qkT],
                                [k[:, 1, 0:width[i]] for k in qkT], True, False)
                        nc.tensor.matmul(ps_s[i][:, i * P:(i + 1) * P], ident16[:], causal[:],
                                         start=False, stop=True).then_inc(pe_s, 1)
                    pe.wait_ge(dve_o, ONE + n)
                    if s == 1:
                        pe.wait_ge(pool_lo, ONE + JOBS * g + 4)
                    for i in range(ST):
                        output(s, i, n)
                    if s + 1 < STEPS:
                        if s + 1 == NB:
                            pe.wait_ge(pool_lo, ONE + JOBS * g + 3)
                        pe.wait_ge(act_exp, ONE + ST * n + ST)
                        for c in range(DC):
                            project(*nxt, 0, c)
                    for k, i in enumerate(TILES):
                        pe.wait_ge(act_exp, ONE + ST * n + k + 1)
                        if k >= 2:
                            pe.wait_ge(dve_t, ONE + ST * n + k - 1)
                        for j in range(i + 1):
                            last = nc.tensor.transpose(ps_t[k % 2][:, j * P:(j + 1) * P], prob[:, i, j * P:(j + 1) * P], ident[:])
                        last.then_inc(pe_t, 1)
                        if s + 1 < STEPS:
                            for c in [(), (0, 1), (2,), (3,)][k]:
                                project(*nxt, 1, c)
                    pe.wait_ge(dve_t, ONE + ST * n + ST)
                    for j in range(ST):
                        last = matmul3(nc, ps_o[:, first[j]:S],
                                       [v[:, b * ST + j, hh * HD:(hh + 1) * HD] for v in v_s],
                                       [p[:, j, first[j]:S] for p in pT], j == 0, j == ST - 1)
                    last.then_inc(pe_o, 1)
            pe.wait_ge(dve_o, ONE + STEPS * HP)
            for i in range(ST):
                output(0, i, STEPS * HP)

        @block.scalar
        def _(act):
            def high_qk(m, done):
                act.wait_ge(pe_qk, ONE + done)
                nc.scalar.mul(qkT[0][:, m, :], ps_p[m][:], SCALE if m == 0 else 1.0).then_inc(act_qk, 1)

            act.wait_ge(pool_0, 8)
            with act.Fori(0, HP) as g:
                high_qk(0, 2 * STEPS * g + 1)
                high_qk(1, 2 * STEPS * g + 2)
                for v in range(VG):
                    act.wait_ge(pe_v, ONE + VG * g + v + 1)
                    nc.scalar.copy(v_s[0][:, 2 * v:2 * v + 2, :],
                                   ps_p[v % 2][:].rearrange("p (k n) -> p k n", k=2)).then_inc(act_v, 1)
                for s in range(STEPS):
                    n = STEPS * g + s
                    for k, i in enumerate(TILES):
                        act.wait_ge(dve_max, ONE + ST * n + k + 1)
                        nc.scalar.activation(prob[:, i, 0:(i + 1) * P], ps_s[i][:, 0:(i + 1) * P], ACT.Exp,
                                             bias=negmax[:, s % 2, i:i + 1],
                                             accum_out=rsum[:, s % 2, i:i + 1]).then_inc(act_exp, 1)
                    if s + 1 < STEPS:
                        high_qk(0, 2 * n + 3)
                    for k, i in enumerate(TILES):
                        act.wait_ge(pe_t, ONE + ST * n + k + 1)
                        nc.scalar.copy(pT[0][:, 0:i + 1, i * P:(i + 1) * P],
                                       ps_t[k % 2][:, 0:(i + 1) * P].rearrange("p (j t) -> p j t", t=P)).then_inc(act_t, 1)
                    if s + 1 < STEPS:
                        high_qk(1, 2 * n + 4)
                    act.wait_ge(pe_o, ONE + n + 1)
                    nc.scalar.copy(oT[0][:], ps_o[:]).then_inc(act_o, 1)

        @block.vector
        def _(dve):
            def low_qk(m, done):
                dve.wait_ge(act_qk, ONE + done)
                nc.vector.scalar_tensor_tensor(out=qkT[1][:, m, :], in0=ps_p[m][:], scalar=SCALE if m == 0 else 1.0,
                                               in1=qkT[0][:, m, :].bitcast(F32), op0=ALU.mult,
                                               op1=ALU.subtract).then_inc(dve_qk, 1)

            def add_output(s, n):
                dve.wait_ge(dve_ri, ONE + n)
                dve.wait_ge(dve_acc, ONE + ST * n)
                for i in range(ST):
                    tile = (s - 1) % NB * ST + i
                    dve.wait_ge(pe_w, ONE + ST * n + i + 1)
                    hs = HS[:, tile * D:(tile + 1) * D]
                    nc.vector.scalar_tensor_tensor(out=hs, in0=ps_w[i % 2][:], scalar=rinv[:, (s - 1) % 2, i:i + 1],
                                                   in1=hs, op0=ALU.mult, op1=ALU.add).then_inc(dve_acc, 1)

            dve.wait_ge(pool_0, 8)
            with dve.Fori(0, HP) as g:
                low_qk(0, 2 * STEPS * g + 1)
                low_qk(1, 2 * STEPS * g + 2)
                for v in range(VG):
                    dve.wait_ge(act_v, ONE + VG * g + v + 1)
                    nc.vector.tensor_tensor(v_s[1][:, 2 * v:2 * v + 2, :], ps_p[v % 2][:].rearrange("p (k n) -> p k n", k=2),
                                            v_s[0][:, 2 * v:2 * v + 2, :].bitcast(F32), ALU.subtract).then_inc(dve_v, 1)
                for s in range(STEPS):
                    n = STEPS * g + s
                    for k, i in enumerate(TILES):
                        dve.wait_ge(pe_s, ONE + ST * n + k + 1)
                        nc.vector.tensor_reduce(negmax[:, s % 2, i:i + 1], ps_s[i][:, 0:(i + 1) * P], AX.X,
                                                ALU.max, negate=True).then_inc(dve_max, 1)
                    add_output(s, n)
                    if s + 1 < STEPS:
                        low_qk(0, 2 * n + 3)
                    dve.wait_ge(act_exp, ONE + ST * n + ST)
                    nc.vector.reciprocal(rinv[:, s % 2, :], rsum[:, s % 2, :]).then_inc(dve_ri, 1)
                    for k, i in enumerate(TILES):
                        dve.wait_ge(act_t, ONE + ST * n + k + 1)
                        w = slice(i * P, (i + 1) * P)
                        nc.vector.tensor_tensor(pT[1][:, 0:i + 1, w], ps_t[k % 2][:, 0:(i + 1) * P].rearrange("p (j t) -> p j t", t=P),
                                                pT[0][:, 0:i + 1, w].bitcast(F32), ALU.subtract).then_inc(dve_t, 1)
                    if s + 1 < STEPS:
                        low_qk(1, 2 * n + 4)
                    dve.wait_ge(act_o, ONE + n + 1)
                    nc.vector.tensor_tensor(oT[1][:], ps_o[:], oT[0][:].bitcast(F32), ALU.subtract).then_inc(dve_o, 1)
            add_output(0, STEPS * HP)


def normed_again(nc, sem, ps, ident, neg_half, eps, HS, hT, logits, rows, pad_rows, ln2, gateT, spill):
    NG = TT // ST
    with ExitStack() as ctx:
        sb = lambda name, shape, dt=F32: ctx.enter_context(nc.sbuf_tensor(name, shape, dt))
        counters, count = counting(sem)
        x1 = [sb(f"x1_{u}", [P, ST, D]) for u in range(2)]
        ln2b = sb("ln2b", [P, D])
        gate = sb("gate", [P, DC, P])
        gate_s = [sb(f"gate_{s}", [P, DC, P], F32R) for s in ("hi", "lo")]
        norm = [sb(f"norm3_{u}", [P, ST, D]) for u in range(2)]
        st6 = sb("st6_3", [P, ST, 6])
        mv = sb("mv3", [P, ST, 2])
        ms = sb("ms3", [P, 2, ST])
        rms = sb("rms3", [P, ST])
        carry = sb("carry3", [P, 1])
        logT = sb("logT", [P, S])

        ld_g, ld_x1 = sem("ld_g"), [sem(f"ld_x1{u}") for u in range(2)]
        stored, padded = [sem(f"rows_stored{u}") for u in range(2)], sem("rows_padded")
        pool_z, act_g, dve_g = sem("pool_z"), sem("act_g"), sem("dve_g")
        dve_st, dve_mv, pool_p, pool_r = count("dve_st3"), count("dve_mv3"), count("pool_p3"), count("pool_r3")
        dve_h, pe_t, act_t, dve_t = count("dve_h3"), count("pe_t3"), count("act_t3"), count("dve_t3")
        pool_a = count("pool_a")
        pe_l, act_l, pe_lt, act_lt = count("pe_l"), count("act_l"), count("pe_lt"), count("act_lt")

        block = ctx.enter_context(nc.Block())

        @block.sync
        def _(sp):
            sp.dma_start(ln2b[:], ln2.partition_broadcast(P)).then_inc(ld_g, 16)
            sp.wait_ge(pool_z, 2)
            sp.dma_start(gate[:, :, 0:E], gateT).then_inc(ld_g, 16)
            for pad in pad_rows:
                sp.dma_start(pad, norm[0][:, 0, :]).then_inc(padded, 16)
            with sp.Fori(0, NG // 2) as g2:
                for u in range(2):
                    g = 2 * g2 + u
                    sp.wait_ge(pool_a, ONE + 2 * ST * g2)
                    sp.dma_start(x1[u][:], spill[bass.ds(g, 1)].rearrange("a p t n -> p (a t) n")).then_inc(ld_x1[u], 16)
                    sp.wait_ge(dve_h, ONE + ST * g + ST)
                    sp.dma_start(rows[bass.ds(g, 1)].rearrange("a p t n -> p (a t) n"), norm[u][:]).then_inc(stored[u], 16)
            for u in range(2):
                sp.wait_ge(stored[u], 16 * (NG // 2))
            sp.wait_ge(padded, 16 * len(pad_rows))

        @block.gpsimd
        def _(pool):
            for counter in counters:
                nc.gpsimd.sem_inc(counter, ONE)
            nc.gpsimd.memset(gate[:], 0.0).then_inc(pool_z, 1)
            nc.gpsimd.memset(norm[0][:, 0, :], 0.0).then_inc(pool_z, 1)
            with pool.Fori(0, NG // 2) as g2:
                for u in range(2):
                    g = 2 * g2 + u
                    pool.wait_ge(dve_mv, ONE + ST * g + ST)
                    nc.gpsimd.tensor_tensor(ms[:, 0, :], mv[:, :, 0], mv[:, :, 0], ALU.mult).then_inc(pool_p, 1)
                    pool.wait_ge(pool_p, ONE + 3 * g + 1)
                    nc.gpsimd.tensor_tensor(ms[:, 0, :], ms[:, 0, :], mv[:, :, 1], ALU.add).then_inc(pool_p, 1)
                    pool.wait_ge(pool_p, ONE + 3 * g + 2)
                    nc.gpsimd.tensor_tensor(ms[:, 1, :], ms[:, 0, :], eps[:, 1, :], ALU.add).then_inc(pool_p, 1)
                    pool.wait_ge(pool_p, ONE + 3 * g + 3)
                    nc.gpsimd.tensor_tensor(rms[:], ms[:, 1, :], neg_half[:, 0:ST], ALU.pow).then_inc(pool_r, 1)
                    pool.wait_ge(ld_x1[u], 16 * g2 + 16)
                    for i in range(ST):
                        row = bass.ds((ST * g + i) * D, D)
                        pool.wait_ge(dve_h, ONE + ST * g + i + 1)
                        nc.gpsimd.tensor_tensor(HS[:, row], HS[:, row], x1[u][:, i, :], ALU.add).then_inc(pool_a, 1)

        @block.tensor
        def _(pe):
            pe.wait_ge(dve_g, 1)
            with pe.Fori(0, NG // 2) as g2:
                for u in range(2):
                    g = 2 * g2 + u
                    for i in range(ST):
                        pe.wait_ge(dve_h, ONE + ST * g + i + 1)
                        pe.wait_ge(dve_t, ONE + ST * g + max(i - 1, 0))
                        for j in range(DC):
                            last = nc.tensor.transpose(ps[i % 2][:, j * P:(j + 1) * P], norm[u][:, i, j * P:(j + 1) * P], ident[:])
                        last.then_inc(pe_t, 1)
                    pe.wait_ge(dve_t, ONE + ST * g + ST)
                    pe.wait_ge(act_l, ONE + g)
                    for c in range(DC):
                        last = matmul3(nc, ps[2][:], [w[:, c, :] for w in gate_s],
                                       [h[:, c, bass.ds(g * S, S)] for h in hT], c == 0, c == DC - 1)
                    last.then_inc(pe_l, 1)
                    pe.wait_ge(act_l, ONE + g + 1)
                    pe.wait_ge(act_lt, ONE + g)
                    for i in range(ST):
                        last = nc.tensor.transpose(ps[3][:, i * P:(i + 1) * P], logT[:, i * P:(i + 1) * P], ident[:])
                    last.then_inc(pe_lt, 1)

        @block.scalar
        def _(act):
            act.wait_ge(ld_g, 32)
            nc.scalar.copy(gate_s[0][:], gate[:]).then_inc(act_g, 1)
            with act.Fori(0, NG) as g:
                for i in range(ST):
                    act.wait_ge(pe_t, ONE + ST * g + i + 1)
                    nc.scalar.copy(hT[0][:, :, bass.ds((ST * g + i) * P, P)],
                                   ps[i % 2][:].rearrange("p (j t) -> p j t", j=DC)).then_inc(act_t, 1)
                act.wait_ge(pe_l, ONE + g + 1)
                act.wait_ge(pe_lt, ONE + g)
                nc.scalar.copy(logT[:], ps[2][:]).then_inc(act_l, 1)
                act.wait_ge(pe_lt, ONE + g + 1)
                nc.scalar.copy(logits[:, bass.ds(g * ST, ST), :],
                               ps[3][:].rearrange("p (t e) -> p t e", e=P)[:, :, 0:E]).then_inc(act_lt, 1)

        @block.vector
        def _(dve):
            dve.wait_ge(ld_g, 32)
            dve.wait_ge(act_g, 1)
            nc.vector.tensor_tensor(gate_s[1][:], gate[:], gate_s[0][:].bitcast(F32), ALU.subtract).then_inc(dve_g, 1)
            dve.wait_ge(padded, 16 * len(pad_rows))
            with dve.Fori(0, NG // 2) as g2:
                for u in range(2):
                    g = 2 * g2 + u
                    for i in range(ST):
                        nc.vector.bn_stats(st6[:, i, :], HS[:, bass.ds((ST * g + i) * D, D)]).then_inc(dve_st, 1)
                    dve.wait_ge(dve_st, ONE + ST * g + ST)
                    nc.vector.memset(carry[:], 0.0)
                    for i in range(ST):
                        nc.vector.bn_aggr(mv[:, i, :], st6[:, i, :]).then_inc(dve_mv, 1)
                    dve.wait_ge(pool_r, ONE + g + 1)
                    dve.wait_ge(stored[u], 16 * g2)
                    for i in range(ST):
                        nc.vector.scalar_tensor_tensor(out=norm[u][:, i, :], in0=HS[:, bass.ds((ST * g + i) * D, D)],
                                                       scalar=rms[:, i:i + 1], in1=ln2b[:], op0=ALU.mult,
                                                       op1=ALU.mult).then_inc(dve_h, 1)
                    for i in range(ST):
                        w = bass.ds((ST * g + i) * P, P)
                        dve.wait_ge(act_t, ONE + ST * g + i + 1)
                        nc.vector.tensor_tensor(hT[1][:, :, w], ps[i % 2][:].rearrange("p (j t) -> p j t", j=DC),
                                                hT[0][:, :, w].bitcast(F32), ALU.subtract).then_inc(dve_t, 1)


def shared_expert(nc, sem, ps, ident, HS, hT, logits, token_of, weight_of, expert_of, wgu, wdn, table, out, pad_out):
    NBLK = T // S
    STEPS = NSH * NBLK
    JOBS = 3
    NI = len(IT)
    with ExitStack() as ctx:
        sb = lambda name, shape, dt=F32: ctx.enter_context(nc.sbuf_tensor(name, shape, dt))
        raw = sb("wx_raw", [P, NI * D])
        wgu_s = [[sb(f"wgu_{k}{s}", [P, 2, DC, I], F32R) for s in ("hi", "lo")] for k in range(NSH)]
        wdn_s = [sb(f"wdn_{s}", [P, NI, D], F32R) for s in ("hi", "lo")]
        hh = [[sb(f"hh_{k}{s}", [P, NI, S], F32R) for s in ("hi", "lo")] for k in range(2)]
        silu = sb("silu", [P, S])
        prod = sb("prod", [P, S])
        ex = sb("ex", [P, TT, E])
        sel = sb("sel", [P, TT, E])
        acc = [sb(f"acc{k}", [P, TT, E]) for k in range(2)]
        pos = sb("pos", [P, TT, E])
        tmp = sb("tmp", [P, TT, E])
        sel16 = sb("sel16", [P, TT, E], BF16)
        before = sb("before", [P, P], BF16)
        ones = sb("ones", [P, P], BF16)
        top = sb("top", [P, TT, 8])
        mx = sb("mx", [P, TT])
        cnt = sb("cnt", [P, TT])
        blocks = sb("blocks", [P, 3, E])
        blocks_i = sb("blocks_i", [P, E], I32)
        pair = sb("pair", [P, TT, TOPK, 2])
        slot = sb("slot", [P, TT, TOPK])
        slot_i = sb("slot_i", [P, TT * TOPK], U32)
        token = sb("token", [P, TT])
        fresh = sb("fresh", [P, SLOTS // P, 2])
        fresh_i = sb("fresh_i", [P, SLOTS // P], I32)
        number = sb("number", [1, NEXP])
        bounds = sb("bounds", [1, NEXP, E])
        wide = lambda a: a.unsqueeze(2).to_broadcast([P, TT, E])
        ps_g, ps_u, ps_d, ps_r, ps_c = ps[0:2], ps[2:4], ps[4:6], ps[6], ps[7]

        ld_w, pool_hi, pool_lo, pool_0 = sem("ld_w4"), sem("pool_hi4"), sem("pool_lo4"), sem("pool_04")
        pe_g, pe_u, act_s, dve_p, act_h, dve_h = (sem(k) for k in ("pe_g", "pe_u", "act_s", "dve_p", "act_h4", "dve_h4"))
        pe_d, dve_acc, stored = sem("pe_d"), sem("dve_acc4"), sem("stored")
        dve_r, dve_c, act_e, pe_r = sem("dve_r"), sem("dve_c"), sem("act_e"), sem("pe_r")
        pool_f, ld_f, scattered, ld_t, pe_tt, dve_tt = (sem(k) for k in ("pool_f", "ld_f4", "scattered", "ld_t", "pe_tt", "dve_tt"))
        act_dn, dve_dn = sem("act_dn"), sem("dve_dn")
        LOGITS, PICKED, PACKED = 1, 2, 3
        block = ctx.enter_context(nc.Block())

        @block.sync
        def _(sp):
            for k in range(NSH):
                for job in range(JOBS):
                    sp.wait_ge(pool_lo, JOBS * k + job)
                    if job < 2:
                        sp.dma_start(raw[:, 0:DC * I], wgu[k][:, job * DC * I:(job + 1) * DC * I]).then_inc(ld_w, 16)
                    else:
                        sp.dma_start(raw[:], wdn[k]).then_inc(ld_w, 16)
                    if k + job == 0:
                        sp.wait_ge(pool_f, 3)
                        sp.dma_start(table.rearrange("(p j) w -> p j w", p=P), fresh[:]).then_inc(ld_f, 16)
            sp.wait_ge(scattered, 16 * TT * TOPK)
            sp.dma_start(fresh[:], table.rearrange("(j p) w -> j p w", p=P)).then_inc(ld_t, 16)
            for b in range(NB):
                sp.wait_ge(dve_acc, ST * (STEPS - NB + b + 1))
                sp.dma_start(out[b], HS[:, b * ST * D:(b + 1) * ST * D].rearrange("p (t n) -> p t n", n=D)).then_inc(stored, 16)
            sp.wait_ge(dve_acc, ST * STEPS + 1)
            for pad in pad_out:
                sp.dma_start(pad, silu[:]).then_inc(stored, 16)
            sp.wait_ge(stored, 16 * (NB + len(pad_out)))

        @block.gpsimd
        def _(pool):
            nc.gpsimd.memset(fresh[:], 0.0).then_inc(pool_0, 1)
            nc.gpsimd.memset(ones[:], 1.0).then_inc(pool_0, 1)
            nc.gpsimd.memset(expert_of[:], 0).then_inc(pool_0, 1)
            nc.gpsimd.iota(fresh_i[:], pattern=[[1, SLOTS // P]], base=0, channel_multiplier=SLOTS // P).then_inc(pool_0, 1)
            nc.gpsimd.iota(number[:], pattern=[[1, NEXP]], base=0, channel_multiplier=0,
                           allow_small_or_imprecise_dtypes=True).then_inc(pool_0, 1)
            nc.gpsimd.iota(token[:], pattern=[[P, TT]], base=0, channel_multiplier=1,
                           allow_small_or_imprecise_dtypes=True).then_inc(pool_0, 1)
            for at in (0, 4 + SLOTS // P):
                nc.gpsimd.iota(token_of[:, at:at + 4].bitcast(I32).rearrange("p (a b) -> p a b", a=2),
                               pattern=[[0, 2], [P, 2]], base=T, channel_multiplier=1).then_inc(pool_0, 1)
            pool.wait_ge(pool_0, 8)
            nc.gpsimd.affine_select(out=before[:], in_=ones[:], compare_op=ALU.is_gt, fill=0.0, base=0,
                                    pattern=[[1, P]], channel_multiplier=-1).then_inc(pool_0, 1)
            for k in range(NSH):
                for job in range(JOBS if k == 0 else 2):
                    n = DC * I if job < 2 else NI * D
                    pool.wait_ge(ld_w, 16 * (JOBS * k + job + 1))
                    if job < 2:
                        dst = [w[:, job].rearrange("p c n -> p (c n)") for w in wgu_s[k]]
                    else:
                        dst = [w[:].rearrange("p c n -> p (c n)") for w in wdn_s]
                    nc.gpsimd.tensor_copy(dst[0], raw[:, 0:n]).then_inc(pool_hi, 1)
                    pool.wait_ge(pool_hi, JOBS * k + job + 1)
                    nc.gpsimd.tensor_tensor(dst[1], raw[:, 0:n], dst[0].bitcast(F32), ALU.subtract).then_inc(pool_lo, 1)
            pool.wait_ge(dve_r, PACKED)
            pool.wait_ge(ld_f, 16)
            for t in range(TT):
                for r in range(TOPK):
                    i = t * TOPK + r
                    nc.gpsimd.indirect_dma_start(table, bass.IndirectOffsetOnAxis(ap=slot_i[:, i:i + 1], axis=0),
                                                 pair[:, t, r, :], None, bounds_check=SLOTS - 1,
                                                 oob_is_err=False).then_inc(scattered, 16)

        @block.tensor
        def _(pe):
            def down(n):
                if n == 0:
                    pe.wait_ge(pool_lo, JOBS)
                elif n == NBLK:
                    pe.wait_ge(dve_dn, 1)
                pe.wait_ge(dve_h, NI * (n + 1))
                for i in range(ST):
                    if ST * n + i >= 2:
                        pe.wait_ge(dve_acc, ST * n + i - 1)
                    for c, (_, w) in enumerate(IT):
                        last = matmul3(nc, ps_d[i % 2][:], [h[0:w, c, i * P:(i + 1) * P] for h in hh[n % 2]],
                                       [x[0:w, c, :] for x in wdn_s], c == 0, c == NI - 1)
                    last.then_inc(pe_d, 1)

            for n in range(STEPS):
                k, blk = n // NBLK, n % NBLK
                if blk == 0:
                    pe.wait_ge(pool_lo, JOBS * k + 2)
                for c, (i0, w) in enumerate(IT):
                    q = NI * n + c
                    if q >= 2:
                        pe.wait_ge(dve_p, q - 1)
                    for m, bank in enumerate((ps_g[q % 2], ps_u[q % 2])):
                        for j in range(DC):
                            last = matmul3(nc, bank[0:w, :], [x[:, m, j, i0:i0 + w] for x in wgu_s[k]],
                                           [h[:, j, blk * S:(blk + 1) * S] for h in hT], j == 0, j == DC - 1)
                        last.then_inc((pe_g, pe_u)[m], 1)
                if n >= 1:
                    down(n - 1)
                if n == 2:
                    pe.wait_ge(dve_r, PICKED)
                    pe.wait_ge(pool_0, 9)
                    chosen = sel16[:].rearrange("p t e -> p (t e)")
                    nc.tensor.matmul(ps_r[:, 0:TT * E], before[:], chosen, start=True, stop=True)
                    nc.tensor.matmul(ps_c[:, 0:TT * E], ones[:], chosen, start=True, stop=True).then_inc(pe_r, 1)
            down(STEPS - 1)
            pe.wait_ge(ld_t, 16)
            nc.tensor.transpose(ps_r[:, 0:P], fresh[:, :, 0], ident[:])
            nc.tensor.transpose(ps_c[:, 0:P], fresh[:, :, 1], ident[:]).then_inc(pe_tt, 1)

        @block.scalar
        def _(act):
            act.wait_ge(dve_r, LOGITS)
            nc.scalar.activation(ex[:], tmp[:], ACT.Exp).then_inc(act_e, 1)
            for n in range(STEPS):
                if n == NBLK + 1:
                    act.wait_ge(ld_w, 16 * NSH * JOBS)
                    act.wait_ge(pe_d, ST * NBLK)
                    nc.scalar.copy(wdn_s[0][:], raw[:].rearrange("p (c n) -> p c n", c=NI)).then_inc(act_dn, 1)
                for c, (_, w) in enumerate(IT):
                    q = NI * n + c
                    act.wait_ge(pe_g, q + 1)
                    if q:
                        act.wait_ge(dve_p, q)
                    nc.scalar.activation(silu[0:w, :], ps_g[q % 2][0:w, :], ACT.Silu).then_inc(act_s, 1)
                    act.wait_ge(dve_p, q + 1)
                    nc.scalar.copy(hh[n % 2][0][0:w, c, :], prod[0:w, :]).then_inc(act_h, 1)

        @block.vector
        def _(dve):
            done = [0]

            def step(ins):
                done[0] += 1
                ins.then_inc(dve_c, 1)
                dve.wait_ge(dve_c, done[0])

            def running(a, b, src, axis, size):
                at = lambda x, lo, hi: x[:, lo:hi, :] if axis == 1 else x[:, :, lo:hi]
                dist = 1
                while dist < size:
                    step(nc.vector.tensor_copy(at(a, 0, dist), at(src, 0, dist)))
                    step(nc.vector.tensor_tensor(at(a, dist, size), at(src, dist, size), at(src, 0, size - dist), ALU.add))
                    src, a, b = a, b, a
                    dist *= 2
                return src

            def logits_less_maximum():
                step(nc.vector.tensor_reduce(mx[:], logits[:], AX.X, ALU.max))
                nc.vector.tensor_tensor(tmp[:], logits[:], wide(mx[:]), ALU.subtract).then_inc(dve_r, 1)

            def pick():
                dve.wait_ge(act_e, 1)
                for t in range(TT):
                    last = nc.vector.max(top[:, t, :], ex[:, t, :])
                step(last)
                sixth = wide(top[:, :, TOPK - 1])
                step(nc.vector.tensor_tensor(sel[:], ex[:], sixth, ALU.is_gt))
                step(nc.vector.tensor_tensor(tmp[:], ex[:], sixth, ALU.is_equal))
                step(nc.vector.tensor_reduce(cnt[:], sel[:], AX.X, ALU.add))
                step(nc.vector.tensor_scalar(cnt[:], cnt[:], -1.0, float(TOPK), ALU.mult, ALU.add))
                equal = running(acc[0][:], acc[1][:], tmp[:], 2, E)
                step(nc.vector.tensor_tensor(pos[:], equal, wide(cnt[:]), ALU.is_le))
                step(nc.vector.tensor_tensor(tmp[:], tmp[:], pos[:], ALU.mult))
                step(nc.vector.tensor_tensor(sel[:], sel[:], tmp[:], ALU.add))
                nc.vector.tensor_copy(sel16[:], sel[:]).then_inc(dve_r, 1)
                step(nc.vector.tensor_tensor(ex[:], ex[:], sel[:], ALU.mult))
                step(nc.vector.tensor_reduce(mx[:], ex[:], AX.X, ALU.add))
                step(nc.vector.reciprocal(cnt[:], mx[:]))
                step(nc.vector.tensor_tensor(ex[:], ex[:], wide(cnt[:]), ALU.mult))

            def place():
                dve.wait_ge(pe_r, 1)
                counts = ps_c[:, 0:TT * E].rearrange("p (t e) -> p t e", e=E)
                step(nc.vector.tensor_copy(tmp[:], counts))
                total = running(acc[0][:], acc[1][:], tmp[:], 1, TT)
                step(nc.vector.tensor_scalar(blocks_i[:], total[:, TT - 1, :], float(BT - 1), None, ALU.add))
                step(nc.vector.tensor_scalar(blocks_i[:], blocks_i[:], BT.bit_length() - 1, None, ALU.arith_shift_right))
                step(nc.vector.tensor_copy(blocks[:, 0, :], blocks_i[:]))
                step(nc.vector.tensor_tensor(pos[:], total, tmp[:], ALU.subtract))
                step(nc.vector.tensor_tensor(pos[:], pos[:], ps_r[:, 0:TT * E].rearrange("p (t e) -> p t e", e=E), ALU.add))
                ends = running(blocks[:, 1:2, :], blocks[:, 2:3, :], blocks[:, 0:1, :], 2, E)
                step(nc.vector.tensor_tensor(bounds[:], ends[0:1].to_broadcast([1, NEXP, E]),
                                             number[:].unsqueeze(2).to_broadcast([1, NEXP, E]), ALU.is_le))
                step(nc.vector.tensor_reduce(number[:], bounds[:], AX.X, ALU.add))
                step(nc.vector.tensor_scalar(expert_of[:], number[:], float(E - 1), None, ALU.min))
                step(nc.vector.tensor_tensor(blocks[:, 0:1, :], ends, blocks[:, 0:1, :], ALU.subtract))
                step(nc.vector.tensor_scalar(blocks[:, 0, :], blocks[:, 0, :], float(BT), None, ALU.mult))
                step(nc.vector.tensor_tensor(pos[:], pos[:], blocks[:, 0:1, :].to_broadcast([P, TT, E]), ALU.add))
                running(acc[0][:], acc[1][:], sel[:], 2, E)

            def pack():
                nth = acc[1]
                for r in range(TOPK):
                    step(nc.vector.scalar_tensor_tensor(out=tmp[:].rearrange("p t e -> p (t e)"),
                                                        in0=nth[:].rearrange("p t e -> p (t e)"), scalar=float(r + 1),
                                                        in1=sel[:].rearrange("p t e -> p (t e)"), op0=ALU.is_equal, op1=ALU.mult))
                    step(nc.vector.tensor_tensor(acc[0][:], tmp[:], pos[:], ALU.mult))
                    step(nc.vector.tensor_tensor(tmp[:], tmp[:], ex[:], ALU.mult))
                    step(nc.vector.tensor_reduce(slot[:, :, r:r + 1], acc[0][:], AX.X, ALU.add))
                    step(nc.vector.tensor_reduce(pair[:, :, r, 1:2], tmp[:], AX.X, ALU.add))
                    step(nc.vector.tensor_copy(pair[:, :, r, 0:1], token[:].unsqueeze(2)))
                nc.vector.tensor_copy(slot_i[:], slot[:].rearrange("p t r -> p (t r)")).then_inc(dve_r, 1)

            dve.wait_ge(pool_0, 9)
            nc.vector.tensor_scalar(fresh_i[:], fresh_i[:], BT - 1, None, ALU.bitwise_and).then_inc(pool_f, 1)
            dve.wait_ge(pool_f, 1)
            nc.vector.tensor_scalar(fresh[:, :, 0], fresh_i[:], float(T), None, ALU.add).then_inc(pool_f, 1)
            nc.vector.memset(weight_of[:], 0.0).then_inc(pool_f, 1)
            logits_less_maximum()
            for n in range(STEPS):
                if n == NBLK + 1:
                    dve.wait_ge(act_dn, 1)
                    nc.vector.tensor_tensor(wdn_s[1][:], raw[:].rearrange("p (c n) -> p c n", c=NI),
                                            wdn_s[0][:].bitcast(F32), ALU.subtract).then_inc(dve_dn, 1)
                for c, (_, w) in enumerate(IT):
                    q = NI * n + c
                    dve.wait_ge(act_s, q + 1)
                    dve.wait_ge(pe_u, q + 1)
                    if q:
                        dve.wait_ge(dve_h, q)
                    nc.vector.tensor_tensor(prod[0:w, :], ps_u[q % 2][0:w, :], silu[0:w, :], ALU.mult).then_inc(dve_p, 1)
                    dve.wait_ge(act_h, q + 1)
                    nc.vector.tensor_tensor(hh[n % 2][1][0:w, c, :], prod[0:w, :],
                                            hh[n % 2][0][0:w, c, :].bitcast(F32), ALU.subtract).then_inc(dve_h, 1)
                if n >= 1:
                    add_down(nc, dve, n - 1, HS, ps_d, pe_d, dve_acc, NBLK)
                if n == 0:
                    pick()
                elif n == 2:
                    place()
                    pack()
            add_down(nc, dve, STEPS - 1, HS, ps_d, pe_d, dve_acc, NBLK)
            nc.vector.memset(silu[:], 0.0).then_inc(dve_acc, 1)
            dve.wait_ge(pe_tt, 1)
            dve.wait_ge(pool_0, 9)
            nc.vector.tensor_copy(token_of[:, 4:4 + SLOTS // P], ps_r[:, 0:P]).then_inc(dve_tt, 1)
            nc.vector.tensor_copy(weight_of[:, 2:2 + SLOTS // P], ps_c[:, 0:P]).then_inc(dve_tt, 1)


def add_down(nc, dve, n, HS, ps_d, pe_d, dve_acc, NBLK):
    if n:
        dve.wait_ge(dve_acc, ST * n)
    for i in range(ST):
        t = n % NBLK * ST + i
        dve.wait_ge(pe_d, ST * n + i + 1)
        hs = HS[:, t * D:(t + 1) * D]
        nc.vector.tensor_tensor(hs, ps_d[i % 2][:], hs, ALU.add).then_inc(dve_acc, 1)


def routed_experts(nc, sem, ps, ident, token_of, weight_of, expert_of, rows, wgu, wdn, out):
    NI = len(IT)
    HALVES = BT // P
    GU, DN = 2 * DC * I, NI * D
    GUP, DNP = 4, NI
    PIECES = GUP + DNP
    assert HALVES == 2 and NBLOCKS % 2 == 0
    with ExitStack() as ctx:
        sb = lambda name, shape, dt=F32: ctx.enter_context(nc.sbuf_tensor(name, shape, dt))
        counters, count = counting(sem)
        gu_raw = [sb(f"gu_raw{q}", [P, GU]) for q in range(2)]
        dn_raw = [sb(f"dn_raw{q}", [P, DN]) for q in range(2)]
        gu_s = [[sb(f"gu_{q}{s}", [P, 2, DC, I], F32R) for s in ("hi", "lo")] for q in range(2)]
        dn_s = [[sb(f"dn_{q}{s}", [P, NI, D], F32R) for s in ("hi", "lo")] for q in range(2)]
        xg = [sb(f"xg{q}", [P, HALVES, D]) for q in range(2)]
        xT = [[sb(f"xT5_{q}{s}", [P, DC, BT], F32R) for s in ("hi", "lo")] for q in range(2)]
        hh = [[sb(f"hh5_{q}{s}", [P, NI, BT], F32R) for s in ("hi", "lo")] for q in range(2)]
        silu = [sb(f"silu5_{k}", [P, BT]) for k in range(2)]
        prod = [sb(f"prod5_{k}", [P, BT]) for k in range(2)]
        y = [sb(f"y{q}", [P, HALVES, D]) for q in range(2)]
        gidx = [[sb(f"gidx{q}{h}", [P, 1], U32) for h in range(HALVES)] for q in range(2)]
        sidx = [[sb(f"sidx{q}{h}", [P, 1], U32) for h in range(HALVES)] for q in range(2)]
        carry = sb("carry5", [P, 1])
        begin = sb("begin", [P, 1])
        FIRST = 16
        ps_g, ps_u, ps_t, ps_d = ps[0:2], ps[2:4], ps[4:6], ps[6:8]

        ld_gu, ld_dn, ld_x = ([sem(f"{k}{q}") for q in range(2)] for k in ("ld_gu", "ld_dn", "ld_xg"))
        added, pool_c = sem("added"), count("pool_c5")
        pool_0 = sem("pool_05")
        act_w, dve_w, act_x, dve_x, pe_x = (count(k) for k in ("act_w5", "dve_w5", "act_x", "dve_x", "pe_x"))
        pe_g, pe_u, act_s, dve_p, act_h, dve_h = (count(k) for k in ("pe_g5", "pe_u5", "act_s5", "dve_p5", "act_h5", "dve_h5"))
        pe_d, dve_y, dve_i = count("pe_d5"), count("dve_y"), count("dve_i")
        block = ctx.enter_context(nc.Block())

        def gu_piece(buf, k):
            return buf.rearrange("p m c i -> p (m c i)")[:, k * GU // GUP:(k + 1) * GU // GUP]

        @block.sync
        def _(sp):
            def expert(n):
                return sp.value_load(expert_of[0:1, n], min_val=0, max_val=E - 1)

            def load(buf, src, e, landed):
                sp.dma_start(buf[:], src[bass.ds(e, 1)].rearrange("a p n -> p (a n)")).then_inc(landed, 16)

            load(gu_raw[0], wgu, expert(slice(0, 1)), ld_gu[0])
            with sp.Fori(0, NBLOCKS // 2) as g:
                for q in range(2):
                    n = 2 * g + q
                    this, following = expert(bass.ds(n, 1)), expert(bass.ds(n + 1, 1))
                    sp.wait_ge(dve_w, ONE + PIECES * n)
                    load(dn_raw[q], wdn, this, ld_dn[q])
                    load(gu_raw[1 - q], wgu, following, ld_gu[1 - q])
            sp.wait_ge(ld_gu[0], 16 * (NBLOCKS // 2 + 1))

        @block.gpsimd
        def _(pool):
            def gather(q):
                for h in range(HALVES):
                    nc.gpsimd.indirect_dma_start(xg[q][:, h, :], None, rows, bass.IndirectOffsetOnAxis(ap=gidx[q][h][:], axis=0),
                                                 bounds_check=T + BT - 1, oob_is_err=True).then_inc(ld_x[q], 16)

            def scatter(q):
                for h in range(HALVES):
                    nc.gpsimd.indirect_dma_start(out, bass.IndirectOffsetOnAxis(ap=sidx[q][h][:], axis=0), y[q][:, h, :], None,
                                                 bounds_check=T + BT - 1, oob_is_err=True,
                                                 compute_op=ALU.add).then_inc(added, 16)

            def take_waits(done):
                pool.wait_ge(pool_c, ONE + done)
                nc.gpsimd.tensor_tensor(carry[:], ident[:, 0:1], ident[:, 0:1], ALU.add).then_inc(pool_c, 1)

            for counter in counters:
                nc.gpsimd.sem_inc(counter, ONE)
            for buf in [y[0], carry] + [b for b in dn_s[1] + hh[1]]:
                nc.gpsimd.memset(buf[:].bitcast(F32), 0.0).then_inc(pool_0, 1)
            pool.wait_ge(pool_0, 6)
            pool.wait_ge(dve_i, ONE + 1)
            nc.gpsimd.dma_start(begin[:], ident[:, 0:1]).then_inc(added, FIRST)
            pool.wait_ge(added, FIRST)
            gather(0)
            gather(1)
            with pool.Fori(0, NBLOCKS // 2) as g:
                for q in range(2):
                    n = 2 * g + q
                    pool.wait_ge(dve_i, ONE + n + 2)
                    pool.wait_ge(pe_x, ONE + HALVES * (n + 1))
                    take_waits(2 * n)
                    gather(q)
                    pool.wait_ge(dve_y, ONE + HALVES * n)
                    pool.wait_ge(added, FIRST + 16 * HALVES * n)
                    take_waits(2 * n + 1)
                    scatter(q)
            pool.wait_ge(dve_i, ONE + NBLOCKS + 2)
            pool.wait_ge(dve_y, ONE + HALVES * NBLOCKS)
            pool.wait_ge(added, FIRST + 16 * HALVES * NBLOCKS)
            scatter(0)
            pool.wait_ge(added, FIRST + 16 * HALVES * (NBLOCKS + 1))
            for q in range(2):
                pool.wait_ge(ld_x[q], 16 * HALVES * (NBLOCKS // 2 + 1))

        @block.tensor
        def _(pe):
            def transposed(q):
                for h in range(HALVES):
                    for j in range(DC):
                        last = nc.tensor.transpose(ps_t[h][:, j * P:(j + 1) * P], xg[q][:, h, j * P:(j + 1) * P], ident[:])
                    last.then_inc(pe_x, 1)

            pe.wait_ge(pool_0, 6)
            pe.wait_ge(ld_x[0], 16 * HALVES)
            transposed(0)
            with pe.Fori(0, NBLOCKS // 2) as g:
                for q in range(2):
                    n = 2 * g + q
                    pe.wait_ge(dve_x, ONE + HALVES * (n + 1))
                    pe.wait_ge(dve_w, ONE + PIECES * n + GUP)
                    for c, (i0, w) in enumerate(IT):
                        k = (NI * q + c) % 2
                        pe.wait_ge(dve_p, ONE + NI * n + max(c - 1, 0))
                        for m, bank in enumerate((ps_g[k], ps_u[k])):
                            for j in range(DC):
                                last = matmul3(nc, bank[0:w, 0:BT], [x[:, m, j, i0:i0 + w] for x in gu_s[q]],
                                               [x[:, j, :] for x in xT[q]], j == 0, j == DC - 1)
                            last.then_inc((pe_g, pe_u)[m], 1)
                    pe.wait_ge(ld_x[1 - q], 16 * HALVES * (g + 1 + q))
                    transposed(1 - q)
                    pe.wait_ge(dve_h, ONE + NI * n)
                    pe.wait_ge(dve_y, ONE + HALVES * n)
                    for h in range(HALVES):
                        for c, (_, w) in enumerate(IT):
                            last = matmul3(nc, ps_d[h][:], [x[0:w, c, h * P:(h + 1) * P] for x in hh[1 - q]],
                                           [x[0:w, c, :] for x in dn_s[1 - q]], c == 0, c == NI - 1)
                        last.then_inc(pe_d, 1)

        @block.scalar
        def _(act):
            def high_rows(q, n, h):
                act.wait_ge(pe_x, ONE + HALVES * (n + 1) + h + 1)
                nc.scalar.copy(xT[q][0][:, :, h * P:(h + 1) * P], ps_t[h][:].rearrange("p (j t) -> p j t", j=DC)).then_inc(act_x, 1)

            def high_gu(q, k):
                nc.scalar.copy(gu_piece(gu_s[q][0][:], k), gu_raw[q][:, k * GU // GUP:(k + 1) * GU // GUP]).then_inc(act_w, 1)

            def high_dn(q, c):
                nc.scalar.copy(dn_s[q][0][:, c, :], dn_raw[q][:, c * D:(c + 1) * D]).then_inc(act_w, 1)

            act.wait_ge(pool_0, 6)
            act.wait_ge(ld_gu[0], 16)
            for k in range(GUP):
                high_gu(0, k)
            for h in range(HALVES):
                high_rows(0, -1, h)
            with act.Fori(0, NBLOCKS // 2) as g:
                for q in range(2):
                    n = 2 * g + q

                    def gated(c):
                        k, w = (NI * q + c) % 2, IT[c][1]
                        act.wait_ge(pe_g, ONE + NI * n + c + 1)
                        act.wait_ge(dve_p, ONE + NI * n + max(c - 1, 0))
                        nc.scalar.activation(silu[k][0:w, :], ps_g[k][0:w, 0:BT], ACT.Silu).then_inc(act_s, 1)

                    def high_product(c):
                        k, w = (NI * q + c) % 2, IT[c][1]
                        act.wait_ge(dve_p, ONE + NI * n + c + 1)
                        nc.scalar.copy(hh[q][0][0:w, c, :], prod[k][0:w, :]).then_inc(act_h, 1)

                    act.wait_ge(ld_dn[q], 16 * (g + 1))
                    act.wait_ge(pe_d, ONE + HALVES * n)
                    high_dn(q, 0)
                    high_dn(q, 1)
                    act.wait_ge(ld_gu[1 - q], 16 * (g + 1 + q))
                    act.wait_ge(pe_u, ONE + NI * n)
                    high_gu(1 - q, 0)
                    gated(0)
                    high_dn(q, 2)
                    high_product(0)
                    high_gu(1 - q, 1)
                    gated(1)
                    high_gu(1 - q, 2)
                    high_product(1)
                    gated(2)
                    high_rows(1 - q, n, 0)
                    high_product(2)
                    high_rows(1 - q, n, 1)
                    high_gu(1 - q, 3)

        @block.vector
        def _(dve):
            def low_rows(q, n, h):
                dve.wait_ge(act_x, ONE + HALVES * (n + 1) + h + 1)
                w = slice(h * P, (h + 1) * P)
                nc.vector.tensor_tensor(xT[q][1][:, :, w], ps_t[h][:].rearrange("p (j t) -> p j t", j=DC),
                                        xT[q][0][:, :, w].bitcast(F32), ALU.subtract).then_inc(dve_x, 1)

            def low_gu(q, k, done):
                dve.wait_ge(act_w, ONE + done)
                nc.vector.tensor_tensor(gu_piece(gu_s[q][1][:], k), gu_raw[q][:, k * GU // GUP:(k + 1) * GU // GUP],
                                        gu_piece(gu_s[q][0][:], k).bitcast(F32), ALU.subtract).then_inc(dve_w, 1)

            def low_dn(q, c, done):
                dve.wait_ge(act_w, ONE + done)
                nc.vector.tensor_tensor(dn_s[q][1][:, c, :], dn_raw[q][:, c * D:(c + 1) * D],
                                        dn_s[q][0][:, c, :].bitcast(F32), ALU.subtract).then_inc(dve_w, 1)

            for q in range(2):
                for h in range(HALVES):
                    at = HALVES * (q + 2) + h
                    last = nc.vector.tensor_copy(gidx[q][h][:], token_of[:, at:at + 1])
            last.then_inc(dve_i, 1)
            dve.wait_ge(pool_0, 6)
            for k in range(GUP):
                low_gu(0, k, k + 1)
            for h in range(HALVES):
                low_rows(0, -1, h)
            with dve.Fori(0, NBLOCKS // 2) as g:
                for q in range(2):
                    n = 2 * g + q
                    split = GUP + PIECES * n

                    def product(c):
                        k, w = (NI * q + c) % 2, IT[c][1]
                        dve.wait_ge(act_s, ONE + NI * n + c + 1)
                        dve.wait_ge(pe_u, ONE + NI * n + c + 1)
                        dve.wait_ge(dve_h, ONE + NI * n + max(c - 1, 0))
                        nc.vector.tensor_tensor(prod[k][0:w, :], ps_u[k][0:w, 0:BT], silu[k][0:w, :], ALU.mult).then_inc(dve_p, 1)

                    def low_product(c):
                        k, w = (NI * q + c) % 2, IT[c][1]
                        dve.wait_ge(act_h, ONE + NI * n + c + 1)
                        nc.vector.tensor_tensor(hh[q][1][0:w, c, :], prod[k][0:w, :], hh[q][0][0:w, c, :].bitcast(F32),
                                                ALU.subtract).then_inc(dve_h, 1)

                    dve.wait_ge(added, FIRST + 16 * HALVES * n)
                    for h in range(HALVES):
                        nc.vector.tensor_copy(sidx[q][h][:], token_of[:, bass.ds(HALVES * n + h, 1)])
                    for h in range(HALVES):
                        last = nc.vector.tensor_copy(gidx[q][h][:], token_of[:, bass.ds(HALVES * (n + 4) + h, 1)])
                    last.then_inc(dve_i, 1)
                    low_dn(q, 0, split + 1)
                    low_dn(q, 1, split + 2)
                    low_gu(1 - q, 0, split + 3)
                    product(0)
                    low_dn(q, 2, split + 4)
                    low_product(0)
                    low_gu(1 - q, 1, split + 5)
                    product(1)
                    low_gu(1 - q, 2, split + 6)
                    low_product(1)
                    product(2)
                    low_rows(1 - q, n, 0)
                    low_product(2)
                    low_rows(1 - q, n, 1)
                    low_gu(1 - q, 3, split + 7)
                    for h in range(HALVES):
                        dve.wait_ge(pe_d, ONE + HALVES * n + h + 1)
                        nc.vector.tensor_scalar(y[1 - q][:, h, :], ps_d[h][:], weight_of[:, bass.ds(HALVES * n + h, 1)], None,
                                                ALU.mult).then_inc(dve_y, 1)
            dve.wait_ge(added, FIRST + 16 * HALVES * NBLOCKS)
            for h in range(HALVES):
                last = nc.vector.tensor_copy(sidx[0][h][:], token_of[:, HALVES * NBLOCKS + h:HALVES * NBLOCKS + h + 1])
            last.then_inc(dve_i, 1)


def program(nc, x, ctxT, wqkT, bqk, ln1, ln2, wqk, wv, wo, gateT, wgu, wdn, out):
    with ExitStack() as ctx:
        sb = lambda name, shape, dt=F32: ctx.enter_context(nc.sbuf_tensor(name, shape, dt))
        sem = lambda name: ctx.enter_context(nc.semaphore(name))
        spill = nc.dram_tensor("x1_spill", [NB, P, ST, D], F32, kind="Internal").ap()
        rows = nc.dram_tensor("normed_rows", [T + BT, D], F32, kind="Internal").ap()
        table = nc.dram_tensor("slot_table", [SLOTS, 2], F32, kind="Internal").ap()
        tiled = lambda a: a[0:T, :].rearrange("(b t p) n -> b p t n", p=P, b=NB)
        pads = lambda a: [a[T + k * P:T + (k + 1) * P, :] for k in range(BT // P)]
        ident = sb("ident", [P, P])
        ident16 = sb("ident16", [P, P], BF16)
        causal = sb("causal", [P, P], BF16)
        neg_half = sb("neg_half", [P, ST])
        eps = sb("eps", [P, 2, ST])
        ps = [ctx.enter_context(nc.psum_tensor(f"ps{k}", [P, 512], F32)) for k in range(8)]
        constants(nc, sem, ident, ident16, causal, neg_half, eps)
        token_of = sb("token_of", [P, SLOTS // P + 8], U32)
        weight_of = sb("weight_of", [P, SLOTS // P + 2])
        expert_of = sb("expert_of", [1, NEXP], I32)
        with ExitStack() as stream:
            HS = stream.enter_context(nc.sbuf_tensor("HS", [P, TT * D], F32))
            hT = [stream.enter_context(nc.sbuf_tensor(f"hT_{s}", [P, DC, T], F32R)) for s in ("hi", "lo")]
            cross_attention(nc, sem, ps, ident, neg_half, eps, HS, hT, x, ctxT, wqkT, bqk, ln1, spill)
            self_attention(nc, sem, ps, ident, ident16, causal, HS, hT, wqk, wv, wo)
            logits = stream.enter_context(nc.sbuf_tensor("logits", [P, TT, E], F32))
            normed_again(nc, sem, ps, ident, neg_half, eps, HS, hT, logits, tiled(rows), pads(rows), ln2, gateT, spill)
            shared_expert(nc, sem, ps, ident, HS, hT, logits, token_of, weight_of, expert_of, wgu[E:NE], wdn[E:NE],
                          table, tiled(out), pads(out))
        routed_experts(nc, sem, ps, ident, token_of, weight_of, expert_of, rows, wgu, wdn, out)


def kernel(**inputs):
    import numpy as np
    import concourse.bacc as bacc
    from concourse.bass_utils import run_bass_kernel_spmd

    a = {k: np.asarray(v) for k, v in inputs.items()}
    w = lambda name: a["L0_ffn_" + name]
    chunks = lambda m: m.reshape(-1, P, m.shape[-1]).transpose(1, 0, 2)
    experts_of = lambda e, s: np.concatenate([w(e), w(s).reshape(NSH, I, D)])
    down = np.concatenate([w("ed_w").transpose(0, 2, 1), w("sd_w").T.reshape(NSH, I, D)])
    down = np.concatenate([down, np.zeros((NE, len(IT) * P - I, D), np.float32)], axis=1)
    gu = np.stack([experts_of("eg_w", "sg_w"), experts_of("eu_w", "su_w")], axis=1)
    qk = np.stack([w("wq").reshape(DC, P, H, HD), w("wk").reshape(DC, P, H, HD)])
    arrays = {
        "x": a["x"].reshape(NB, ST, P, D).transpose(0, 2, 1, 3),
        "ctxT": a["ctx_1024"].transpose(0, 2, 1).reshape(NB, CC, P, S).transpose(0, 2, 1, 3),
        "wqkT": np.stack([chunks(a["L0_xattn_Wq"].T), chunks(a["L0_xattn_Wk"].T)], axis=1),
        "bqk": np.stack([a["L0_xattn_bq"], a["L0_xattn_bk"]], axis=1),
        "ln1": w("ln1_w"),
        "ln2": w("ln2_w"),
        "wqk": qk.transpose(3, 2, 0, 1, 4).reshape(H, P, 2 * DC * HD),
        "wv": w("wv").reshape(DC, P, HP, 2 * HD).transpose(2, 1, 0, 3).reshape(HP, P, DC * 2 * HD),
        "wo": w("wo").reshape(HP, 2, P, D).transpose(0, 2, 1, 3).reshape(HP, P, 2 * D),
        "gateT": chunks(w("gate_w").T),
        "wgu": gu.transpose(0, 1, 3, 2).reshape(NE, 2, DC, P, I).transpose(0, 3, 1, 2, 4).reshape(NE, P, 2 * DC * I),
        "wdn": down.reshape(NE, len(IT), P, D).transpose(0, 2, 1, 3).reshape(NE, P, len(IT) * D),
    }
    nc = bacc.Bacc("TRN2", target_bir_lowering=False, num_devices=1)
    arrays = {"in_" + k: np.ascontiguousarray(v) for k, v in arrays.items()}
    args = [nc.dram_tensor(k, v.shape, mybir.dt.from_np(v.dtype), kind="ExternalInput").ap() for k, v in arrays.items()]
    out = nc.dram_tensor("out", (T + BT, D), F32, kind="ExternalOutput").ap()
    program(nc, *args, out)
    r = run_bass_kernel_spmd(nc, [arrays], core_ids=[0])
    return r.results[0]["out"][0:T].reshape(NB, S, D)
```

```python
from contextlib import ExitStack

import concourse.bass as bass
from concourse import mybir

F32 = mybir.dt.float32
F32R = mybir.dt.float32r
BF16 = mybir.dt.bfloat16
I32 = mybir.dt.int32
U32 = mybir.dt.uint32
ALU = mybir.AluOpType
ACT = mybir.ActivationFunctionType
AX = mybir.AxisListType

P = 128
NB = 4
S = 512
D = 512
DC = D // P
C = 256
CC = C // P
ST = S // P
T = NB * S
TT = T // P
H = 16
HD = 128
HP = H // 2
E = 16
TOPK = 6
I = 352
NSH = 2
NE = E + NSH
IT = [(0, 128), (128, 128), (256, 96)]
BT = 256
NBLOCKS = (T * TOPK + E * (BT - 1)) // BT // 2 * 2 + 2
SLOTS = NBLOCKS * BT
LN_EPS = 1e-5
RMS_EPS = 1e-6
MASKED = -1e30
SCALE = float(HD) ** -0.5
ONE = 1


def matmul3(nc, out, lhs, rhs, start, stop):
    nc.tensor.matmul(out, lhs[0], rhs[0], start=start, stop=False)
    nc.tensor.matmul(out, lhs[0], rhs[1], start=False, stop=False)
    return nc.tensor.matmul(out, lhs[1], rhs[0], start=False, stop=stop)


def counting(sem):
    counters = []

    def count(name):
        counters.append(sem(name))
        return counters[-1]

    return counters, count


def constants(nc, sem, ident, ident16, causal, neg_half, eps):
    made = sem("const_made")
    with nc.Block() as block:
        @block.gpsimd
        def _(pool):
            nc.gpsimd.memset(ident[:], 0.0).then_inc(made, 1)
            nc.gpsimd.memset(causal[:], 0.0).then_inc(made, 1)
            nc.gpsimd.memset(neg_half[:], -0.5).then_inc(made, 1)
            nc.gpsimd.memset(eps[:, 0, :], LN_EPS).then_inc(made, 1)
            nc.gpsimd.memset(eps[:, 1, :], RMS_EPS).then_inc(made, 1)
            pool.wait_ge(made, 5)
            nc.gpsimd.affine_select(out=ident[:], in_=ident[:], compare_op=ALU.not_equal, fill=1.0, base=0,
                                    pattern=[[-1, P]], channel_multiplier=1).then_inc(made, 1)
            nc.gpsimd.affine_select(out=causal[:], in_=causal[:], compare_op=ALU.is_ge, fill=MASKED, base=0,
                                    pattern=[[-1, P]], channel_multiplier=1).then_inc(made, 1)
            pool.wait_ge(made, 7)
            nc.gpsimd.tensor_copy(ident16[:], ident[:]).then_inc(made, 1)


def cross_attention(nc, sem, ps, ident, neg_half, eps, HS, hT, space, x, ctxT, wqkT, bqk, ln1, spill,
                    next_raw, next_w, ld_next, next_wqk, qkT):
    with ExitStack() as ctx:
        sb = lambda name, shape, dt=F32: ctx.enter_context(nc.sbuf_tensor(name, shape, dt))
        X = [sb(f"x_{u}", [P, ST, S]) for u in range(2)]
        feat = [sb(f"feat_{u}", [P, CC, S]) for u in range(2)]
        feat_s = [w.rearrange("p (c n) -> p c n", c=CC) for w in next_wqk]
        w_raw = sb("wqk_raw", [P, 2, CC, P])
        w_s = [w[:, ST * S:ST * S + 2 * CC * P].rearrange("p (m c n) -> p m c n", m=2, c=CC) for w in space]
        bias = sb("bqk", [P, 2])
        ln1b = sb("ln1b", [P, D])
        xT = [sb(f"xT_{s}", [P, ST, S], F32R) for s in ("hi", "lo")]
        aT = [w[:, 0:ST * S].rearrange("p (j m) -> p j m", j=ST) for w in space]
        prob = sb("prob1", [P, ST, S])
        norm = sb("norm1", [P, ST, S])
        st6 = sb("st6", [P, 2, ST, 6])
        mv = sb("mv", [P, 2, ST, 2])
        rstd = sb("rstd", [P, 2, ST])
        shift = sb("shift", [P, 2, ST])
        ms = sb("ms", [P, ST])
        rms = sb("rms", [P, ST])
        negmax = sb("negmax1", [P, ST])
        rsum = sb("rsum1", [P, ST])
        rinv = sb("rinv1", [P, ST])
        ps_qk, ps_e = ps[0:2], ps[2:4] + ps[0:2]
        ps_t = ps_m = ps[4:8]

        ld_w, ld_b, ld_x, ld_f = sem("ld_w"), sem("ld_b"), [sem(f"ld_x{u}") for u in range(2)], [sem(f"ld_f{u}") for u in range(2)]
        spilled = [sem(f"spilled{u}") for u in range(2)]
        act_w, dve_w = sem("act_w1"), sem("dve_w1")
        act_f, dve_f, pool_f = sem("act_f"), sem("dve_f1"), sem("pool_f1")
        pe_qk, act_qk, dve_qk = sem("pe_qk1"), sem("act_qk1"), sem("dve_qk1")
        dve_st, dve_mv, pool_x, act_xn = sem("dve_st"), sem("dve_mv"), sem("pool_x"), sem("act_xn")
        dve_st1, dve_mv1, pool_x1, pool_c = sem("dve_st1"), sem("dve_mv1"), sem("pool_x1"), sem("pool_c1")
        pe_t, act_t, dve_t = sem("pe_t1"), sem("act_t1"), sem("dve_t1")
        pe_e, dve_max, act_exp = sem("pe_e1"), sem("dve_max1"), sem("act_exp1")
        dve_ri, act_nrm = sem("dve_ri1"), sem("act_nrm")
        pe_m, dve_x1 = sem("pe_m"), sem("dve_x1")
        pool_s1, act_hs, dve_h = sem("pool_s1"), sem("act_hs"), sem("dve_h1")

        act_nw, dve_nw, pe_nq, act_nq, dve_nq = (sem(k) for k in ("act_nw", "dve_nw", "pe_nq", "act_nq", "dve_nq"))
        next_w_s = [w.rearrange("p (m c n) -> p m c n", m=2, c=DC) for w in next_wqk]

        x_tile = lambda n: 3 * ST * n - ST if n else 0
        h_tile = lambda n: 3 * ST * (n + 1) - (ST if n == NB - 1 else 0)
        a_tile = lambda n: 3 * ST * n + ST

        block = ctx.enter_context(nc.Block())

        @block.sync
        def _(sp):
            sp.dma_start(w_raw[:], wqkT).then_inc(ld_w, 16)
            sp.dma_start(X[0][:], x[0]).then_inc(ld_x[0], 16)
            sp.dma_start(ln1b[:], ln1.partition_broadcast(P)).then_inc(ld_b, 16)
            sp.dma_start(feat[1][:], ctxT[1]).then_inc(ld_f[1], 16)
            sp.dma_start(X[1][:], x[1]).then_inc(ld_x[1], 16)
            for raw, src, landed in zip(next_raw, next_w, ld_next):
                sp.dma_start(raw, src).then_inc(landed, 16)
            for n in range(NB):
                u = n % 2
                if n + 2 < NB:
                    if n:
                        sp.wait_ge(pool_f, n)
                    else:
                        sp.wait_ge(dve_f, 1)
                    sp.dma_start(feat[u][:], ctxT[n + 2]).then_inc(ld_f[u], 16)
                sp.wait_ge(dve_x1, ST * (n + 1))
                sp.dma_start(spill[n], X[u][:]).then_inc(spilled[u], 16)
                if n + 2 < NB:
                    sp.wait_ge(spilled[u], 16)
                    sp.wait_ge(act_hs, ST * (n + 1))
                    sp.dma_start(X[u][:], x[n + 2]).then_inc(ld_x[u], 16)
            for u in range(2):
                sp.wait_ge(spilled[u], 16 * (NB // 2))

        @block.gpsimd
        def _(pool):
            done = [0]

            def step(out, a, b, op):
                done[0] += 1
                nc.gpsimd.tensor_tensor(out, a, b, op).then_inc(pool_c, 1)
                pool.wait_ge(pool_c, done[0])

            def deviation(k, ready):
                step(rstd[:, k, :], mv[:, k, :, 1], eps[:, 0, :], ALU.add)
                step(rstd[:, k, :], rstd[:, k, :], neg_half[:, 0:ST], ALU.pow)
                step(shift[:, k, :], mv[:, k, :, 0], neg_half[:, 0:ST], ALU.mult)
                step(shift[:, k, :], shift[:, k, :], shift[:, k, :], ALU.add)
                nc.gpsimd.tensor_tensor(shift[:, k, :], shift[:, k, :], rstd[:, k, :], ALU.mult).then_inc(ready, 1)

            def of_x(n):
                pool.wait_ge(dve_mv, ST * (n + 1))
                deviation(0, pool_x)

            def low_feat(n):
                pool.wait_ge(act_f, n + 1)
                nc.gpsimd.tensor_tensor(feat_s[1], feat[n % 2][:], feat_s[0].bitcast(F32), ALU.subtract).then_inc(pool_f, 1)

            of_x(0)
            for n in range(NB):
                if n + 1 < NB:
                    low_feat(n + 1)
                    of_x(n + 1)
                pool.wait_ge(dve_mv1, ST * (n + 1))
                deviation(1, pool_s1)
                step(ms[:], mv[:, 1, :, 1], rstd[:, 1, :], ALU.mult)
                step(ms[:], ms[:], rstd[:, 1, :], ALU.mult)
                step(rms[:], ms[:], eps[:, 1, :], ALU.add)
                nc.gpsimd.tensor_tensor(rms[:], rms[:], neg_half[:, 0:ST], ALU.pow).then_inc(pool_x1, 1)

        @block.tensor
        def _(pe):
            def transposed(src, i, k):
                if k >= ST:
                    pe.wait_ge(dve_t, k - ST + 1)
                for j in range(ST):
                    last = nc.tensor.transpose(ps_t[i][:, j * P:(j + 1) * P], src[:, i, j * P:(j + 1) * P], ident[:])
                last.then_inc(pe_t, 1)

            def normed_rows(n):
                for i in range(ST):
                    pe.wait_ge(dve_h, ST * n + i + 1)
                    transposed(norm, i, h_tile(n) + i)

            pe.wait_ge(dve_w, 1)
            for n in range(NB):
                if n == 0:
                    pe.wait_ge(dve_f, 1)
                else:
                    pe.wait_ge(pool_f, n)
                    pe.wait_ge(act_exp, ST * n)
                for m in range(2):
                    for c in range(CC):
                        last = matmul3(nc, ps_qk[m][:], [w[:, m, c, :] for w in w_s], [f[:, c, :] for f in feat_s],
                                       c == 0, c == CC - 1)
                    last.then_inc(pe_qk, 1)
                for i in range(ST):
                    pe.wait_ge(act_xn, ST * n + i + 1)
                    if n:
                        pe.wait_ge(dve_x1, ST * (n - 1) + i + 1)
                    transposed(norm, i, x_tile(n) + i)
                pe.wait_ge(dve_qk, 2 * n + 2)
                for i in range(ST):
                    matmul3(nc, ps_e[i][:], [q[:, 0, i * P:(i + 1) * P] for q in qkT],
                            [k[:, 1, :] for k in qkT], True, True).then_inc(pe_e, 1)
                if n:
                    normed_rows(n - 1)
                for i in range(ST):
                    pe.wait_ge(act_nrm, ST * n + i + 1)
                    transposed(prob, i, a_tile(n) + i)
                pe.wait_ge(act_t, a_tile(n) + ST)
                for i in range(2):
                    pe.wait_ge(dve_t, a_tile(n) + i + 1)
                    for x_part in xT:
                        for j in range(ST):
                            nc.tensor.matmul(ps_m[i][:], x_part[:, j, i * P:(i + 1) * P], aT[0][:, j, :],
                                             start=x_part is xT[0] and j == 0, stop=False)
                pe.wait_ge(dve_t, a_tile(n) + ST)
                for i in range(2):
                    for j in range(ST):
                        last = nc.tensor.matmul(ps_m[i][:], xT[0][:, j, i * P:(i + 1) * P], aT[1][:, j, :],
                                                start=False, stop=j == ST - 1)
                    last.then_inc(pe_m, 1)
                for i in range(2, ST):
                    for j in range(ST):
                        last = matmul3(nc, ps_m[i][:], [a[:, j, i * P:(i + 1) * P] for a in xT],
                                       [a[:, j, :] for a in aT], j == 0, j == ST - 1)
                    last.then_inc(pe_m, 1)
            pe.wait_ge(dve_nw, 1)
            for m in range(2):
                for c in range(DC):
                    last = matmul3(nc, ps_qk[m][:], [w[:, m, c, :] for w in next_w_s], [h[:, c, 0:S] for h in hT],
                                   c == 0, c == DC - 1)
                last.then_inc(pe_nq, 1)
            pe.wait_ge(dve_x1, ST * NB)
            normed_rows(NB - 1)

        @block.scalar
        def _(act):
            def high_of_tile(hi, i, k):
                act.wait_ge(pe_t, k + 1)
                nc.scalar.copy(hi, ps_t[i][:].rearrange("p (j t) -> p j t", j=ST)).then_inc(act_t, 1)

            def high_feat(n):
                act.wait_ge(ld_f[n % 2], 16 * (n // 2 + 1))
                if n:
                    act.wait_ge(pe_qk, 2 * n)
                nc.scalar.copy(feat_s[0], feat[n % 2][:]).then_inc(act_f, 1)

            def layer_norm(n):
                if n:
                    act.wait_ge(pe_t, h_tile(n - 2) + ST if n > 1 else x_tile(0) + ST)
                act.wait_ge(pool_x, n + 1)
                for i in range(ST):
                    nc.scalar.activation(norm[:, i, :], X[n % 2][:, i, :], ACT.Identity, bias=shift[:, 0, i:i + 1],
                                         scale=rstd[:, 0, i:i + 1]).then_inc(act_xn, 1)

            def normed_x1(n):
                act.wait_ge(pool_s1, n + 1)
                for i in range(ST):
                    nc.scalar.activation(HS[:, (ST * n + i) * D:(ST * n + i + 1) * D], X[n % 2][:, i, :], ACT.Identity,
                                         bias=shift[:, 1, i:i + 1], scale=rstd[:, 1, i:i + 1]).then_inc(act_hs, 1)

            def normed_rows(n):
                for i in range(ST):
                    high_of_tile(hT[0][:, :, (ST * n + i) * P:(ST * n + i + 1) * P], i, h_tile(n) + i)

            act.dma_start(feat[0][:], ctxT[0]).then_inc(ld_f[0], 16)
            act.dma_start(bias[:], bqk).then_inc(ld_b, 16)
            act.wait_ge(ld_w, 16)
            nc.scalar.copy(w_s[0][:], w_raw[:]).then_inc(act_w, 1)
            high_feat(0)
            act.wait_ge(ld_b, 32)
            layer_norm(0)
            for n in range(NB):
                for m in range(2):
                    act.wait_ge(pe_qk, 2 * n + m + 1)
                    nc.scalar.activation(qkT[0][:, m, :], ps_qk[m][:], ACT.Identity, bias=bias[:, m:m + 1]).then_inc(act_qk, 1)
                for i in range(ST):
                    high_of_tile(xT[0][:, :, i * P:(i + 1) * P], i, x_tile(n) + i)
                if n:
                    normed_x1(n - 1)
                for i in range(ST):
                    act.wait_ge(dve_max, ST * n + i + 1)
                    nc.scalar.activation(prob[:, i, :], ps_e[i][:], ACT.Exp, bias=negmax[:, i:i + 1],
                                         accum_out=rsum[:, i:i + 1]).then_inc(act_exp, 1)
                for i in range(ST):
                    act.wait_ge(dve_ri, ST * n + i + 1)
                    nc.scalar.mul(prob[:, i, :], prob[:, i, :], rinv[:, i:i + 1]).then_inc(act_nrm, 1)
                if n:
                    normed_rows(n - 1)
                for i in range(ST):
                    high_of_tile(aT[0][:, :, i * P:(i + 1) * P], i, a_tile(n) + i)
                if n + 1 < NB:
                    high_feat(n + 1)
                    layer_norm(n + 1)
            act.wait_ge(ld_next[0], 16)
            act.wait_ge(pe_qk, 2 * NB)
            nc.scalar.copy(next_wqk[0], next_raw[0]).then_inc(act_nw, 1)
            for m in range(2):
                act.wait_ge(pe_nq, m + 1)
                nc.scalar.mul(qkT[0][:, m, :], ps_qk[m][:], SCALE if m == 0 else 1.0).then_inc(act_nq, 1)
            normed_x1(NB - 1)
            normed_rows(NB - 1)

        @block.vector
        def _(dve):
            def statistics(n):
                dve.wait_ge(ld_x[n % 2], 16 * (n // 2 + 1))
                for i in range(ST):
                    nc.vector.bn_stats(st6[:, 0, i, :], X[n % 2][:, i, :]).then_inc(dve_st, 1)
                dve.wait_ge(dve_st, ST * (n + 1))
                for i in range(ST):
                    nc.vector.bn_aggr(mv[:, 0, i, :], st6[:, 0, i, :]).then_inc(dve_mv, 1)

            def low_of_tile(lo, hi, i, k):
                dve.wait_ge(act_t, k + 1)
                nc.vector.tensor_tensor(lo, ps_t[i][:].rearrange("p (j t) -> p j t", j=ST),
                                        hi.bitcast(F32), ALU.subtract).then_inc(dve_t, 1)

            def normed(n, i):
                row = slice((ST * n + i) * D, (ST * n + i + 1) * D)
                dve.wait_ge(act_hs, ST * n + i + 1)
                nc.vector.scalar_tensor_tensor(out=norm[:, i, :], in0=HS[:, row], scalar=rms[:, i:i + 1],
                                               in1=ln1b[:], op0=ALU.mult, op1=ALU.mult).then_inc(dve_h, 1)

            def low_of_rows(n):
                for i in range(ST):
                    w = slice((ST * n + i) * P, (ST * n + i + 1) * P)
                    low_of_tile(hT[1][:, :, w], hT[0][:, :, w], i, h_tile(n) + i)

            dve.wait_ge(ld_w, 16)
            dve.wait_ge(act_w, 1)
            nc.vector.tensor_tensor(w_s[1][:], w_raw[:], w_s[0][:].bitcast(F32), ALU.subtract).then_inc(dve_w, 1)
            dve.wait_ge(act_f, 1)
            nc.vector.tensor_tensor(feat_s[1], feat[0][:], feat_s[0].bitcast(F32), ALU.subtract).then_inc(dve_f, 1)
            statistics(0)
            dve.wait_ge(ld_b, 32)
            for n in range(NB):
                for m in range(2):
                    dve.wait_ge(act_qk, 2 * n + m + 1)
                    nc.vector.scalar_tensor_tensor(out=qkT[1][:, m, :], in0=ps_qk[m][:], scalar=bias[:, m:m + 1],
                                                   in1=qkT[0][:, m, :].bitcast(F32), op0=ALU.add,
                                                   op1=ALU.subtract).then_inc(dve_qk, 1)
                for i in range(ST):
                    w = slice(i * P, (i + 1) * P)
                    low_of_tile(xT[1][:, :, w], xT[0][:, :, w], i, x_tile(n) + i)
                for i in range(ST):
                    dve.wait_ge(pe_e, ST * n + i + 1)
                    nc.vector.tensor_reduce(negmax[:, i:i + 1], ps_e[i][:], AX.X, ALU.max, negate=True).then_inc(dve_max, 1)
                for i in range(ST):
                    if n:
                        dve.wait_ge(pool_x1, n)
                        normed(n - 1, i)
                    dve.wait_ge(act_exp, ST * n + i + 1)
                    nc.vector.reciprocal(rinv[:, i:i + 1], rsum[:, i:i + 1]).then_inc(dve_ri, 1)
                if n:
                    low_of_rows(n - 1)
                for i in range(ST):
                    w = slice(i * P, (i + 1) * P)
                    low_of_tile(aT[1][:, :, w], aT[0][:, :, w], i, a_tile(n) + i)
                if n + 1 < NB:
                    statistics(n + 1)
                else:
                    dve.wait_ge(act_nw, 1)
                    nc.vector.tensor_tensor(next_wqk[1], next_raw[0], next_wqk[0].bitcast(F32), ALU.subtract).then_inc(dve_nw, 1)
                for i in range(ST):
                    dve.wait_ge(pe_m, ST * n + i + 1)
                    nc.vector.tensor_tensor(X[n % 2][:, i, :], ps_m[i][:], X[n % 2][:, i, :], ALU.add).then_inc(dve_x1, 1)
                    dve.wait_ge(dve_x1, ST * n + i + 1)
                    nc.vector.bn_stats(st6[:, 1, i, :], X[n % 2][:, i, :]).then_inc(dve_st1, 1)
                dve.wait_ge(dve_st1, ST * (n + 1))
                for i in range(ST):
                    nc.vector.bn_aggr(mv[:, 1, i, :], st6[:, 1, i, :]).then_inc(dve_mv1, 1)
            for m in range(2):
                dve.wait_ge(act_nq, m + 1)
                nc.vector.scalar_tensor_tensor(out=qkT[1][:, m, :], in0=ps_qk[m][:], scalar=SCALE if m == 0 else 1.0,
                                               in1=qkT[0][:, m, :].bitcast(F32), op0=ALU.mult,
                                               op1=ALU.subtract).then_inc(dve_nq, 1)
            dve.wait_ge(pool_x1, NB)
            for i in range(ST):
                normed(NB - 1, i)
            low_of_rows(NB - 1)


def self_attention(nc, sem, ps, ident, ident16, causal, HS, hT, space, raw, ld_raw, wqk_0, qkT, wqk, wv, wo):
    STEPS = 2 * NB
    VG = TT // 2
    with ExitStack() as ctx:
        sb = lambda name, shape, dt=F32: ctx.enter_context(nc.sbuf_tensor(name, shape, dt))
        counters, count = counting(sem)
        wqk_s = [[w.rearrange("p (m c n) -> p m c n", m=2, c=DC) for w in wqk_0],
                 [sb(f"wqk_1{s}", [P, 2, DC, HD], F32R)[:] for s in ("hi", "lo")]]
        wv_s = [sb(f"wv_{s}", [P, DC, 2 * HD], F32R) for s in ("hi", "lo")]
        wo_s = [sb(f"wo_{s}", [P, 2, D], F32R) for s in ("hi", "lo")]
        v_s = [sb(f"v_{s}", [P, TT, 2 * HD], F32R) for s in ("hi", "lo")]
        prob = [sb(f"prob_{i}", [P, (i + 1) * P]) for i in range(ST)]
        pT = [w[:, 0:ST * S].rearrange("p (j t) -> p j t", j=ST) for w in space]
        oT = [w[:, ST * S:(ST + 1) * S] for w in space]
        negmax = sb("negmax", [P, 2, ST])
        rsum = sb("rsum", [P, 2, ST])
        rinv = sb("rinv", [P, 2, ST])
        zero = sb("zero", [P, 1])
        ps_t, ps_p, ps_w = ps[2:4], ps[4:6], ps[6:8] + ps[2:4]
        ps_s = [ps_p[1], ps_p[0], ps[1], ps[0]]
        TILES = list(reversed(range(ST)))
        ps_o = ps_t[0]
        width = [max(2, i + 1) * P for i in range(ST)]
        first = [0, P, 2 * P, 2 * P]

        pool_hi, pool_lo, pool_0 = count("pool_hi"), count("pool_lo"), sem("pool_0")
        pe_qk, act_qk, dve_qk = count("pe_qk"), count("act_qk"), count("dve_qk")
        pe_v, act_v, dve_v = count("pe_v"), count("act_v"), count("dve_v")
        pe_s, dve_max, act_exp = count("pe_s"), count("dve_max"), count("act_exp")
        pe_t, act_t, dve_t = count("pe_t"), count("act_t"), count("dve_t")
        pe_o, act_o, dve_o = count("pe_o"), count("act_o"), count("dve_o")
        dve_ri, pe_w, dve_acc = count("dve_ri"), count("pe_w"), count("dve_acc")

        JOBS, EARLY = 4, 1
        flat_qk = [[w.rearrange("p a c n -> p (a c n)") for w in wqk_s[hh]] for hh in range(2)]
        flat_v = [w[:].rearrange("p c n -> p (c n)") for w in wv_s]
        flat_o = [w[:].rearrange("p a n -> p (a n)") for w in wo_s]
        block = ctx.enter_context(nc.Block())

        @block.sync
        def _(sp):
            def load(r, src):
                sp.dma_start(raw[r], src.rearrange("a p n -> p (a n)")).then_inc(ld_raw[r], 16)

            with sp.Fori(0, HP) as g:
                for job in range(JOBS):
                    src = [wqk[bass.ds(2 * g + 1, 1)], wo[bass.ds(g, 1)], wqk[bass.ds(2 * g + 2, 1)], wv[bass.ds(g + 1, 1)]][job]
                    sp.wait_ge(pool_lo, ONE + JOBS * g + job)
                    load(job % 2, src)

        @block.gpsimd
        def _(pool):
            for counter in counters:
                nc.gpsimd.sem_inc(counter, ONE)

            def split(r, dst, done):
                nc.gpsimd.tensor_tensor(dst[0], raw[r], zero[:].to_broadcast([P, 1024]), ALU.add).then_inc(pool_hi, 1)
                pool.wait_ge(pool_hi, ONE + done + 1)
                nc.gpsimd.tensor_tensor(dst[1], raw[r], dst[0].bitcast(F32), ALU.subtract).then_inc(pool_lo, 1)

            for counter in (pe_qk, act_qk, dve_qk):
                nc.gpsimd.sem_inc(counter, 2)
            nc.gpsimd.memset(zero[:], 0.0).then_inc(pool_0, 1)
            pool.wait_ge(pool_0, 1)
            pool.wait_ge(ld_raw[1], 16)
            split(1, flat_v, 0)
            for buf in oT + wo_s:
                nc.gpsimd.memset(buf[:].bitcast(F32), 0.0).then_inc(pool_0, 1)
            for buf in pT:
                nc.gpsimd.memset(buf[:].bitcast(F32), 0.0).then_inc(pool_0, 1)
            nc.gpsimd.memset(rinv[:], 0.0).then_inc(pool_0, 1)
            with pool.Fori(0, HP) as g:
                for job in range(JOBS):
                    pool.wait_ge(ld_raw[job % 2], 32 * g + 16 * (job // 2) + 32)
                    if job == 0:
                        pool.wait_ge(pe_qk, ONE + 2 * STEPS * g)
                    elif job == 1:
                        pool.wait_ge(pe_w, ONE + ST * (STEPS * g + 1))
                    elif job == 2:
                        pool.wait_ge(pe_qk, ONE + 2 * STEPS * g + 2 * NB)
                    else:
                        pool.wait_ge(pe_v, ONE + VG * g + VG)
                    split(job % 2, [flat_qk[1], flat_o, flat_qk[0], flat_v][job], EARLY + JOBS * g + job)

        @block.tensor
        def _(pe):
            def project(hh, b, m, c):
                last = matmul3(nc, ps_p[m][:], [w[:, m, c, :] for w in wqk_s[hh]],
                               [h[:, c, b * S:(b + 1) * S] for h in hT], c == 0, c == DC - 1)
                if c == DC - 1:
                    last.then_inc(pe_qk, 1)

            def output(s, i, n):
                hh = (s - 1) % STEPS // NB
                matmul3(nc, ps_w[i][:], [o[:, i * P:(i + 1) * P] for o in oT], [w[:, hh, :] for w in wo_s],
                        True, True).then_inc(pe_w, 1)

            pe.wait_ge(pool_0, 1)
            with pe.Fori(0, HP) as g:
                pe.wait_ge(pool_lo, ONE + JOBS * g + EARLY)
                for v in range(VG):
                    if v < 2:
                        pe.wait_ge(dve_qk, ONE + 2 * STEPS * g + v + 1)
                    else:
                        pe.wait_ge(dve_v, ONE + VG * g + v - 1)
                    for k in range(2):
                        for c in range(DC):
                            last = matmul3(nc, ps_p[v % 2][:, k * 2 * HD:(k + 1) * 2 * HD],
                                           [h[:, c, (2 * v + k) * P:(2 * v + k + 1) * P] for h in hT],
                                           [w[:, c, :] for w in wv_s], c == 0, c == DC - 1)
                    last.then_inc(pe_v, 1)
                for s in range(STEPS):
                    hh, b = s // NB, s % NB
                    n = STEPS * g + s
                    nxt = ((s + 1) % STEPS // NB, (s + 1) % NB)
                    pe.wait_ge(dve_qk, ONE + 2 * n + 2)
                    for i in TILES:
                        if s == 0 and i == 1:
                            pe.wait_ge(dve_v, ONE + VG * g + VG)
                        matmul3(nc, ps_s[i][:, 0:width[i]], [q[:, 0, i * P:(i + 1) * P] for q in qkT],
                                [k[:, 1, 0:width[i]] for k in qkT], True, False)
                        nc.tensor.matmul(ps_s[i][:, i * P:(i + 1) * P], ident16[:], causal[:],
                                         start=False, stop=True).then_inc(pe_s, 1)
                    pe.wait_ge(dve_o, ONE + n)
                    if s == 0:
                        pe.wait_ge(pool_0, 8)
                    elif s == 1:
                        pe.wait_ge(pool_lo, ONE + JOBS * g + EARLY + 2)
                    for i in range(ST):
                        output(s, i, n)
                    if s + 1 == NB:
                        pe.wait_ge(pool_lo, ONE + JOBS * g + EARLY + 1)
                    elif s + 1 == STEPS:
                        pe.wait_ge(pool_lo, ONE + JOBS * g + EARLY + 3)
                    pe.wait_ge(act_exp, ONE + ST * n + ST)
                    for c in range(DC):
                        project(*nxt, 0, c)
                    for k, i in enumerate(TILES):
                        if k < 2:
                            pe.wait_ge(dve_acc, ONE + ST * n + 3 + k)
                        else:
                            pe.wait_ge(dve_t, ONE + ST * n + k - 1)
                        for j in range(i + 1):
                            last = nc.tensor.transpose(ps_t[k % 2][:, j * P:(j + 1) * P], prob[i][:, j * P:(j + 1) * P], ident[:])
                        last.then_inc(pe_t, 1)
                        for c in [(), (0, 1), (2,), (3,)][k]:
                            project(*nxt, 1, c)
                    pe.wait_ge(act_t, ONE + ST * n + ST)
                    for j in range(ST):
                        o, (v_hi, v_lo) = ps_o[:, first[j]:S], [v[:, b * ST + j, hh * HD:(hh + 1) * HD] for v in v_s]
                        p_hi, p_lo = [p[:, j, first[j]:S] for p in pT]
                        if j == 0:
                            pe.wait_ge(dve_t, ONE + ST * n + ST - 1)
                        nc.tensor.matmul(o, v_hi, p_hi, start=j == 0, stop=False)
                        nc.tensor.matmul(o, v_lo, p_hi, start=False, stop=False)
                        if j == 0:
                            pe.wait_ge(dve_t, ONE + ST * n + ST)
                        last = nc.tensor.matmul(o, v_hi, p_lo, start=False, stop=j == ST - 1)
                    last.then_inc(pe_o, 1)
            pe.wait_ge(dve_o, ONE + STEPS * HP)
            for i in range(ST):
                output(0, i, STEPS * HP)

        @block.scalar
        def _(act):
            def high_qk(m, done):
                act.wait_ge(pe_qk, ONE + done)
                nc.scalar.mul(qkT[0][:, m, :], ps_p[m][:], SCALE if m == 0 else 1.0).then_inc(act_qk, 1)

            act.wait_ge(pool_0, 1)
            with act.Fori(0, HP) as g:
                for v in range(VG):
                    act.wait_ge(pe_v, ONE + VG * g + v + 1)
                    nc.scalar.copy(v_s[0][:, 2 * v:2 * v + 2, :],
                                   ps_p[v % 2][:].rearrange("p (k n) -> p k n", k=2)).then_inc(act_v, 1)
                for s in range(STEPS):
                    n = STEPS * g + s
                    if s == 0:
                        act.wait_ge(pool_0, 8)
                    for k, i in enumerate(TILES):
                        act.wait_ge(dve_max, ONE + ST * n + k + 1)
                        nc.scalar.activation(prob[i][:], ps_s[i][:, 0:(i + 1) * P], ACT.Exp,
                                             bias=negmax[:, s % 2, i:i + 1],
                                             accum_out=rsum[:, s % 2, i:i + 1]).then_inc(act_exp, 1)
                    high_qk(0, 2 * n + 3)
                    for k, i in enumerate(TILES):
                        act.wait_ge(pe_t, ONE + ST * n + k + 1)
                        nc.scalar.copy(pT[0][:, 0:i + 1, i * P:(i + 1) * P],
                                       ps_t[k % 2][:, 0:(i + 1) * P].rearrange("p (j t) -> p j t", t=P)).then_inc(act_t, 1)
                    high_qk(1, 2 * n + 4)
                    act.wait_ge(pe_o, ONE + n + 1)
                    nc.scalar.copy(oT[0][:], ps_o[:]).then_inc(act_o, 1)

        @block.vector
        def _(dve):
            def low_qk(m, done):
                dve.wait_ge(act_qk, ONE + done)
                nc.vector.scalar_tensor_tensor(out=qkT[1][:, m, :], in0=ps_p[m][:], scalar=SCALE if m == 0 else 1.0,
                                               in1=qkT[0][:, m, :].bitcast(F32), op0=ALU.mult,
                                               op1=ALU.subtract).then_inc(dve_qk, 1)

            def add_output(s, n):
                dve.wait_ge(dve_ri, ONE + n)
                dve.wait_ge(dve_acc, ONE + ST * n)
                for i in range(ST):
                    tile = (s - 1) % NB * ST + i
                    dve.wait_ge(pe_w, ONE + ST * n + i + 1)
                    hs = HS[:, tile * D:(tile + 1) * D]
                    nc.vector.scalar_tensor_tensor(out=hs, in0=ps_w[i][:], scalar=rinv[:, (s - 1) % 2, i:i + 1],
                                                   in1=hs, op0=ALU.mult, op1=ALU.add).then_inc(dve_acc, 1)

            dve.wait_ge(pool_0, 1)
            with dve.Fori(0, HP) as g:
                for v in range(VG):
                    dve.wait_ge(act_v, ONE + VG * g + v + 1)
                    nc.vector.tensor_tensor(v_s[1][:, 2 * v:2 * v + 2, :], ps_p[v % 2][:].rearrange("p (k n) -> p k n", k=2),
                                            v_s[0][:, 2 * v:2 * v + 2, :].bitcast(F32), ALU.subtract).then_inc(dve_v, 1)
                for s in range(STEPS):
                    n = STEPS * g + s
                    if s == 0:
                        dve.wait_ge(pool_0, 8)
                    for k, i in enumerate(TILES):
                        dve.wait_ge(pe_s, ONE + ST * n + k + 1)
                        nc.vector.tensor_reduce(negmax[:, s % 2, i:i + 1], ps_s[i][:, 0:(i + 1) * P], AX.X,
                                                ALU.max, negate=True).then_inc(dve_max, 1)
                    add_output(s, n)
                    dve.wait_ge(act_exp, ONE + ST * n + ST)
                    nc.vector.reciprocal(rinv[:, s % 2, :], rsum[:, s % 2, :]).then_inc(dve_ri, 1)
                    for k, i in enumerate(TILES):
                        dve.wait_ge(act_t, ONE + ST * n + k + 1)
                        w = slice(i * P, (i + 1) * P)
                        nc.vector.tensor_tensor(pT[1][:, 0:i + 1, w], ps_t[k % 2][:, 0:(i + 1) * P].rearrange("p (j t) -> p j t", t=P),
                                                pT[0][:, 0:i + 1, w].bitcast(F32), ALU.subtract).then_inc(dve_t, 1)
                        if k == 1:
                            low_qk(0, 2 * n + 3)
                    low_qk(1, 2 * n + 4)
                    dve.wait_ge(act_o, ONE + n + 1)
                    nc.vector.tensor_tensor(oT[1][:], ps_o[:], oT[0][:].bitcast(F32), ALU.subtract).then_inc(dve_o, 1)
            add_output(0, STEPS * HP)


def normed_again(nc, sem, ps, ident, neg_half, eps, HS, hT, logits, rows, pad_rows, ln2, gateT, spill, space, wgu0):
    NG = TT // ST
    GU = 2 * DC * I
    PIECE = GU // NG
    with ExitStack() as ctx:
        sb = lambda name, shape, dt=F32: ctx.enter_context(nc.sbuf_tensor(name, shape, dt))
        x1 = [sb(f"x1_{u}", [P, ST, D]) for u in range(2)]
        ln2b = sb("ln2b", [P, D])
        gate = sb("gate", [P, DC, P])
        gate_s = [sb(f"gate_{s}", [P, DC, P], F32R) for s in ("hi", "lo")]
        norm = [sb(f"norm3_{u}", [P, ST, D]) for u in range(2)]
        zeros = sb("zeros3", [P, D])
        squares = sb("squares", [P, D])
        sumsq = sb("sumsq", [P, NG, ST])
        inv_d = sb("inv_d", [P, ST])
        ms = sb("ms3", [P, ST])
        rms = sb("rms3", [P, 2, ST])
        logT = sb("logT", [P, S])
        w_raw = sb("w_raw3", [P, GU])
        w_s = space
        ps_t, ps_l, ps_lt = ps[0:4], ps[4:6], ps[6:8]

        ld_g, ld_x1, ld_w = sem("ld_g"), [sem(f"ld_x1{u}") for u in range(2)], sem("ld_w3")
        stored, padded = [sem(f"rows_stored{u}") for u in range(2)], sem("rows_padded")
        pool_z, act_g, dve_g, act_w, dve_w = sem("pool_z"), sem("act_g"), sem("dve_g"), sem("act_w3"), sem("dve_w3")
        act_sq, pool_c, pool_r = sem("act_sq3"), sem("pool_c3"), sem("pool_r3")
        dve_h, pe_t, act_t, dve_t = sem("dve_h3"), sem("pe_t3"), sem("act_t3"), sem("dve_t3")
        pool_a = sem("pool_a")
        pe_l, act_l, pe_lt, act_lt = sem("pe_l"), sem("act_l"), sem("pe_lt"), sem("act_lt")

        block = ctx.enter_context(nc.Block())

        @block.sync
        def _(sp):
            sp.dma_start(ln2b[:], ln2.partition_broadcast(P)).then_inc(ld_g, 16)
            sp.wait_ge(pool_z, 2)
            sp.dma_start(gate[:, :, 0:E], gateT).then_inc(ld_g, 16)
            for u in range(2):
                sp.dma_start(x1[u][:], spill[u]).then_inc(ld_x1[u], 16)
            sp.dma_start(w_raw[:], wgu0).then_inc(ld_w, 16)
            for pad in pad_rows:
                sp.dma_start(pad, zeros[:]).then_inc(padded, 16)
            for g in range(NG):
                sp.wait_ge(dve_h, ST * (g + 1))
                sp.dma_start(rows[g], norm[g % 2][:]).then_inc(stored[g % 2], 16)
                if g + 2 < NG:
                    sp.wait_ge(pool_a, ST * (g + 1))
                    sp.dma_start(x1[g % 2][:], spill[g + 2]).then_inc(ld_x1[g % 2], 16)
            for u in range(2):
                sp.wait_ge(stored[u], 16 * (NG // 2))
            sp.wait_ge(padded, 16 * len(pad_rows))

        @block.gpsimd
        def _(pool):
            done = [0]

            def step(out, a, b, op):
                done[0] += 1
                nc.gpsimd.tensor_tensor(out, a, b, op).then_inc(pool_c, 1)
                pool.wait_ge(pool_c, done[0])

            def inverse_rms(g):
                u = g % 2
                if g:
                    pool.wait_ge(pool_r, g)
                pool.wait_ge(act_sq, ST * (g + 1))
                step(ms[:], sumsq[:, g, :], inv_d[:], ALU.mult)
                step(ms[:], ms[:], eps[:, 1, :], ALU.add)
                nc.gpsimd.tensor_tensor(rms[:, u, :], ms[:], neg_half[:, 0:ST], ALU.pow).then_inc(pool_r, 1)

            nc.gpsimd.memset(gate[:], 0.0).then_inc(pool_z, 1)
            nc.gpsimd.memset(zeros[:], 0.0).then_inc(pool_z, 1)
            nc.gpsimd.memset(inv_d[:], 1.0 / D).then_inc(pool_z, 1)
            pool.wait_ge(pool_z, 3)
            inverse_rms(0)
            for g in range(NG):
                if g + 1 < NG:
                    inverse_rms(g + 1)
                pool.wait_ge(ld_x1[g % 2], 16 * (g // 2 + 1))
                for i in range(ST):
                    row = slice((ST * g + i) * D, (ST * g + i + 1) * D)
                    pool.wait_ge(dve_h, ST * g + i + 1)
                    nc.gpsimd.tensor_tensor(HS[:, row], HS[:, row], x1[g % 2][:, i, :], ALU.add).then_inc(pool_a, 1)

        @block.tensor
        def _(pe):
            def expert_logits(g):
                pe.wait_ge(dve_t, ST * (g + 1))
                if g == 0:
                    pe.wait_ge(dve_g, 1)
                elif g >= 2:
                    pe.wait_ge(act_l, g - 1)
                for c in range(DC):
                    last = matmul3(nc, ps_l[g % 2][:], [w[:, c, :] for w in gate_s],
                                   [h[:, c, g * S:(g + 1) * S] for h in hT], c == 0, c == DC - 1)
                last.then_inc(pe_l, 1)

            def logits_by_token(g):
                pe.wait_ge(act_l, g + 1)
                if g >= 2:
                    pe.wait_ge(act_lt, g - 1)
                for i in range(ST):
                    last = nc.tensor.transpose(ps_lt[g % 2][:, i * P:(i + 1) * P], logT[:, i * P:(i + 1) * P], ident[:])
                last.then_inc(pe_lt, 1)

            for g in range(NG):
                for i in range(ST):
                    pe.wait_ge(dve_h, ST * g + i + 1)
                    if g:
                        pe.wait_ge(dve_t, ST * (g - 1) + i + 1)
                    for j in range(DC):
                        last = nc.tensor.transpose(ps_t[i][:, j * P:(j + 1) * P], norm[g % 2][:, i, j * P:(j + 1) * P], ident[:])
                    last.then_inc(pe_t, 1)
                if g >= 1:
                    logits_by_token(g - 1)
                expert_logits(g)
            logits_by_token(NG - 1)

        @block.scalar
        def _(act):
            def logits_out(g):
                act.wait_ge(pe_lt, g + 1)
                nc.scalar.copy(logits[:, g * ST:(g + 1) * ST, :],
                               ps_lt[g % 2][:].rearrange("p (t e) -> p t e", e=P)[:, :, 0:E]).then_inc(act_lt, 1)

            def sums_of_squares(g):
                for i in range(ST):
                    if g + i:
                        act.wait_ge(act_sq, ST * g + i)
                    nc.scalar.activation(squares[:], HS[:, (ST * g + i) * D:(ST * g + i + 1) * D], ACT.Square,
                                         accum_out=sumsq[:, g, i:i + 1]).then_inc(act_sq, 1)

            sums_of_squares(0)
            act.wait_ge(ld_g, 32)
            nc.scalar.copy(gate_s[0][:], gate[:]).then_inc(act_g, 1)
            sums_of_squares(1)
            for g in range(NG):
                for i in range(ST):
                    act.wait_ge(pe_t, ST * g + i + 1)
                    nc.scalar.copy(hT[0][:, :, (ST * g + i) * P:(ST * g + i + 1) * P],
                                   ps_t[i][:].rearrange("p (j t) -> p j t", j=DC)).then_inc(act_t, 1)
                if g >= 1:
                    logits_out(g - 1)
                act.wait_ge(ld_w, 16)
                w = slice(g * PIECE, (g + 1) * PIECE)
                nc.scalar.copy(w_s[0][:, w], w_raw[:, w]).then_inc(act_w, 1)
                act.wait_ge(pe_l, g + 1)
                nc.scalar.copy(logT[:], ps_l[g % 2][:]).then_inc(act_l, 1)
                if g + 2 < NG:
                    sums_of_squares(g + 2)
            logits_out(NG - 1)

        @block.vector
        def _(dve):
            for g in range(NG):
                dve.wait_ge(pool_r, g + 1)
                if g == 0:
                    dve.wait_ge(ld_g, 32)
                if g >= 2:
                    dve.wait_ge(stored[g % 2], 16)
                    dve.wait_ge(pe_t, ST * (g - 1))
                for i in range(ST):
                    nc.vector.scalar_tensor_tensor(out=norm[g % 2][:, i, :], in0=HS[:, (ST * g + i) * D:(ST * g + i + 1) * D],
                                                   scalar=rms[:, g % 2, i:i + 1], in1=ln2b[:], op0=ALU.mult,
                                                   op1=ALU.mult).then_inc(dve_h, 1)
                if g == 0:
                    dve.wait_ge(act_g, 1)
                    nc.vector.tensor_tensor(gate_s[1][:], gate[:], gate_s[0][:].bitcast(F32), ALU.subtract).then_inc(dve_g, 1)
                for i in range(ST):
                    w = slice((ST * g + i) * P, (ST * g + i + 1) * P)
                    dve.wait_ge(act_t, ST * g + i + 1)
                    nc.vector.tensor_tensor(hT[1][:, :, w], ps_t[i][:].rearrange("p (j t) -> p j t", j=DC),
                                            hT[0][:, :, w].bitcast(F32), ALU.subtract).then_inc(dve_t, 1)
                w = slice(g * PIECE, (g + 1) * PIECE)
                dve.wait_ge(act_w, g + 1)
                nc.vector.tensor_tensor(w_s[1][:, w], w_raw[:, w], w_s[0][:, w].bitcast(F32), ALU.subtract).then_inc(dve_w, 1)


def shared_expert(nc, sem, ps, ident, HS, hT, logits, token_of, weight_of, expert_of, first_wgu,
                  all_wgu, wdn, table, out, pad_out, first_rows, rows, ld_rows, added, begin):
    NBLK = T // S
    STEPS = NSH * NBLK
    POOL_JOBS = 3
    NI = len(IT)
    wgu = all_wgu[E:NE]
    with ExitStack() as ctx:
        sb = lambda name, shape, dt=F32: ctx.enter_context(nc.sbuf_tensor(name, shape, dt))
        raw = sb("wx_raw", [P, NI * D])
        wgu_s = [first_wgu, [sb(f"wgu_1{s}", [P, 2, DC, I], F32R) for s in ("hi", "lo")]]
        wdn_s = [sb(f"wdn_{s}", [P, NI, D], F32R) for s in ("hi", "lo")]
        hh = [[sb(f"hh_{k}{s}", [P, NI, S], F32R) for s in ("hi", "lo")] for k in range(2)]
        silu = sb("silu", [P, S])
        prod = sb("prod", [P, S])
        ex = sb("ex", [P, TT, E])
        sel = sb("sel", [P, TT, E])
        acc = [sb(f"acc{k}", [P, TT, E]) for k in range(2)]
        pos = sb("pos", [P, TT, E])
        tmp = sb("tmp", [P, TT, E])
        sel16 = sb("sel16", [P, TT, E], BF16)
        before = sb("before", [P, P], BF16)
        ones = sb("ones", [P, P], BF16)
        top = sb("top", [P, TT, 8])
        mx = sb("mx", [P, TT])
        cnt = sb("cnt", [P, TT])
        blocks = sb("blocks", [P, 3, E])
        blocks_i = sb("blocks_i", [P, E], I32)
        pair = sb("pair", [P, TT, TOPK, 2])
        free = [w[:].rearrange("p h n -> p (h n)") for w in first_rows]
        slot = free[0][:, SLOTS // P:SLOTS // P + TT * TOPK].rearrange("p (t r) -> p t r", t=TT)
        slot_i = sb("slot_i", [P, TT, TOPK], U32)
        token = sb("token", [P, TT])
        fresh = sb("fresh", [P, SLOTS // P, 2])
        fresh_i = free[0][:, 0:SLOTS // P].bitcast(I32)
        number = sb("number", [1, NBLOCKS])
        bounds = free[1][0:1, 0:NBLOCKS * E].rearrange("p (n e) -> p n e", e=E)
        wide = lambda a: a.unsqueeze(2).to_broadcast([P, TT, E])
        ps_g, ps_u, ps_d, ps_r, ps_c = ps[0:2], ps[2:4], ps[4:6], ps[6], ps[7]

        ld_w, pool_hi, pool_lo, pool_0 = sem("ld_w4"), sem("pool_hi4"), sem("pool_lo4"), sem("pool_04")
        pe_g, pe_u, act_s, dve_p, act_h, dve_h = (sem(k) for k in ("pe_g", "pe_u", "act_s", "dve_p", "act_h4", "dve_h4"))
        pe_d, dve_acc, stored = sem("pe_d"), sem("dve_acc4"), sem("stored")
        dve_r, dve_c, act_e, pe_r = sem("dve_r"), sem("dve_c"), sem("act_e"), sem("pe_r")
        pool_f, ld_f, scattered, ld_t, pe_tt, dve_tt = (sem(k) for k in ("pool_f", "ld_f4", "scattered", "ld_t", "pe_tt", "dve_tt"))
        dve_z = sem("dve_z4")
        act_late, dve_late = sem("act_late"), sem("dve_late")
        LOGITS, PICKED, PACKED = 1, 2, 3
        block = ctx.enter_context(nc.Block())

        @block.sync
        def _(sp):
            def load(src):
                sp.dma_start(raw[:, 0:src.shape[-1]], src).then_inc(ld_w, 16)

            gate_or_up = lambda w, m: w[:, m * DC * I:(m + 1) * DC * I]
            load(wdn[0])
            sp.wait_ge(pool_f, 3)
            sp.dma_start(table.rearrange("(p j) w -> p j w", p=P), fresh[:]).then_inc(ld_f, 16)
            for job, src in enumerate([gate_or_up(wgu[1], 0), gate_or_up(wgu[1], 1), wdn[1]]):
                sp.wait_ge(pool_lo, job + 1)
                load(src)
            sp.wait_ge(dve_r, PACKED)
            expert = sp.value_load(expert_of[0:1, 0:1], min_val=0, max_val=E - 1)
            for m in range(2):
                sp.wait_ge(dve_late, m + 1)
                load(gate_or_up(all_wgu[bass.ds(expert, 1)].rearrange("a p n -> p (a n)"), m))
            sp.wait_ge(scattered, 16 * TT * TOPK)
            sp.dma_start(fresh[:], table.rearrange("(j p) w -> j p w", p=P)).then_inc(ld_t, 16)
            for b in range(NB - 1):
                sp.wait_ge(dve_acc, ST * (STEPS - NB + b + 1))
                sp.dma_start(out[b], HS[:, b * ST * D:(b + 1) * ST * D].rearrange("p (t n) -> p t n", n=D)).then_inc(stored, 16)
            for i in range(ST):
                t = TT - ST + i
                sp.wait_ge(dve_acc, ST * (STEPS - 1) + i + 1)
                sp.dma_start(out[NB - 1][:, i, :], HS[:, t * D:(t + 1) * D]).then_inc(stored, 16)
            sp.wait_ge(dve_z, 1)
            for pad in pad_out:
                sp.dma_start(pad, silu[:]).then_inc(stored, 16)
            sp.wait_ge(stored, 16 * (NB - 1 + ST + len(pad_out)))

        @block.gpsimd
        def _(pool):
            nc.gpsimd.memset(fresh[:], 0.0).then_inc(pool_0, 1)
            nc.gpsimd.memset(ones[:], 1.0).then_inc(pool_0, 1)
            nc.gpsimd.memset(expert_of[:], 0).then_inc(pool_0, 1)
            nc.gpsimd.iota(fresh_i, pattern=[[1, SLOTS // P]], base=0, channel_multiplier=SLOTS // P).then_inc(pool_0, 1)
            nc.gpsimd.iota(number[:], pattern=[[1, NBLOCKS]], base=0, channel_multiplier=0,
                           allow_small_or_imprecise_dtypes=True).then_inc(pool_0, 1)
            nc.gpsimd.iota(token[:], pattern=[[P, TT]], base=0, channel_multiplier=1,
                           allow_small_or_imprecise_dtypes=True).then_inc(pool_0, 1)
            for at in (0, 4 + SLOTS // P):
                nc.gpsimd.iota(token_of[:, at:at + 4].bitcast(I32).rearrange("p (a b) -> p a b", a=2),
                               pattern=[[0, 2], [P, 2]], base=T, channel_multiplier=1).then_inc(pool_0, 1)
            pool.wait_ge(pool_0, 8)
            nc.gpsimd.affine_select(out=before[:], in_=ones[:], compare_op=ALU.is_gt, fill=0.0, base=0,
                                    pattern=[[1, P]], channel_multiplier=-1).then_inc(pool_0, 1)
            for job in range(POOL_JOBS):
                if job:
                    n, dst = DC * I, [w[:, job - 1].rearrange("p c n -> p (c n)") for w in wgu_s[1]]
                else:
                    n, dst = NI * D, [w[:].rearrange("p c n -> p (c n)") for w in wdn_s]
                pool.wait_ge(ld_w, 16 * (job + 1))
                nc.gpsimd.tensor_copy(dst[0], raw[:, 0:n]).then_inc(pool_hi, 1)
                pool.wait_ge(pool_hi, job + 1)
                nc.gpsimd.tensor_tensor(dst[1], raw[:, 0:n], dst[0].bitcast(F32), ALU.subtract).then_inc(pool_lo, 1)
            pool.wait_ge(ld_f, 16)
            for r in range(TOPK):
                pool.wait_ge(dve_r, PACKED + r)
                for t in range(TT):
                    nc.gpsimd.indirect_dma_start(table, bass.IndirectOffsetOnAxis(ap=slot_i[:, t, r:r + 1], axis=0),
                                                 pair[:, t, r, :], None, bounds_check=SLOTS - 1,
                                                 oob_is_err=False).then_inc(scattered, 16)
            for k in range(begin.shape[-1]):
                nc.gpsimd.dma_start(begin[:, k:k + 1], ident[:, 0:1]).then_inc(added, 16)
            pool.wait_ge(dve_tt, 1)
            for q, (buf, landed) in enumerate(zip(first_rows, ld_rows)):
                for h in range(BT // P):
                    at = 4 + q * (BT // P) + h
                    nc.gpsimd.indirect_dma_start(buf[:, h, :], None, rows, bass.IndirectOffsetOnAxis(ap=token_of[:, at:at + 1], axis=0),
                                                 bounds_check=T + BT - 1, oob_is_err=True).then_inc(landed, 16)

        @block.tensor
        def _(pe):
            def down(n):
                if n == 0:
                    pe.wait_ge(pool_lo, 1)
                elif n == NBLK:
                    pe.wait_ge(dve_late, 1)
                pe.wait_ge(dve_h, NI * (n + 1))
                for i in range(ST):
                    if ST * n + i >= 2:
                        pe.wait_ge(dve_acc, ST * n + i - 1)
                    for c, (_, w) in enumerate(IT):
                        last = matmul3(nc, ps_d[i % 2][:], [h[0:w, c, i * P:(i + 1) * P] for h in hh[n % 2]],
                                       [x[0:w, c, :] for x in wdn_s], c == 0, c == NI - 1)
                    last.then_inc(pe_d, 1)

            for n in range(STEPS):
                k, blk = n // NBLK, n % NBLK
                if n == NBLK:
                    pe.wait_ge(pool_lo, POOL_JOBS)
                for c, (i0, w) in enumerate(IT):
                    q = NI * n + c
                    if q >= 2:
                        pe.wait_ge(dve_p, q - 1)
                    for m, bank in enumerate((ps_g[q % 2], ps_u[q % 2])):
                        for j in range(DC):
                            last = matmul3(nc, bank[0:w, :], [x[:, m, j, i0:i0 + w] for x in wgu_s[k]],
                                           [h[:, j, blk * S:(blk + 1) * S] for h in hT], j == 0, j == DC - 1)
                        last.then_inc((pe_g, pe_u)[m], 1)
                if n >= 1:
                    down(n - 1)
                if n == 1:
                    pe.wait_ge(dve_r, PICKED)
                    pe.wait_ge(pool_0, 9)
                    chosen = sel16[:].rearrange("p t e -> p (t e)")
                    nc.tensor.matmul(ps_r[:, 0:TT * E], before[:], chosen, start=True, stop=True)
                    nc.tensor.matmul(ps_c[:, 0:TT * E], ones[:], chosen, start=True, stop=True).then_inc(pe_r, 1)
            pe.wait_ge(ld_t, 16)
            nc.tensor.transpose(ps_r[:, 0:P], fresh[:, :, 0], ident[:])
            nc.tensor.transpose(ps_c[:, 0:P], fresh[:, :, 1], ident[:]).then_inc(pe_tt, 1)
            down(STEPS - 1)

        @block.scalar
        def _(act):
            act.wait_ge(dve_r, LOGITS)
            nc.scalar.activation(ex[:], tmp[:], ACT.Exp).then_inc(act_e, 1)
            for n in range(STEPS):
                late = n - NBLK - 1
                if late >= 0:
                    act.wait_ge(ld_w, 16 * (POOL_JOBS + late + 1))
                if late == 0:
                    act.wait_ge(pe_d, ST * NBLK)
                    nc.scalar.copy(wdn_s[0][:], raw[:].rearrange("p (c n) -> p c n", c=NI)).then_inc(act_late, 1)
                elif late > 0:
                    nc.scalar.copy(first_wgu[0][:, late - 1],
                                   raw[:, 0:DC * I].rearrange("p (c n) -> p c n", c=DC)).then_inc(act_late, 1)
                for c, (_, w) in enumerate(IT):
                    q = NI * n + c
                    act.wait_ge(pe_g, q + 1)
                    if q:
                        act.wait_ge(dve_p, q)
                    nc.scalar.activation(silu[0:w, :], ps_g[q % 2][0:w, :], ACT.Silu).then_inc(act_s, 1)
                    act.wait_ge(dve_p, q + 1)
                    nc.scalar.copy(hh[n % 2][0][0:w, c, :], prod[0:w, :]).then_inc(act_h, 1)

        @block.vector
        def _(dve):
            done = [0]

            def step(ins):
                done[0] += 1
                ins.then_inc(dve_c, 1)
                dve.wait_ge(dve_c, done[0])

            def running(a, b, src, axis, size):
                at = lambda x, lo, hi: x[:, lo:hi, :] if axis == 1 else x[:, :, lo:hi]
                dist = 1
                while dist < size:
                    step(nc.vector.tensor_copy(at(a, 0, dist), at(src, 0, dist)))
                    step(nc.vector.tensor_tensor(at(a, dist, size), at(src, dist, size), at(src, 0, size - dist), ALU.add))
                    src, a, b = a, b, a
                    dist *= 2
                return src

            def logits_less_maximum():
                step(nc.vector.tensor_reduce(mx[:], logits[:], AX.X, ALU.max))
                nc.vector.tensor_tensor(tmp[:], logits[:], wide(mx[:]), ALU.subtract).then_inc(dve_r, 1)

            def pick():
                dve.wait_ge(act_e, 1)
                for t in range(TT):
                    last = nc.vector.max(top[:, t, :], ex[:, t, :])
                step(last)
                sixth = wide(top[:, :, TOPK - 1])
                step(nc.vector.tensor_tensor(sel[:], ex[:], sixth, ALU.is_gt))
                step(nc.vector.tensor_tensor(tmp[:], ex[:], sixth, ALU.is_equal))
                step(nc.vector.tensor_reduce(cnt[:], sel[:], AX.X, ALU.add))
                step(nc.vector.tensor_scalar(cnt[:], cnt[:], -1.0, float(TOPK), ALU.mult, ALU.add))
                equal = running(acc[0][:], acc[1][:], tmp[:], 2, E)
                step(nc.vector.tensor_tensor(pos[:], equal, wide(cnt[:]), ALU.is_le))
                step(nc.vector.tensor_tensor(tmp[:], tmp[:], pos[:], ALU.mult))
                step(nc.vector.tensor_tensor(sel[:], sel[:], tmp[:], ALU.add))
                nc.vector.tensor_copy(sel16[:], sel[:]).then_inc(dve_r, 1)
                step(nc.vector.tensor_tensor(ex[:], ex[:], sel[:], ALU.mult))
                step(nc.vector.tensor_reduce(mx[:], ex[:], AX.X, ALU.add))
                step(nc.vector.reciprocal(cnt[:], mx[:]))
                step(nc.vector.tensor_tensor(ex[:], ex[:], wide(cnt[:]), ALU.mult))

            def count_tokens():
                dve.wait_ge(pe_r, 1)
                counts = ps_c[:, 0:TT * E].rearrange("p (t e) -> p t e", e=E)
                step(nc.vector.tensor_copy(tmp[:], counts))
                return running(acc[0][:], acc[1][:], tmp[:], 1, TT)

            def place(total):
                step(nc.vector.tensor_scalar(blocks_i[:], total[:, TT - 1, :], float(BT - 1), None, ALU.add))
                step(nc.vector.tensor_scalar(blocks_i[:], blocks_i[:], BT.bit_length() - 1, None, ALU.arith_shift_right))
                step(nc.vector.tensor_copy(blocks[:, 0, :], blocks_i[:]))
                step(nc.vector.tensor_tensor(pos[:], total, tmp[:], ALU.subtract))
                step(nc.vector.tensor_tensor(pos[:], pos[:], ps_r[:, 0:TT * E].rearrange("p (t e) -> p t e", e=E), ALU.add))
                return running(blocks[:, 1:2, :], blocks[:, 2:3, :], blocks[:, 0:1, :], 2, E)

            def place_blocks(ends):
                step(nc.vector.tensor_tensor(bounds, ends[0:1].to_broadcast([1, NBLOCKS, E]),
                                             number[:].unsqueeze(2).to_broadcast([1, NBLOCKS, E]), ALU.is_le))
                step(nc.vector.tensor_reduce(number[:], bounds, AX.X, ALU.add))
                step(nc.vector.tensor_scalar(expert_of[:], number[:], float(E - 1), None, ALU.min))
                step(nc.vector.tensor_tensor(blocks[:, 0:1, :], ends, blocks[:, 0:1, :], ALU.subtract))
                step(nc.vector.tensor_scalar(blocks[:, 0, :], blocks[:, 0, :], float(BT), None, ALU.mult))
                step(nc.vector.tensor_tensor(pos[:], pos[:], blocks[:, 0:1, :].to_broadcast([P, TT, E]), ALU.add))
                running(acc[0][:], acc[1][:], sel[:], 2, E)

            def pack(r):
                nth = acc[1]
                step(nc.vector.scalar_tensor_tensor(out=tmp[:].rearrange("p t e -> p (t e)"),
                                                    in0=nth[:].rearrange("p t e -> p (t e)"), scalar=float(r + 1),
                                                    in1=sel[:].rearrange("p t e -> p (t e)"), op0=ALU.is_equal, op1=ALU.mult))
                step(nc.vector.tensor_tensor(acc[0][:], tmp[:], pos[:], ALU.mult))
                step(nc.vector.tensor_tensor(tmp[:], tmp[:], ex[:], ALU.mult))
                step(nc.vector.tensor_reduce(slot[:, :, r:r + 1], acc[0][:], AX.X, ALU.add))
                step(nc.vector.tensor_reduce(pair[:, :, r, 1:2], tmp[:], AX.X, ALU.add))
                step(nc.vector.tensor_copy(pair[:, :, r, 0:1], token[:].unsqueeze(2)))
                nc.vector.tensor_copy(slot_i[:, :, r:r + 1], slot[:, :, r:r + 1]).then_inc(dve_r, 1)

            dve.wait_ge(pool_0, 9)
            nc.vector.tensor_scalar(fresh_i, fresh_i, BT - 1, None, ALU.bitwise_and).then_inc(pool_f, 1)
            dve.wait_ge(pool_f, 1)
            nc.vector.tensor_scalar(fresh[:, :, 0], fresh_i, float(T), None, ALU.add).then_inc(pool_f, 1)
            nc.vector.memset(weight_of[:], 0.0).then_inc(pool_f, 1)
            logits_less_maximum()
            for n in range(STEPS):
                late = n - NBLK - 1
                if late >= 0:
                    dve.wait_ge(act_late, late + 1)
                if late == 0:
                    nc.vector.tensor_tensor(wdn_s[1][:], raw[:].rearrange("p (c n) -> p c n", c=NI),
                                            wdn_s[0][:].bitcast(F32), ALU.subtract).then_inc(dve_late, 1)
                elif late > 0:
                    nc.vector.tensor_tensor(first_wgu[1][:, late - 1], raw[:, 0:DC * I].rearrange("p (c n) -> p c n", c=DC),
                                            first_wgu[0][:, late - 1].bitcast(F32), ALU.subtract).then_inc(dve_late, 1)
                for c, (_, w) in enumerate(IT):
                    q = NI * n + c
                    dve.wait_ge(act_s, q + 1)
                    dve.wait_ge(pe_u, q + 1)
                    if q:
                        dve.wait_ge(dve_h, q)
                    nc.vector.tensor_tensor(prod[0:w, :], ps_u[q % 2][0:w, :], silu[0:w, :], ALU.mult).then_inc(dve_p, 1)
                    dve.wait_ge(act_h, q + 1)
                    nc.vector.tensor_tensor(hh[n % 2][1][0:w, c, :], prod[0:w, :],
                                            hh[n % 2][0][0:w, c, :].bitcast(F32), ALU.subtract).then_inc(dve_h, 1)
                    piece = 2 * (n - 2) + c if c < 2 else None
                    if piece == 0:
                        ends = place(total)
                    elif piece == 1:
                        place_blocks(ends)
                    elif piece in range(2, 2 + TOPK):
                        pack(piece - 2)
                if n >= 1:
                    add_down(nc, dve, n - 1, HS, ps_d, pe_d, dve_acc, NBLK)
                if n == 0:
                    pick()
                elif n == 1:
                    total = count_tokens()
            nc.vector.memset(silu[:], 0.0).then_inc(dve_z, 1)
            dve.wait_ge(pe_tt, 1)
            dve.wait_ge(pool_0, 9)
            nc.vector.tensor_copy(token_of[:, 4:4 + SLOTS // P], ps_r[:, 0:P]).then_inc(dve_tt, 1)
            nc.vector.tensor_copy(weight_of[:, 2:2 + SLOTS // P], ps_c[:, 0:P]).then_inc(dve_tt, 1)
            add_down(nc, dve, STEPS - 1, HS, ps_d, pe_d, dve_acc, NBLK)


def add_down(nc, dve, n, HS, ps_d, pe_d, dve_acc, NBLK):
    if n:
        dve.wait_ge(dve_acc, ST * n)
    for i in range(ST):
        t = n % NBLK * ST + i
        dve.wait_ge(pe_d, ST * n + i + 1)
        hs = HS[:, t * D:(t + 1) * D]
        nc.vector.tensor_tensor(hs, ps_d[i % 2][:], hs, ALU.add).then_inc(dve_acc, 1)


def routed_experts(nc, sem, ps, ident, token_of, weight_of, expert_of, rows, first_wgu, xg, ld_x, added, begin,
                   wgu, wdn, out):
    NI = len(IT)
    HALVES = BT // P
    GU, DN = 2 * DC * I, NI * D
    GUP, DNP = 4, NI
    PIECES = GUP + DNP
    TURNS = NBLOCKS // 2 - 1
    assert HALVES == 2 and NBLOCKS % 2 == 0
    with ExitStack() as ctx:
        sb = lambda name, shape, dt=F32: ctx.enter_context(nc.sbuf_tensor(name, shape, dt))
        counters, count = counting(sem)
        gu_raw = [sb(f"gu_raw{q}", [P, GU]) for q in range(2)]
        dn_raw = [sb(f"dn_raw{q}", [P, DN]) for q in range(2)]
        gu_s = [first_wgu, [sb(f"gu_1{s}", [P, 2, DC, I], F32R) for s in ("hi", "lo")]]
        dn_s = [[sb(f"dn_{q}{s}", [P, NI, D], F32R) for s in ("hi", "lo")] for q in range(2)]
        xT = [[sb(f"xT5_{q}{s}", [P, DC, BT], F32R) for s in ("hi", "lo")] for q in range(2)]
        hh = [[sb(f"hh5_{q}{s}", [P, NI, BT], F32R) for s in ("hi", "lo")] for q in range(2)]
        silu = [sb(f"silu5_{k}", [P, BT]) for k in range(2)]
        prod = [sb(f"prod5_{k}", [P, BT]) for k in range(2)]
        y = [sb(f"y{q}", [P, HALVES, D]) for q in range(2)]
        gidx = [[sb(f"gidx{q}{h}", [P, 1], U32) for h in range(HALVES)] for q in range(2)]
        sidx = [[sb(f"sidx{q}{h}", [P, 1], U32) for h in range(HALVES)] for q in range(2)]
        carry = sb("carry5", [P, 1])
        FIRST = 16 * begin.shape[-1]
        SPLIT = ONE + PIECES
        ps_g, ps_u, ps_t, ps_d = ps[0:2], ps[2:4], ps[4:6], ps[6:8]

        ld_gu, ld_dn = ([sem(f"{k}{q}") for q in range(2)] for k in ("ld_gu", "ld_dn"))
        pool_c = count("pool_c5")
        pool_0, dve_0 = sem("pool_05"), sem("dve_05")
        act_w, dve_w, act_x, dve_x, pe_x = (count(k) for k in ("act_w5", "dve_w5", "act_x", "dve_x", "pe_x"))
        pe_g, pe_u, act_s, dve_p, act_h, dve_h = (count(k) for k in ("pe_g5", "pe_u5", "act_s5", "dve_p5", "act_h5", "dve_h5"))
        pe_d, dve_y, dve_i = count("pe_d5"), count("dve_y"), count("dve_i")
        block = ctx.enter_context(nc.Block())

        def gu_piece(buf, k):
            return buf.rearrange("p m c i -> p (m c i)")[:, k * GU // GUP:(k + 1) * GU // GUP]

        @block.sync
        def _(sp):
            def expert(n):
                return sp.value_load(expert_of[0:1, n], min_val=0, max_val=E - 1)

            def load(buf, src, e, landed):
                sp.dma_start(buf[:], src[bass.ds(e, 1)].rearrange("a p n -> p (a n)")).then_inc(landed, 16)

            def step(g, q, more=True):
                n = 2 * g + q
                this = expert(bass.ds(n, 1))
                sp.wait_ge(dve_w, SPLIT + PIECES * (n - 1))
                load(dn_raw[q], wdn, this, ld_dn[q])
                if more:
                    load(gu_raw[1 - q], wgu, expert(bass.ds(n + 1, 1)), ld_gu[1 - q])

            with sp.Fori(0, TURNS) as g:
                for q in range(2):
                    step(g, q)
            step(TURNS, 0, False)

        @block.gpsimd
        def _(pool):
            def gather(q):
                for h in range(HALVES):
                    nc.gpsimd.indirect_dma_start(xg[q][:, h, :], None, rows, bass.IndirectOffsetOnAxis(ap=gidx[q][h][:], axis=0),
                                                 bounds_check=T + BT - 1, oob_is_err=True).then_inc(ld_x[q], 16)

            def scatter(q):
                for h in range(HALVES):
                    nc.gpsimd.indirect_dma_start(out, bass.IndirectOffsetOnAxis(ap=sidx[q][h][:], axis=0), y[q][:, h, :], None,
                                                 bounds_check=T + BT - 1, oob_is_err=True,
                                                 compute_op=ALU.add).then_inc(added, 16)

            def take_waits(done):
                pool.wait_ge(pool_c, ONE + done)
                nc.gpsimd.tensor_tensor(carry[:], ident[:, 0:1], ident[:, 0:1], ALU.add).then_inc(pool_c, 1)

            for counter in counters:
                nc.gpsimd.sem_inc(counter, ONE)
            nc.gpsimd.sem_inc(dve_w, PIECES)
            for buf in [y[0], carry]:
                nc.gpsimd.memset(buf[:], 0.0).then_inc(pool_0, 1)
            pool.wait_ge(pool_0, 2)
            pool.wait_ge(added, FIRST)
            with pool.Fori(0, TURNS) as g:
                for q in range(2):
                    n = 2 * g + q
                    pool.wait_ge(dve_i, ONE + n + 1)
                    pool.wait_ge(pe_x, ONE + HALVES * (n + 1))
                    take_waits(2 * n)
                    gather(q)
                    pool.wait_ge(dve_y, ONE + HALVES * n)
                    pool.wait_ge(added, FIRST + 16 * HALVES * n)
                    take_waits(2 * n + 1)
                    scatter(q)
            for n in range(2 * TURNS, 2 * TURNS + 3):
                pool.wait_ge(dve_i, ONE + n + 1)
                pool.wait_ge(dve_y, ONE + HALVES * n)
                pool.wait_ge(added, FIRST + 16 * HALVES * n)
                scatter(n % 2)
            pool.wait_ge(added, FIRST + 16 * HALVES * (2 * TURNS + 3))
            pool.wait_ge(ld_x[1], 16 * HALVES * (TURNS + 1))

        @block.tensor
        def _(pe):
            def transposed(q):
                for h in range(HALVES):
                    for j in range(DC):
                        last = nc.tensor.transpose(ps_t[h][:, j * P:(j + 1) * P], xg[q][:, h, j * P:(j + 1) * P], ident[:])
                    last.then_inc(pe_x, 1)

            pe.wait_ge(pool_0, 1)
            pe.wait_ge(ld_x[0], 16 * HALVES)
            transposed(0)
            pe.wait_ge(dve_0, 4)

            def down(n, q):
                pe.wait_ge(dve_h, ONE + NI * n)
                pe.wait_ge(dve_y, ONE + HALVES * n)
                for h in range(HALVES):
                    for c, (_, w) in enumerate(IT):
                        last = matmul3(nc, ps_d[h][:], [x[0:w, c, h * P:(h + 1) * P] for x in hh[1 - q]],
                                       [x[0:w, c, :] for x in dn_s[1 - q]], c == 0, c == NI - 1)
                    last.then_inc(pe_d, 1)

            def step(g, q, more=True):
                n = 2 * g + q
                pe.wait_ge(dve_x, ONE + HALVES * (n + 1))
                pe.wait_ge(dve_w, SPLIT + PIECES * n)
                for c, (i0, w) in enumerate(IT):
                    k = (NI * q + c) % 2
                    pe.wait_ge(dve_p, ONE + NI * n + max(c - 1, 0))
                    for m, bank in enumerate((ps_g[k], ps_u[k])):
                        for j in range(DC):
                            last = matmul3(nc, bank[0:w, 0:BT], [x[:, m, j, i0:i0 + w] for x in gu_s[q]],
                                           [x[:, j, :] for x in xT[q]], j == 0, j == DC - 1)
                        last.then_inc((pe_g, pe_u)[m], 1)
                if more:
                    pe.wait_ge(ld_x[1 - q], 16 * HALVES * (g + 1 + q))
                    transposed(1 - q)
                down(n, q)

            with pe.Fori(0, TURNS) as g:
                for q in range(2):
                    step(g, q)
            step(TURNS, 0, False)
            pe.wait_ge(dve_w, SPLIT + PIECES * 2 * TURNS + DNP)
            down(2 * TURNS + 1, 1)

        @block.scalar
        def _(act):
            def high_rows(q, n, h):
                act.wait_ge(pe_x, ONE + HALVES * (n + 1) + h + 1)
                nc.scalar.copy(xT[q][0][:, :, h * P:(h + 1) * P], ps_t[h][:].rearrange("p (j t) -> p j t", j=DC)).then_inc(act_x, 1)

            def high_gu(q, k):
                nc.scalar.copy(gu_piece(gu_s[q][0][:], k), gu_raw[q][:, k * GU // GUP:(k + 1) * GU // GUP]).then_inc(act_w, 1)

            def high_dn(q, c):
                nc.scalar.copy(dn_s[q][0][:, c, :], dn_raw[q][:, c * D:(c + 1) * D]).then_inc(act_w, 1)

            for h in range(HALVES):
                high_rows(0, -1, h)
            act.wait_ge(dve_0, 4)

            def step(g, q, more=True):
                n = 2 * g + q

                def gated(c):
                    k, w = (NI * q + c) % 2, IT[c][1]
                    act.wait_ge(pe_g, ONE + NI * n + c + 1)
                    act.wait_ge(dve_p, ONE + NI * n + max(c - 1, 0))
                    nc.scalar.activation(silu[k][0:w, :], ps_g[k][0:w, 0:BT], ACT.Silu).then_inc(act_s, 1)

                def high_product(c):
                    k, w = (NI * q + c) % 2, IT[c][1]
                    act.wait_ge(dve_p, ONE + NI * n + c + 1)
                    nc.scalar.copy(hh[q][0][0:w, c, :], prod[k][0:w, :]).then_inc(act_h, 1)

                def ahead(k):
                    if more:
                        high_gu(1 - q, k)

                act.wait_ge(ld_dn[q], 16 * (g + 1))
                act.wait_ge(pe_d, ONE + HALVES * n)
                high_dn(q, 0)
                high_dn(q, 1)
                if more:
                    act.wait_ge(ld_gu[1 - q], 16 * (g + 1))
                    act.wait_ge(pe_u, ONE + NI * n)
                ahead(0)
                gated(0)
                high_dn(q, 2)
                high_product(0)
                ahead(1)
                gated(1)
                ahead(2)
                high_product(1)
                gated(2)
                if more:
                    high_rows(1 - q, n, 0)
                high_product(2)
                if more:
                    high_rows(1 - q, n, 1)
                ahead(3)

            with act.Fori(0, TURNS) as g:
                for q in range(2):
                    step(g, q)
            step(TURNS, 0, False)

        @block.vector
        def _(dve):
            def low_rows(q, n, h):
                dve.wait_ge(act_x, ONE + HALVES * (n + 1) + h + 1)
                w = slice(h * P, (h + 1) * P)
                nc.vector.tensor_tensor(xT[q][1][:, :, w], ps_t[h][:].rearrange("p (j t) -> p j t", j=DC),
                                        xT[q][0][:, :, w].bitcast(F32), ALU.subtract).then_inc(dve_x, 1)

            def low_gu(q, k, done):
                dve.wait_ge(act_w, ONE + done)
                nc.vector.tensor_tensor(gu_piece(gu_s[q][1][:], k), gu_raw[q][:, k * GU // GUP:(k + 1) * GU // GUP],
                                        gu_piece(gu_s[q][0][:], k).bitcast(F32), ALU.subtract).then_inc(dve_w, 1)

            def low_dn(q, c, done):
                dve.wait_ge(act_w, ONE + done)
                nc.vector.tensor_tensor(dn_s[q][1][:, c, :], dn_raw[q][:, c * D:(c + 1) * D],
                                        dn_s[q][0][:, c, :].bitcast(F32), ALU.subtract).then_inc(dve_w, 1)

            for buf in dn_s[1] + hh[1]:
                nc.vector.memset(buf[:].bitcast(F32), 0.0).then_inc(dve_0, 1)
            dve.wait_ge(pool_0, 2)
            for h in range(HALVES):
                low_rows(0, -1, h)

            def add_indices(n, q):
                dve.wait_ge(added, FIRST + 16 * HALVES * (n - 1))
                for h in range(HALVES):
                    last = nc.vector.tensor_copy(sidx[q][h][:], token_of[:, bass.ds(HALVES * n + h, 1)])
                return last

            def weigh(n, q):
                dve.wait_ge(added, FIRST + 16 * HALVES * n)
                for h in range(HALVES):
                    dve.wait_ge(pe_d, ONE + HALVES * n + h + 1)
                    nc.vector.tensor_scalar(y[1 - q][:, h, :], ps_d[h][:], weight_of[:, bass.ds(HALVES * n + h, 1)], None,
                                            ALU.mult).then_inc(dve_y, 1)

            def step(g, q, more=True):
                n = 2 * g + q
                split = PIECES * n

                def product(c):
                    k, w = (NI * q + c) % 2, IT[c][1]
                    dve.wait_ge(act_s, ONE + NI * n + c + 1)
                    dve.wait_ge(pe_u, ONE + NI * n + c + 1)
                    dve.wait_ge(dve_h, ONE + NI * n + max(c - 1, 0))
                    nc.vector.tensor_tensor(prod[k][0:w, :], ps_u[k][0:w, 0:BT], silu[k][0:w, :], ALU.mult).then_inc(dve_p, 1)

                def low_product(c):
                    k, w = (NI * q + c) % 2, IT[c][1]
                    dve.wait_ge(act_h, ONE + NI * n + c + 1)
                    nc.vector.tensor_tensor(hh[q][1][0:w, c, :], prod[k][0:w, :], hh[q][0][0:w, c, :].bitcast(F32),
                                            ALU.subtract).then_inc(dve_h, 1)

                def ahead(k, done):
                    if more:
                        low_gu(1 - q, k, split + done)

                last = add_indices(n, q)
                if more:
                    for h in range(HALVES):
                        last = nc.vector.tensor_copy(gidx[q][h][:], token_of[:, bass.ds(HALVES * (n + 4) + h, 1)])
                last.then_inc(dve_i, 1)
                low_dn(q, 0, split + 1)
                low_dn(q, 1, split + 2)
                ahead(0, 3)
                product(0)
                low_dn(q, 2, split + (4 if more else 3))
                low_product(0)
                ahead(1, 5)
                product(1)
                ahead(2, 6)
                low_product(1)
                product(2)
                if more:
                    low_rows(1 - q, n, 0)
                low_product(2)
                if more:
                    low_rows(1 - q, n, 1)
                ahead(3, 7)
                weigh(n, q)

            dve.wait_ge(added, FIRST)
            with dve.Fori(0, TURNS) as g:
                for q in range(2):
                    step(g, q)
            step(TURNS, 0, False)
            n = 2 * TURNS + 1
            add_indices(n, 1).then_inc(dve_i, 1)
            weigh(n, 1)
            add_indices(n + 1, 0).then_inc(dve_i, 1)


def program(nc, x, ctxT, wqkT, bqk, ln1, ln2, wqk, wv, wo, gateT, wgu, wdn, out):
    with ExitStack() as ctx:
        sb = lambda name, shape, dt=F32: ctx.enter_context(nc.sbuf_tensor(name, shape, dt))
        sem = lambda name: ctx.enter_context(nc.semaphore(name))
        spill = nc.dram_tensor("x1_spill", [NB, P, ST, D], F32, kind="Internal").ap()
        rows = nc.dram_tensor("normed_rows", [T + BT, D], F32, kind="Internal").ap()
        table = nc.dram_tensor("slot_table", [SLOTS, 2], F32, kind="Internal").ap()
        tiled = lambda a: a[0:T, :].rearrange("(b t p) n -> b p t n", p=P, b=NB)
        pads = lambda a: [a[T + k * P:T + (k + 1) * P, :] for k in range(BT // P)]
        ident = sb("ident", [P, P])
        ident16 = sb("ident16", [P, P], BF16)
        causal = sb("causal", [P, P], BF16)
        neg_half = sb("neg_half", [P, ST])
        eps = sb("eps", [P, 2, ST])
        ps = [ctx.enter_context(nc.psum_tensor(f"ps{k}", [P, 512], F32)) for k in range(8)]
        constants(nc, sem, ident, ident16, causal, neg_half, eps)
        token_of = sb("token_of", [P, SLOTS // P + 8], U32)
        weight_of = sb("weight_of", [P, SLOTS // P + 2])
        expert_of = sb("expert_of", [1, NBLOCKS], I32)
        space = [sb(f"space_{s}", [P, 2 * DC * I], F32R) for s in ("hi", "lo")]
        first_wgu = [w[:].rearrange("p (m c i) -> p m c i", m=2, c=DC) for w in space]
        xg = [sb(f"xg{q}", [P, BT // P, D]) for q in range(2)]
        begin = sb("begin", [P, 3])
        ld_xg, added = [sem(f"ld_xg{q}") for q in range(2)], sem("added")
        with ExitStack() as stream:
            HS = stream.enter_context(nc.sbuf_tensor("HS", [P, TT * D], F32))
            hT = [stream.enter_context(nc.sbuf_tensor(f"hT_{s}", [P, DC, T], F32R)) for s in ("hi", "lo")]
            with ExitStack() as early:
                wqk_0 = [early.enter_context(nc.sbuf_tensor(f"wqk_0{s}", [P, 1024], F32R))[:] for s in ("hi", "lo")]
                qkT = [early.enter_context(nc.sbuf_tensor(f"qkT_{s}", [P, 2, S], F32R)) for s in ("hi", "lo")]
                raw = [w[:].rearrange("p h n -> p (h n)") for w in xg]
                ld_raw = [sem(f"ld_raw{r}") for r in range(2)]
                cross_attention(nc, sem, ps, ident, neg_half, eps, HS, hT, space, x, ctxT, wqkT, bqk, ln1, spill,
                                raw, (wqk[0], wv[0]), ld_raw, wqk_0, qkT)
                self_attention(nc, sem, ps, ident, ident16, causal, HS, hT, space, raw, ld_raw, wqk_0, qkT, wqk, wv, wo)
            logits = stream.enter_context(nc.sbuf_tensor("logits", [P, TT, E], F32))
            normed_again(nc, sem, ps, ident, neg_half, eps, HS, hT, logits, tiled(rows), pads(rows), ln2, gateT, spill,
                         space, wgu[E])
            shared_expert(nc, sem, ps, ident, HS, hT, logits, token_of, weight_of, expert_of, first_wgu, wgu, wdn[E:NE],
                          table, tiled(out), pads(out), xg, rows, ld_xg, added, begin)
        routed_experts(nc, sem, ps, ident, token_of, weight_of, expert_of, rows, first_wgu, xg, ld_xg, added, begin,
                       wgu, wdn, out)


def kernel(**inputs):
    import numpy as np
    import concourse.bacc as bacc
    from concourse.bass_utils import run_bass_kernel_spmd

    a = {k: np.asarray(v) for k, v in inputs.items()}
    w = lambda name: a["L0_ffn_" + name]
    chunks = lambda m: m.reshape(-1, P, m.shape[-1]).transpose(1, 0, 2)
    experts_of = lambda e, s: np.concatenate([w(e), w(s).reshape(NSH, I, D)])
    down = np.concatenate([w("ed_w").transpose(0, 2, 1), w("sd_w").T.reshape(NSH, I, D)])
    down = np.concatenate([down, np.zeros((NE, len(IT) * P - I, D), np.float32)], axis=1)
    gu = np.stack([experts_of("eg_w", "sg_w"), experts_of("eu_w", "su_w")], axis=1)
    qk = np.stack([w("wq").reshape(DC, P, H, HD), w("wk").reshape(DC, P, H, HD)])
    cycled = lambda m: np.concatenate([m, m[0:1]])
    arrays = {
        "x": a["x"].reshape(NB, ST, P, D).transpose(0, 2, 1, 3),
        "ctxT": a["ctx_1024"].transpose(0, 2, 1).reshape(NB, CC, P, S).transpose(0, 2, 1, 3),
        "wqkT": np.stack([chunks(a["L0_xattn_Wq"].T), chunks(a["L0_xattn_Wk"].T)], axis=1),
        "bqk": np.stack([a["L0_xattn_bq"], a["L0_xattn_bk"]], axis=1),
        "ln1": w("ln1_w"),
        "ln2": w("ln2_w"),
        "wqk": cycled(qk.transpose(3, 2, 0, 1, 4).reshape(H, P, 2 * DC * HD)),
        "wv": cycled(w("wv").reshape(DC, P, HP, 2 * HD).transpose(2, 1, 0, 3).reshape(HP, P, DC * 2 * HD)),
        "wo": w("wo").reshape(HP, 2, P, D).transpose(0, 2, 1, 3).reshape(HP, P, 2 * D),
        "gateT": chunks(w("gate_w").T),
        "wgu": gu.transpose(0, 1, 3, 2).reshape(NE, 2, DC, P, I).transpose(0, 3, 1, 2, 4).reshape(NE, P, 2 * DC * I),
        "wdn": down.reshape(NE, len(IT), P, D).transpose(0, 2, 1, 3).reshape(NE, P, len(IT) * D),
    }
    nc = bacc.Bacc("TRN2", target_bir_lowering=False, num_devices=1)
    arrays = {"in_" + k: np.ascontiguousarray(v) for k, v in arrays.items()}
    args = [nc.dram_tensor(k, v.shape, mybir.dt.from_np(v.dtype), kind="ExternalInput").ap() for k, v in arrays.items()]
    out = nc.dram_tensor("out", (T + BT, D), F32, kind="ExternalOutput").ap()
    program(nc, *args, out)
    r = run_bass_kernel_spmd(nc, [arrays], core_ids=[0])
    return r.results[0]["out"][0:T].reshape(NB, S, D)
```
